# Optimizing a Trainium2 kernel written in Bass

```python
import numpy as np
import jax
import jax.numpy as jnp

def _softmax(x, axis=-1):
    return jax.nn.softmax(x, axis=axis)

def _gelu(x):
    return jax.nn.gelu(x, approximate=True)

def _silu(x):
    return jax.nn.silu(x)

def _sigmoid(x):
    return jax.nn.sigmoid(x)

def _layernorm(x, axis=-1, eps=1e-05):
    m = jnp.mean(x, axis=axis, keepdims=True)
    v = jnp.var(x, axis=axis, keepdims=True)
    return (x - m) / jnp.sqrt(v + eps)

def _scatter_add(tgt, idx, src, axis=0):
    return tgt.at[idx].add(src)

def _segment_sum(src, seg, n):
    return jax.ops.segment_sum(src, seg, n)
kernel_name = 'mk_adaln_d2_jaxref_r8_1eb60a'

def setup_inputs(seed: int=0):
    np.random.seed(seed)
    _w = jnp.asarray

    def _L0_attn_setup():
        import jax, jax.numpy as jnp
        import numpy as np
        EPS = 1e-06
        key = jax.random.key(seed)
        ks = jax.random.split(key, 8)
        b, n, d, h = (2, 256, 128, 16)
        std = 0.02
        x = jax.random.normal(ks[0], (b, n, d), jnp.float32)
        Wq = jax.random.normal(ks[1], (d, d), jnp.float32) * std
        Wk = jax.random.normal(ks[2], (d, d), jnp.float32) * std
        Wv = jax.random.normal(ks[3], (d, d), jnp.float32) * std
        Wo = jax.random.normal(ks[4], (d, d), jnp.float32) * std
        Wbet = jax.random.normal(ks[5], (d, h), jnp.float32) * std
        Wf = jax.random.normal(ks[6], (d, h), jnp.float32) * std
        norm_w = jnp.ones((d,), jnp.float32)
        return {'x': x, 'Wq': Wq, 'Wk': Wk, 'Wv': Wv, 'Wo': Wo, 'Wbet': Wbet, 'Wf': Wf, 'norm_w': norm_w}
    _L0_attn_in = _L0_attn_setup()

    def _L0_ffn_setup():
        import jax, jax.numpy as jnp
        import numpy as np
        D_MODEL = 128
        N_HEADS = 16
        N_KV = 4
        NUM_REP = N_HEADS // N_KV
        HEAD_DIM = D_MODEL // N_HEADS
        N_EXPERTS = 8
        TOP_K = 2
        CAP_FACTOR = 1.25
        EPS_NORM = 1e-06

        def _rmsnorm(x, w):
            var = jnp.mean(x * x, axis=-1, keepdims=True)
            return w * (x * jax.lax.rsqrt(var + EPS_NORM))

        def _gqa(x, qw, qb, kw, kb, vw, vb, ow, ob):
            B, S, D = x.shape
            q = (x @ qw + qb).reshape(B, S, N_HEADS, HEAD_DIM).transpose(0, 2, 1, 3)
            k = (x @ kw + kb).reshape(B, S, N_KV, HEAD_DIM).transpose(0, 2, 1, 3)
            v = (x @ vw + vb).reshape(B, S, N_KV, HEAD_DIM).transpose(0, 2, 1, 3)
            k = jnp.repeat(k, NUM_REP, axis=1)
            v = jnp.repeat(v, NUM_REP, axis=1)
            scores = jnp.einsum('bhqd,bhkd->bhqk', q, k) / np.sqrt(HEAD_DIM).astype(np.float32)
            attn = jax.nn.softmax(scores, axis=-1)
            out = jnp.einsum('bhqk,bhkd->bhqd', attn, v)
            out = out.transpose(0, 2, 1, 3).reshape(B, S, D)
            return out @ ow + ob

        def _moe(x, gate_w, w1, w2):
            B, S, D = x.shape
            T = B * S
            x_flat = x.reshape(T, D)
            capacity = int(CAP_FACTOR * T * TOP_K / N_EXPERTS)
            logits = x_flat @ gate_w
            probs = jax.nn.sigmoid(logits)
            _, sel = jax.lax.top_k(probs, TOP_K)
            w_topk = jnp.take_along_axis(probs, sel, axis=1)
            w_topk = w_topk / (jnp.sum(w_topk, axis=-1, keepdims=True) + 1e-06)
            flat_sel = sel.reshape(-1)
            em = jax.nn.one_hot(flat_sel, N_EXPERTS, dtype=jnp.int32)
            ranks = jnp.take_along_axis(jnp.cumsum(em, axis=0), flat_sel[:, None], axis=1)[:, 0] - 1
            valid = ranks < capacity
            slot = flat_sel * capacity + ranks
            scatter_idx = jnp.where(valid, slot, N_EXPERTS * capacity)
            x_rep = jnp.repeat(x_flat, TOP_K, axis=0)
            padded = jnp.zeros((N_EXPERTS * capacity + 1, D), x.dtype).at[scatter_idx].set(x_rep)
            padded_x = padded[:N_EXPERTS * capacity].reshape(N_EXPERTS, capacity, D)
            h = jax.nn.gelu(jnp.einsum('ecd,edf->ecf', padded_x, w1), approximate=False)
            out_padded = jnp.einsum('ecf,efd->ecd', h, w2).reshape(N_EXPERTS * capacity, D)
            gather_idx = jnp.where(valid, slot, 0)
            out_rep = jnp.where(valid[:, None], out_padded[gather_idx], 0.0)
            out_w = out_rep * w_topk.reshape(-1)[:, None]
            return out_w.reshape(T, TOP_K, D).sum(axis=1).reshape(B, S, D)
        key = jax.random.key(seed)
        ks = jax.random.split(key, 12)
        s = 0.02
        return {'x': jax.random.normal(ks[0], (4, 128, D_MODEL), jnp.float32), 'qw': jax.random.normal(ks[1], (D_MODEL, D_MODEL), jnp.float32) * s, 'qb': jnp.zeros((D_MODEL,), jnp.float32), 'kw': jax.random.normal(ks[2], (D_MODEL, N_KV * HEAD_DIM), jnp.float32) * s, 'kb': jnp.zeros((N_KV * HEAD_DIM,), jnp.float32), 'vw': jax.random.normal(ks[3], (D_MODEL, N_KV * HEAD_DIM), jnp.float32) * s, 'vb': jnp.zeros((N_KV * HEAD_DIM,), jnp.float32), 'ow': jax.random.normal(ks[4], (D_MODEL, D_MODEL), jnp.float32) * s, 'ob': jnp.zeros((D_MODEL,), jnp.float32), 'gate_w': jax.random.normal(ks[5], (D_MODEL, N_EXPERTS), jnp.float32) * s, 'w1': jax.random.normal(ks[6], (N_EXPERTS, D_MODEL, 256), jnp.float32) * s, 'w2': jax.random.normal(ks[7], (N_EXPERTS, 256, D_MODEL), jnp.float32) * s, 'norm1_w': jnp.ones((D_MODEL,), jnp.float32), 'norm2_w': jnp.ones((D_MODEL,), jnp.float32)}
    _L0_ffn_in = _L0_ffn_setup()
    _L0_c = _w((lambda *s: np.random.randn(*s).astype(np.float32) * 0.05)(1, 128))
    _L0_wmod = _w((lambda *s: np.random.randn(*s).astype(np.float32) * 0.05)(128, 6 * 128) * 128 ** (-0.5))

    def _L1_attn_setup():
        import jax, jax.numpy as jnp
        import numpy as np
        N, L, D, A, F, B = (4, 512, 128, 128, 512, 8)
        EPS_LN = 1e-06
        EPS_Z = 1e-06

        def _layernorm(x, scale, bias):
            m = jnp.mean(x, axis=-1, keepdims=True)
            v = jnp.mean(jnp.square(x - m), axis=-1, keepdims=True)
            return (x - m) * jax.lax.rsqrt(v + EPS_LN) * scale + bias

        def _block(x, p):
            Wq, bq, Wk, bk, Wv, bv, Wo, bo, ln1_s, ln1_b, Wf1, bf1, Wf2, bf2, ln2_s, ln2_b = p
            residual = x
            q = jnp.einsum('nld,da->nla', x, Wq) + bq
            k = jnp.einsum('nld,da->nla', x, Wk) + bk
            v = jnp.einsum('nld,da->nla', x, Wv) + bv
            Q = jax.nn.elu(q) + 1.0
            K = jax.nn.elu(k) + 1.0
            KV = jnp.einsum('nsh,nsh->nh', K, v)
            Ksum = jnp.sum(K, axis=1)
            Z = 1.0 / (Q * Ksum[:, None, :] + EPS_Z)
            V = Q * KV[:, None, :] * Z
            attn = jax.nn.gelu(jnp.einsum('nla,ad->nld', V, Wo) + bo)
            x = _layernorm(attn + residual, ln1_s, ln1_b)
            residual = x
            h = jax.nn.gelu(jnp.einsum('nld,df->nlf', x, Wf1) + bf1)
            ff = jax.nn.gelu(jnp.einsum('nlf,fd->nld', h, Wf2) + bf2)
            x = _layernorm(ff + residual, ln2_s, ln2_b)
            return (x, None)
        key = jax.random.key(seed)
        ks = jax.random.split(key, 10)
        s = 0.02
        x = jax.random.normal(ks[0], (N, L, D), dtype=jnp.float32)
        Wq = jax.random.normal(ks[1], (B, D, A), dtype=jnp.float32) * s
        Wk = jax.random.normal(ks[2], (B, D, A), dtype=jnp.float32) * s
        Wv = jax.random.normal(ks[3], (B, D, A), dtype=jnp.float32) * s
        Wo = jax.random.normal(ks[4], (B, A, D), dtype=jnp.float32) * s
        Wf1 = jax.random.normal(ks[5], (B, D, F), dtype=jnp.float32) * s
        Wf2 = jax.random.normal(ks[6], (B, F, D), dtype=jnp.float32) * s
        return {'x': x, 'Wq': Wq, 'bq': jnp.zeros((B, A), jnp.float32), 'Wk': Wk, 'bk': jnp.zeros((B, A), jnp.float32), 'Wv': Wv, 'bv': jnp.zeros((B, A), jnp.float32), 'Wo': Wo, 'bo': jnp.zeros((B, D), jnp.float32), 'ln1_s': jnp.ones((B, D), jnp.float32), 'ln1_b': jnp.zeros((B, D), jnp.float32), 'Wf1': Wf1, 'bf1': jnp.zeros((B, F), jnp.float32), 'Wf2': Wf2, 'bf2': jnp.zeros((B, D), jnp.float32), 'ln2_s': jnp.ones((B, D), jnp.float32), 'ln2_b': jnp.zeros((B, D), jnp.float32)}
    _L1_attn_in = _L1_attn_setup()

    def _L1_ffn_setup():
        import jax, jax.numpy as jnp
        import numpy as np
        TOP_K = 2

        def _route(x2d, gate_w, num_experts, top_k):
            scores = jax.nn.softmax((x2d @ gate_w.T).astype(jnp.float32), axis=1)
            top_scores, sel = jax.lax.top_k(scores, top_k)
            sel_flat = sel.reshape(-1)
            counts = jnp.bincount(sel_flat, length=num_experts)
            order = jnp.argsort(sel_flat, stable=True)
            top_scores_sorted = top_scores.reshape(-1)[order]
            token_idx = order // top_k
            return (top_scores_sorted, token_idx, counts)

        def _grouped_swiglu(xr, w1, w2, w3, eid):
            out = jnp.zeros((xr.shape[0], w2.shape[-1]), dtype=xr.dtype)
            for e in range(w1.shape[0]):
                xe = jnp.where((eid == e)[:, None], xr, 0.0)
                h = jax.nn.silu(xe @ w1[e]) * (xe @ w3[e])
                out = out + h @ w2[e]
            return out
        key = jax.random.key(seed)
        ks = jax.random.split(key, 5)
        bs, slen, dim, hidden, E = (2, 256, 128, 352, 8)
        x = jax.random.normal(ks[0], (bs, slen, dim), dtype=jnp.float32)
        gate_w = jax.random.normal(ks[1], (E, dim), dtype=jnp.float32) * 0.02
        w1 = jax.random.normal(ks[2], (E, dim, hidden), dtype=jnp.float32) * 0.02
        w2 = jax.random.normal(ks[3], (E, hidden, dim), dtype=jnp.float32) * 0.02
        w3 = jax.random.normal(ks[4], (E, dim, hidden), dtype=jnp.float32) * 0.02
        return {'x': x, 'gate_w': gate_w, 'w1': w1, 'w2': w2, 'w3': w3}
    _L1_ffn_in = _L1_ffn_setup()
    _L1_c = _w((lambda *s: np.random.randn(*s).astype(np.float32) * 0.05)(1, 128))
    _L1_wmod = _w((lambda *s: np.random.randn(*s).astype(np.float32) * 0.05)(128, 6 * 128) * 128 ** (-0.5))
    _d = {'L0_attn_x': _L0_attn_in['x'], 'L0_attn_Wq': _L0_attn_in['Wq'], 'L0_attn_Wk': _L0_attn_in['Wk'], 'L0_attn_Wv': _L0_attn_in['Wv'], 'L0_attn_Wo': _L0_attn_in['Wo'], 'L0_attn_Wbet': _L0_attn_in['Wbet'], 'L0_attn_Wf': _L0_attn_in['Wf'], 'L0_attn_norm_w': _L0_attn_in['norm_w'], 'L0_ffn_qw': _L0_ffn_in['qw'], 'L0_ffn_qb': _L0_ffn_in['qb'], 'L0_ffn_kw': _L0_ffn_in['kw'], 'L0_ffn_kb': _L0_ffn_in['kb'], 'L0_ffn_vw': _L0_ffn_in['vw'], 'L0_ffn_vb': _L0_ffn_in['vb'], 'L0_ffn_ow': _L0_ffn_in['ow'], 'L0_ffn_ob': _L0_ffn_in['ob'], 'L0_ffn_gate_w': _L0_ffn_in['gate_w'], 'L0_ffn_w1': _L0_ffn_in['w1'], 'L0_ffn_w2': _L0_ffn_in['w2'], 'L0_ffn_norm1_w': _L0_ffn_in['norm1_w'], 'L0_ffn_norm2_w': _L0_ffn_in['norm2_w'], 'L0_c': _L0_c, 'L0_wmod': _L0_wmod, 'L1_attn_Wq': _L1_attn_in['Wq'], 'L1_attn_bq': _L1_attn_in['bq'], 'L1_attn_Wk': _L1_attn_in['Wk'], 'L1_attn_bk': _L1_attn_in['bk'], 'L1_attn_Wv': _L1_attn_in['Wv'], 'L1_attn_bv': _L1_attn_in['bv'], 'L1_attn_Wo': _L1_attn_in['Wo'], 'L1_attn_bo': _L1_attn_in['bo'], 'L1_attn_ln1_s': _L1_attn_in['ln1_s'], 'L1_attn_ln1_b': _L1_attn_in['ln1_b'], 'L1_attn_Wf1': _L1_attn_in['Wf1'], 'L1_attn_bf1': _L1_attn_in['bf1'], 'L1_attn_Wf2': _L1_attn_in['Wf2'], 'L1_attn_bf2': _L1_attn_in['bf2'], 'L1_attn_ln2_s': _L1_attn_in['ln2_s'], 'L1_attn_ln2_b': _L1_attn_in['ln2_b'], 'L1_ffn_gate_w': _L1_ffn_in['gate_w'], 'L1_ffn_w1': _L1_ffn_in['w1'], 'L1_ffn_w2': _L1_ffn_in['w2'], 'L1_ffn_w3': _L1_ffn_in['w3'], 'L1_c': _L1_c, 'L1_wmod': _L1_wmod}
    _x0 = _d['L0_attn_x']
    _d['L0_attn_x'] = jax.random.normal(jax.random.fold_in(jax.random.key(seed), 1), (1, 2048, 128), dtype=_x0.dtype)
    del _x0
    return _d

def reference(L0_attn_x, L0_attn_Wq, L0_attn_Wk, L0_attn_Wv, L0_attn_Wo, L0_attn_Wbet, L0_attn_Wf, L0_attn_norm_w, L0_ffn_qw, L0_ffn_qb, L0_ffn_kw, L0_ffn_kb, L0_ffn_vw, L0_ffn_vb, L0_ffn_ow, L0_ffn_ob, L0_ffn_gate_w, L0_ffn_w1, L0_ffn_w2, L0_ffn_norm1_w, L0_ffn_norm2_w, L0_c, L0_wmod, L1_attn_Wq, L1_attn_bq, L1_attn_Wk, L1_attn_bk, L1_attn_Wv, L1_attn_bv, L1_attn_Wo, L1_attn_bo, L1_attn_ln1_s, L1_attn_ln1_b, L1_attn_Wf1, L1_attn_bf1, L1_attn_Wf2, L1_attn_bf2, L1_attn_ln2_s, L1_attn_ln2_b, L1_ffn_gate_w, L1_ffn_w1, L1_ffn_w2, L1_ffn_w3, L1_c, L1_wmod):

    def _L0_attn_ref(x, Wq, Wk, Wv, Wo, Wbet, Wf, norm_w):
        import jax, jax.numpy as jnp
        import numpy as np
        EPS = 1e-06
        b, n, d = x.shape
        h = Wbet.shape[1]
        hd = d // h
        q = jax.nn.silu(x @ Wq).reshape(b, n, h, hd)
        k = jax.nn.silu(x @ Wk).reshape(b, n, h, hd)
        k = k * jax.lax.rsqrt(jnp.sum(k * k, -1, keepdims=True) + 1e-12)
        v = (x @ Wv).reshape(b, n, h, hd)
        beta = 2.0 * jax.nn.sigmoid(x @ Wbet)
        a = jax.nn.sigmoid(x @ Wf)

        def step(S, inp):
            qt, kt, vt, at, bt = inp
            Sd = at[..., None, None] * S
            u = vt - jnp.einsum('bhk,bhkv->bhv', kt, Sd)
            Sn = Sd + bt[..., None, None] * kt[..., None] * u[:, :, None, :]
            o = jnp.einsum('bhk,bhkv->bhv', qt, Sn)
            return (Sn, o)
        tfirst = lambda z: jnp.moveaxis(z, 1, 0)
        S0 = jnp.zeros((b, h, hd, hd), x.dtype)
        _, o = jax.lax.scan(step, S0, (tfirst(q), tfirst(k), tfirst(v), tfirst(a), tfirst(beta)))
        o = jnp.moveaxis(o, 0, 1)
        o = o * jax.lax.rsqrt(jnp.mean(o * o, -1, keepdims=True) + EPS)
        o = o.reshape(b, n, d) * norm_w
        return o @ Wo

    def _L0_ffn_ref(x, qw, qb, kw, kb, vw, vb, ow, ob, gate_w, w1, w2, norm1_w, norm2_w):
        import jax, jax.numpy as jnp
        import numpy as np
        D_MODEL = 128
        N_HEADS = 16
        N_KV = 4
        NUM_REP = N_HEADS // N_KV
        HEAD_DIM = D_MODEL // N_HEADS
        N_EXPERTS = 8
        TOP_K = 2
        CAP_FACTOR = 1.25
        EPS_NORM = 1e-06

        def _rmsnorm(x, w):
            var = jnp.mean(x * x, axis=-1, keepdims=True)
            return w * (x * jax.lax.rsqrt(var + EPS_NORM))

        def _gqa(x, qw, qb, kw, kb, vw, vb, ow, ob):
            B, S, D = x.shape
            q = (x @ qw + qb).reshape(B, S, N_HEADS, HEAD_DIM).transpose(0, 2, 1, 3)
            k = (x @ kw + kb).reshape(B, S, N_KV, HEAD_DIM).transpose(0, 2, 1, 3)
            v = (x @ vw + vb).reshape(B, S, N_KV, HEAD_DIM).transpose(0, 2, 1, 3)
            k = jnp.repeat(k, NUM_REP, axis=1)
            v = jnp.repeat(v, NUM_REP, axis=1)
            scores = jnp.einsum('bhqd,bhkd->bhqk', q, k) / np.sqrt(HEAD_DIM).astype(np.float32)
            attn = jax.nn.softmax(scores, axis=-1)
            out = jnp.einsum('bhqk,bhkd->bhqd', attn, v)
            out = out.transpose(0, 2, 1, 3).reshape(B, S, D)
            return out @ ow + ob

        def _moe(x, gate_w, w1, w2):
            B, S, D = x.shape
            T = B * S
            x_flat = x.reshape(T, D)
            capacity = int(CAP_FACTOR * T * TOP_K / N_EXPERTS)
            logits = x_flat @ gate_w
            probs = jax.nn.sigmoid(logits)
            _, sel = jax.lax.top_k(probs, TOP_K)
            w_topk = jnp.take_along_axis(probs, sel, axis=1)
            w_topk = w_topk / (jnp.sum(w_topk, axis=-1, keepdims=True) + 1e-06)
            flat_sel = sel.reshape(-1)
            em = jax.nn.one_hot(flat_sel, N_EXPERTS, dtype=jnp.int32)
            ranks = jnp.take_along_axis(jnp.cumsum(em, axis=0), flat_sel[:, None], axis=1)[:, 0] - 1
            valid = ranks < capacity
            slot = flat_sel * capacity + ranks
            scatter_idx = jnp.where(valid, slot, N_EXPERTS * capacity)
            x_rep = jnp.repeat(x_flat, TOP_K, axis=0)
            padded = jnp.zeros((N_EXPERTS * capacity + 1, D), x.dtype).at[scatter_idx].set(x_rep)
            padded_x = padded[:N_EXPERTS * capacity].reshape(N_EXPERTS, capacity, D)
            h = jax.nn.gelu(jnp.einsum('ecd,edf->ecf', padded_x, w1), approximate=False)
            out_padded = jnp.einsum('ecf,efd->ecd', h, w2).reshape(N_EXPERTS * capacity, D)
            gather_idx = jnp.where(valid, slot, 0)
            out_rep = jnp.where(valid[:, None], out_padded[gather_idx], 0.0)
            out_w = out_rep * w_topk.reshape(-1)[:, None]
            return out_w.reshape(T, TOP_K, D).sum(axis=1).reshape(B, S, D)
        src = x + _gqa(x, qw, qb, kw, kb, vw, vb, ow, ob)
        src = _rmsnorm(src, norm1_w)
        src = src + _moe(src, gate_w, w1, w2)
        return _rmsnorm(src, norm2_w)

    def _L1_attn_ref(x, Wq, bq, Wk, bk, Wv, bv, Wo, bo, ln1_s, ln1_b, Wf1, bf1, Wf2, bf2, ln2_s, ln2_b):
        import jax, jax.numpy as jnp
        import numpy as np
        N, L, D, A, F, B = (4, 512, 128, 128, 512, 8)
        EPS_LN = 1e-06
        EPS_Z = 1e-06

        def _layernorm(x, scale, bias):
            m = jnp.mean(x, axis=-1, keepdims=True)
            v = jnp.mean(jnp.square(x - m), axis=-1, keepdims=True)
            return (x - m) * jax.lax.rsqrt(v + EPS_LN) * scale + bias

        def _block(x, p):
            Wq, bq, Wk, bk, Wv, bv, Wo, bo, ln1_s, ln1_b, Wf1, bf1, Wf2, bf2, ln2_s, ln2_b = p
            residual = x
            q = jnp.einsum('nld,da->nla', x, Wq) + bq
            k = jnp.einsum('nld,da->nla', x, Wk) + bk
            v = jnp.einsum('nld,da->nla', x, Wv) + bv
            Q = jax.nn.elu(q) + 1.0
            K = jax.nn.elu(k) + 1.0
            KV = jnp.einsum('nsh,nsh->nh', K, v)
            Ksum = jnp.sum(K, axis=1)
            Z = 1.0 / (Q * Ksum[:, None, :] + EPS_Z)
            V = Q * KV[:, None, :] * Z
            attn = jax.nn.gelu(jnp.einsum('nla,ad->nld', V, Wo) + bo)
            x = _layernorm(attn + residual, ln1_s, ln1_b)
            residual = x
            h = jax.nn.gelu(jnp.einsum('nld,df->nlf', x, Wf1) + bf1)
            ff = jax.nn.gelu(jnp.einsum('nlf,fd->nld', h, Wf2) + bf2)
            x = _layernorm(ff + residual, ln2_s, ln2_b)
            return (x, None)
        params = (Wq, bq, Wk, bk, Wv, bv, Wo, bo, ln1_s, ln1_b, Wf1, bf1, Wf2, bf2, ln2_s, ln2_b)
        out, _ = jax.lax.scan(_block, x, params)
        return out

    def _L1_ffn_ref(x, gate_w, w1, w2, w3):
        import jax, jax.numpy as jnp
        import numpy as np
        TOP_K = 2

        def _route(x2d, gate_w, num_experts, top_k):
            scores = jax.nn.softmax((x2d @ gate_w.T).astype(jnp.float32), axis=1)
            top_scores, sel = jax.lax.top_k(scores, top_k)
            sel_flat = sel.reshape(-1)
            counts = jnp.bincount(sel_flat, length=num_experts)
            order = jnp.argsort(sel_flat, stable=True)
            top_scores_sorted = top_scores.reshape(-1)[order]
            token_idx = order // top_k
            return (top_scores_sorted, token_idx, counts)

        def _grouped_swiglu(xr, w1, w2, w3, eid):
            out = jnp.zeros((xr.shape[0], w2.shape[-1]), dtype=xr.dtype)
            for e in range(w1.shape[0]):
                xe = jnp.where((eid == e)[:, None], xr, 0.0)
                h = jax.nn.silu(xe @ w1[e]) * (xe @ w3[e])
                out = out + h @ w2[e]
            return out
        bs, slen, dim = x.shape
        E, top_k = (gate_w.shape[0], TOP_K)
        x2d = x.reshape(bs * slen, dim)
        top_scores, token_idx, counts = _route(x2d, gate_w, E, top_k)
        routed_in = (x2d[token_idx].astype(jnp.float32) * top_scores[:, None]).astype(x.dtype)
        Tr = bs * slen * top_k
        eid = jnp.repeat(jnp.arange(E), counts, total_repeat_length=Tr)
        routed_out = _grouped_swiglu(routed_in, w1, w2, w3, eid)
        out = jnp.zeros((bs * slen, dim), dtype=x.dtype).at[token_idx].add(routed_out)
        return out.reshape(bs, slen, dim)
    x = L0_attn_x
    mod = (_silu(L0_c) @ L0_wmod).reshape(L0_c.shape[0], 6, 1, -1)
    sa, ca, ga, sb, cb, gb = (mod[:, 0], mod[:, 1], mod[:, 2], mod[:, 3], mod[:, 4], mod[:, 5])
    ga = (2 * (ga >= 0) - 1) * jnp.maximum(jnp.abs(ga), 0.25)
    gb = (2 * (gb >= 0) - 1) * jnp.maximum(jnp.abs(gb), 0.25)
    h = _layernorm(x, axis=-1) * (1 + ca) + sa
    x = x + ga * _L0_attn_ref(h, L0_attn_Wq, L0_attn_Wk, L0_attn_Wv, L0_attn_Wo, L0_attn_Wbet, L0_attn_Wf, L0_attn_norm_w)
    h = _layernorm(x, axis=-1) * (1 + cb) + sb
    x = x + gb * _L0_ffn_ref(h, L0_ffn_qw, L0_ffn_qb, L0_ffn_kw, L0_ffn_kb, L0_ffn_vw, L0_ffn_vb, L0_ffn_ow, L0_ffn_ob, L0_ffn_gate_w, L0_ffn_w1, L0_ffn_w2, L0_ffn_norm1_w, L0_ffn_norm2_w)
    mod = (_silu(L1_c) @ L1_wmod).reshape(L1_c.shape[0], 6, 1, -1)
    sa, ca, ga, sb, cb, gb = (mod[:, 0], mod[:, 1], mod[:, 2], mod[:, 3], mod[:, 4], mod[:, 5])
    ga = (2 * (ga >= 0) - 1) * jnp.maximum(jnp.abs(ga), 0.25)
    gb = (2 * (gb >= 0) - 1) * jnp.maximum(jnp.abs(gb), 0.25)
    h = _layernorm(x, axis=-1) * (1 + ca) + sa
    x = x + ga * _L1_attn_ref(h, L1_attn_Wq, L1_attn_bq, L1_attn_Wk, L1_attn_bk, L1_attn_Wv, L1_attn_bv, L1_attn_Wo, L1_attn_bo, L1_attn_ln1_s, L1_attn_ln1_b, L1_attn_Wf1, L1_attn_bf1, L1_attn_Wf2, L1_attn_bf2, L1_attn_ln2_s, L1_attn_ln2_b)
    h = _layernorm(x, axis=-1) * (1 + cb) + sb
    x = x + gb * _L1_ffn_ref(h, L1_ffn_gate_w, L1_ffn_w1, L1_ffn_w2, L1_ffn_w3)
    return x

_drawn_inputs = setup_inputs


def setup_inputs(seed=0):
    import zlib

    import numpy as np

    out = dict(_drawn_inputs(seed))
    spreads = {'L0_attn_norm_w': (1.0, 0.6),
     'L0_ffn_qb': (0.0, 0.8),
     'L0_ffn_kb': (0.0, 2.0),
     'L0_ffn_vb': (0.0, 0.8),
     'L0_ffn_ob': (0.0, 0.318),
     'L0_ffn_norm1_w': (1.0, 0.2),
     'L0_ffn_norm2_w': (1.0, 0.2),
     'L1_attn_bq': (0.0, 2.0),
     'L1_attn_bk': (0.0, 2.0),
     'L1_attn_bv': (0.0, 0.8),
     'L1_attn_bo': (0.0, 0.293),
     'L1_attn_ln1_s': (1.0, 0.2),
     'L1_attn_ln1_b': (0.0, 0.1),
     'L1_attn_bf1': (0.0, 0.8),
     'L1_attn_bf2': (0.0, 0.275),
     'L1_attn_ln2_s': (1.0, 0.2),
     'L1_attn_ln2_b': (0.0, 0.1)}
    factors = {'L0_attn_Wbet': 8.0,
     'L0_attn_Wf': 8.0,
     'L0_ffn_qw': 8.0,
     'L0_ffn_kw': 8.0,
     'L0_ffn_vw': 8.0,
     'L0_ffn_ow': 8.0,
     'L0_ffn_gate_w': 8.0,
     'L0_ffn_w1': 8.0,
     'L0_ffn_w2': 8.0,
     'L1_attn_Wq': 64.0,
     'L1_attn_Wk': 8.0,
     'L1_attn_Wv': 8.0,
     'L1_attn_Wo': 6.356,
     'L1_attn_Wf1': 3.182,
     'L1_attn_Wf2': 2.983,
     'L1_ffn_gate_w': 8.0,
     'L1_ffn_w1': 8.0,
     'L1_ffn_w2': 8.0,
     'L1_ffn_w3': 8.0}
    for name, (base, spread) in spreads.items():
        noise = np.random.default_rng([zlib.crc32(name.encode()), seed]).standard_normal(out[name].shape)
        drawn = base * np.exp(spread * noise) if base else spread * noise
        out[name] = jnp.asarray(drawn.astype(out[name].dtype))
    for name, factor in factors.items():
        out[name] = (out[name] * factor).astype(out[name].dtype)
    return out
```

```python
from contextlib import ExitStack

import concourse.bass as bass
from concourse import mybir

F32 = mybir.dt.float32
BF16 = mybir.dt.bfloat16
I32 = mybir.dt.int32
ALU = mybir.AluOpType
ACT = mybir.ActivationFunctionType
AX = mybir.AxisListType

P = 128
T = 2048
D = 128
NT = T // P
CH = 512
NC = T // CH
TPC = CH // P
RSQRT_SEED = float(0x5F3759DF - 0x400000)
NEWTON = 3

H0, HD = 16, 8
NKV, REP = 4, 4
E0, F0 = 8, 256
CAP = int(1.25 * T * 2 / E0)
NB, FB = 8, 512
E1, F1 = 8, 352
STACK = 9 * HD


class Chain:

    def __init__(self, eng, sem):
        self.eng, self.sem, self.n = eng, sem, 0

    def link(self, ins):
        self.n += 1
        ins.then_inc(self.sem, 1)
        self.eng.wait_ge(self.sem, self.n)

    def take_back(self, n):
        self.eng.sem_inc(self.sem, n - self.n)
        self.n = n



def build(nc, A, out):
    ctx = ExitStack()
    with ctx:
        def sb(name, shape, dt=F32, stack=ctx):
            return stack.enter_context(nc.sbuf_tensor(name, shape, dt))

        def sem(name):
            return ctx.enter_context(nc.semaphore(name))

        PS = ctx.enter_context(nc.psum_tensor("PS", [P, 8, CH], F32))

        X = sb("X", [P, NT, D])
        Y = sb("Y", [P, NT, D])
        XN = sb("XN", [P, NT, D])
        H = sb("H", [P, NT, D])
        HT = sb("HT", [P, T])
        ident = sb("ident", [P, P])
        st = sb("st", [P, NT, 6])
        ag = sb("ag", [P, NT, 2])
        vh = sb("vh", [P, NT])
        rs = sb("rs", [P, NT])
        nt = sb("nt", [P, NT])
        nb = sb("nb", [P, NT])
        modr = sb("modr", [P, 2, 6, D])
        modc = sb("modc", [P, 2, 6])
        zero1 = sb("zero1", [P, 1])
        eps1 = sb("eps1", [P, 1])

        ch_v, ch_g, ch_a = sem("ch_v"), sem("ch_g"), sem("ch_a")
        s_const = sem("s_const")
        s_done = sem("s_done")
        s_x = sem("s_x")
        s_mod_in = sem("s_mod_in")
        s_sc, s_scb = sem("s_sc"), sem("s_scb")
        s_modps, s_mod = sem("s_modps"), sem("s_mod")
        s_w0 = sem("s_w0")

        def norm_set(tag, **kw):
            s = {n: sem(f"s_{n}{tag}") for n in ("stat", "rstd", "normed", "normg", "turned", "feat", "tok") if n not in kw}
            s.update(kw)
            return s

        SM = norm_set("M")
        S1, S2 = norm_set("A"), norm_set("B")
        S4 = dict(SM, feat=S2["feat"], tok=S2["tok"])

        def upto(k, c):
            return NC * k + c + 1

        def tiles(c):
            return range(TPC * c, TPC * c + TPC)

        def ts_(c):
            return slice(TPC * c, TPC * c + TPC)

        def cs(c):
            return slice(CH * c, CH * c + CH)

        def norm_stats(v, chain, S_, src, c, eps, rms):
            for t in tiles(c):
                last = v.bn_stats(st[:, t, :], src[:, t, :])
            chain.link(last)
            for t in tiles(c):
                last = v.bn_aggr(ag[:, t, :], st[:, t, :])
            chain.link(last)
            if rms:
                chain.link(v.tensor_tensor(vh[:, ts_(c)], ag[:, ts_(c), 0], ag[:, ts_(c), 0], ALU.mult))
                chain.link(v.tensor_tensor(vh[:, ts_(c)], vh[:, ts_(c)], ag[:, ts_(c), 1], ALU.add))
                chain.link(v.tensor_scalar(vh[:, ts_(c)], vh[:, ts_(c)], eps, 0.5, ALU.add, ALU.mult))
            else:
                chain.link(v.tensor_scalar(vh[:, ts_(c)], ag[:, ts_(c), 1], eps, 0.5, ALU.add, ALU.mult))
            v.tensor_scalar(rs[:, ts_(c)].bitcast(I32), vh[:, ts_(c)].bitcast(I32), -0.5, RSQRT_SEED,
                            ALU.mult, ALU.add).then_inc(S_["stat"], 1)

        def norm_rstd(g, chain, S_, k, c, rms):
            g.wait_ge(S_["stat"], upto(k, c))
            a = ts_(c)
            for _ in range(NEWTON):
                chain.link(g.tensor_tensor(nt[:, a], rs[:, a], rs[:, a], ALU.mult))
                chain.link(g.tensor_tensor(nt[:, a], nt[:, a], vh[:, a], ALU.mult))
                chain.link(g.tensor_scalar(nt[:, a], nt[:, a], -1.0, 1.5, ALU.mult, ALU.add))
                chain.link(g.tensor_tensor(rs[:, a], rs[:, a], nt[:, a], ALU.mult))
            if rms:
                g.tensor_scalar(nb[:, a], ag[:, a, 0], 0.0, None, ALU.mult).then_inc(S_["rstd"], 1)
            else:
                chain.link(g.tensor_scalar(nt[:, a], ag[:, a, 0], -1.0, None, ALU.mult))
                g.tensor_tensor(nb[:, a], nt[:, a], rs[:, a], ALU.mult).then_inc(S_["rstd"], 1)

        def norm_apply(a, S_, src, k, c):
            a.wait_ge(S_["rstd"], upto(k, c))
            for t in tiles(c):
                last = a.activation(XN[:, t, :], src[:, t, :], ACT.Identity, scale=rs[:, t:t + 1],
                                    bias=nb[:, t:t + 1])
            last.then_inc(S_["normed"], 1)

        def norm_turn(pe, S_, k, c, free=None):
            pe.wait_ge(S_["normed"], upto(k, c))
            pe.sem_inc(S_["normg"], 1)
            if free:
                pe.wait_ge(*free)
            for j, t in enumerate(tiles(c)):
                last = pe.transpose(PS[:, 7, P * j:P * j + P], XN[:, t, :], ident[:, :])
            last.then_inc(S_["turned"], 1)

        def norm_feat(a, S_, k, c, scale, bias):
            a.wait_ge(S_["turned"], upto(k, c))
            return a.activation(HT[:, cs(c)], PS[:, 7, :], ACT.Identity, scale=scale, bias=bias).then_inc(S_["feat"], 1)

        def norm_tok(g, chain, S_, k, c, scale, bias):
            g.wait_ge(S_["normg"], upto(k, c))
            a = ts_(c)
            m = g.tensor_tensor(H[:, a, :], XN[:, a, :], scale.unsqueeze(1).to_broadcast([P, TPC, D]), ALU.mult)
            if bias is not None:
                chain.link(m)
                m = g.tensor_tensor(H[:, a, :], H[:, a, :], bias.unsqueeze(1).to_broadcast([P, TPC, D]), ALU.add)
            m.then_inc(S_["tok"], 1)

        a0 = ExitStack()
        NQ = 2 * D + 2 * H0
        WC = sb("WC", [P, NQ + D], F32, a0)
        Wo0 = sb("Wo0", [P, D], F32, a0)
        nw0 = sb("nw0", [P, 1], F32, a0)
        scol = sb("scol", [P, 2], F32, a0)
        ccol = sb("ccol", [P, 2], F32, a0)
        scb = sb("scb", [P, 2, P], F32, a0)
        gt = sb("gt", [P, 2, 2, D + 1], F32, a0)
        SG = sb("SG", [P, NT, NQ], F32, a0)
        QK = sb("QK", [P, NT, 2 * D], F32, a0)
        V0 = sb("V0", [P, NT, D], F32, a0)
        KA = sb("KA", [P, NT, D], F32, a0)
        KN = sb("KN", [P, NT, D], F32, a0)
        kn2 = sb("kn2", [P, NT * H0], F32, a0)
        ba = sb("ba", [P, NT, H0], F32, a0)
        S = sb("S", [P, 2, H0, 2 * HD, HD], F32, a0)
        ASPR = sb("ASPR", [P, 2, H0, 2 * HD, HD], F32, a0)
        AS, PR = ASPR[:, 0, :, :, :], ASPR[:, 1, :, :, :]
        QS = sb("QS", [P, 2, H0, 2 * HD, HD], F32, a0)
        wm = QS[:, :, :, :, :].rearrange("p b h c i -> p (b h c i)")[:, 0:2 * 6 * D].rearrange("p (l n) -> p l n", l=2)
        W = sb("W", [P, H0, 2 * HD], F32, a0)
        O = sb("O", [P, NT, H0, 2 * HD], F32, a0)
        hmask = sb("hmask", [P, H0], F32, a0)
        MT = sb("MT", [P, HD, P], F32, a0)
        BD = ASPR[:, :, :, :, :].rearrange("q b h c i -> q (b h c i)").rearrange("q (b s h i) -> q b s h i", b=2, s=16, h=H0)
        NTt = sb("NTt", [P, P, HD], F32, a0)
        SH = sb("SH", [P, P + 1, HD], F32, a0)
        S0t = sb("S0t", [P, H0, HD, HD], F32, a0)

        s_amm, s_asig, s_av, s_aev = sem("s_amm"), sem("s_asig"), sem("s_av"), sem("s_aev")
        s_kn2, s_ksq = sem("s_kn2"), sem("s_ksq")
        s_state, s_as, s_qs, s_red = sem("s_state"), sem("s_as"), sem("s_qs"), sem("s_red")
        s_mt, s_mtc, s_bd, s_bdu = sem("s_mt"), sem("s_mtc"), sem("s_bd"), sem("s_bdu")
        s_nt, s_ntc, s_chain, s_sh = sem("s_nt"), sem("s_ntc"), sem("s_chain"), sem("s_sh")
        s_s0, s_s0c, s_o2, s_o2r = sem("s_s0"), sem("s_s0c"), sem("s_o2"), sem("s_o2r")
        s_on2, s_osq, s_on = sem("s_on2"), sem("s_osq"), sem("s_on")
        s_ot, s_otc, s_op, s_x1 = sem("s_ot"), sem("s_otc"), sem("s_op"), sem("s_x1")
        s_sfc = sem("s_sfc")

        def hb(ap):
            return ap.rearrange("p (h i) -> p h i", h=H0).unsqueeze(2).to_broadcast([P, H0, 2 * HD, HD])

        def sp_pre(sp):
            sp.dma_start(X[:, :, :], A["L0_attn_x"][0].rearrange("(p s) d -> p s d", p=P)).then_inc(s_x, 16)
            at = 0
            for n, w in (("Wq", D), ("Wk", D), ("Wbet", H0), ("Wf", H0), ("Wv", D)):
                sp.dma_start(WC[:, at:at + w], A["L0_attn_" + n]).then_inc(s_w0, 16)
                at += w
            sp.dma_start(Wo0[:, :], A["L0_attn_Wo"]).then_inc(s_w0, 16)
            sp.dma_start(nw0[:, :], A["L0_attn_norm_w"].rearrange("(p a) -> p a", a=1)).then_inc(s_w0, 16)

        def act_pre(a):
            for l in range(2):
                a.dma_start(ccol[:, l:l + 1], A[f"L{l}_c"].rearrange("a d -> d a")).then_inc(s_mod_in, 16)
                a.dma_start(wm[:, l, :], A[f"L{l}_wmod"]).then_inc(s_mod_in, 16)
            a.wait_ge(s_mod_in, 64)
            a.activation(scol[:, :], ccol[:, :], ACT.Silu).then_inc(s_sc, 1)

        def g_pre(g, chain):
            chain.link(g.memset(ident[:, :], 0.0))
            chain.link(g.memset(hmask[:, :], 1.0))
            g.memset(zero1[:, :], 0.0)
            chain.link(g.memset(eps1[:, :], 1e-6))
            chain.link(g.affine_select(out=ident[:, :], in_=ident[:, :], compare_op=ALU.not_equal, fill=1.0,
                                       base=0, pattern=[[-1, P]], channel_multiplier=1))
            chain.link(g.affine_select(out=hmask[:, :], in_=hmask[:, :], compare_op=ALU.is_ge, fill=0.0,
                                       base=0, pattern=[[-HD, H0]], channel_multiplier=1))
            g.affine_select(out=hmask[:, :], in_=hmask[:, :], compare_op=ALU.is_ge, fill=0.0,
                            base=HD - 1, pattern=[[HD, H0]], channel_multiplier=-1).then_inc(s_const, 1)

        def pe_pre(pe):
            pe.wait_ge(s_scb, 1)
            for l in range(2):
                for half in range(2):
                    pe.matmul(PS[:, 2 * l + half, 0:3 * D], scb[:, l, :], wm[:, l, half * 3 * D:(half + 1) * 3 * D],
                              start=True, stop=True)
                for j in range(6):
                    last = pe.matmul(PS[:, 4 + l, j:j + 1], wm[:, l, j * D:(j + 1) * D], scol[:, l:l + 1],
                                     start=True, stop=True)
            last.then_inc(s_modps, 1)

        def v_pre(v, chain):
            v.wait_ge(s_sc, 1)
            v.tensor_copy(scb[:, :, :], scol[:, :].unsqueeze(2).to_broadcast([P, 2, P])).then_inc(s_scb, 1)
            v.wait_ge(s_modps, 1)
            for l in range(2):
                v.tensor_copy(modr[:, l, 0:3, :], PS[:, 2 * l, 0:3 * D].rearrange("p (a d) -> p a d", a=3))
                v.tensor_copy(modr[:, l, 3:6, :], PS[:, 2 * l + 1, 0:3 * D].rearrange("p (a d) -> p a d", a=3))
                last = v.tensor_copy(modc[:, l, :], PS[:, 4 + l, 0:6])
            chain.link(last)
            for l in range(2):
                for j in (1, 4):
                    for m in (modr[:, l, j, :], modc[:, l, j:j + 1]):
                        last = v.tensor_scalar(m, m, 1.0, None, ALU.add)
            chain.link(last)
            for l in range(2):
                for n, j in enumerate((2, 5)):
                    for m, w in ((modr[:, l, j, :], slice(0, D)), (modc[:, l, j:j + 1], slice(D, D + 1))):
                        s, t = gt[:, 0, n, w], gt[:, 1, n, w]
                        v.tensor_scalar(s, m, 0.0, 2.0, ALU.is_ge, ALU.mult)
                        chain.link(v.tensor_scalar(t, m, -1.0, None, ALU.mult))
                        chain.link(v.tensor_tensor(t, t, m, ALU.max))
                        v.tensor_scalar(t, t, 0.25, None, ALU.max)
                        chain.link(v.tensor_scalar(s, s, -1.0, None, ALU.add))
                        chain.link(v.tensor_tensor(m, s, t, ALU.mult))
            v.wait_ge(s_w0, 7 * 16)
            chain.link(v.tensor_scalar(Wo0[:, :], Wo0[:, :], nw0[:, 0:1], None, ALU.mult))
            chain.link(v.tensor_tensor(Wo0[:, :], Wo0[:, :], modr[:, 0, 2, :], ALU.mult))
            v.sem_inc(s_mod, 1)

        def pe_a0(pe):
            pe.wait_ge(s_w0, 7 * 16)
            for s in range(NT):
                pe.wait_ge(SM["feat"], s // TPC + 1)
                if s >= 4:
                    pe.wait_ge(s_aev, s - 3)
                    pe.wait_ge(s_av, s - 3)
                pe.matmul(PS[:, s % 4, 0:NQ + D], HT[:, P * s:P * s + P], WC[:, :], start=True, stop=True).then_inc(s_amm, 1)

        def act_a0(a):
            for s in range(NT):
                a.wait_ge(s_amm, s + 1)
                a.activation(SG[:, s, :], PS[:, s % 4, 0:NQ], ACT.Sigmoid).then_inc(s_asig, 1)
                a.activation(V0[:, s, :], PS[:, s % 4, NQ:NQ + D], ACT.Copy).then_inc(s_av, 1)
            a.wait_ge(s_kn2, 1)
            a.activation(kn2[:, :], kn2[:, :], ACT.Sqrt).then_inc(s_ksq, 1)

        def v_a0(v, chain):
            for s in range(NT):
                v.wait_ge(s_av, s + 1)
                v.tensor_tensor(QK[:, s, :], PS[:, s % 4, 0:2 * D], SG[:, s, 0:2 * D], ALU.mult).then_inc(s_aev, 1)
            v.wait_ge(s_aev, NT)
            v.wait_ge(s_av, NT)
            kv = QK[:, :, D:2 * D]
            chain.link(v.tensor_tensor(KN[:, :, :], kv, kv, ALU.mult))
            chain.link(v.tensor_reduce(kn2[:, :], KN[:, :, :].rearrange("p s (h i) -> p (s h) i", i=HD), AX.X, ALU.add))
            v.tensor_scalar(kn2[:, :], kn2[:, :], 1e-12, None, ALU.add).then_inc(s_kn2, 1)
            beta = SG[:, :, 2 * D:2 * D + H0]
            alpha = SG[:, :, 2 * D + H0:NQ]
            chain.link(v.tensor_scalar(beta, beta, 2.0, None, ALU.mult))
            chain.link(v.tensor_scalar(ba[:, :, :], alpha, -1.0, None, ALU.mult))
            chain.link(v.tensor_tensor(ba[:, :, :], ba[:, :, :], beta, ALU.mult))
            v4 = V0[:, :, :].rearrange("p s (h c) -> p s h c", h=H0)
            chain.link(v.tensor_tensor(v4, v4, beta.unsqueeze(3).to_broadcast([P, NT, H0, HD]), ALU.mult))
            v.wait_ge(s_ksq, 1)
            chain.link(v.reciprocal(kn2[:, :], kn2[:, :]))
            chain.link(v.tensor_tensor(KN[:, :, :].rearrange("p s (h i) -> p s h i", h=H0),
                                       kv.rearrange("p s (h i) -> p s h i", h=H0),
                                       kn2[:, :].rearrange("p (s h) -> p s h", s=NT).unsqueeze(3).to_broadcast([P, NT, H0, HD]),
                                       ALU.mult))
            chain.link(v.tensor_tensor(KA[:, :, :].rearrange("p s (h i) -> p s h i", h=H0),
                                       KN[:, :, :].rearrange("p s (h i) -> p s h i", h=H0),
                                       ba[:, :, :].unsqueeze(3).to_broadcast([P, NT, H0, HD]), ALU.mult))
            chain.link(v.memset(S[:, 0, :, :, :], 0.0))
            v.memset(S[:, 0, :, :, :].rearrange("p h c i -> p h (c i)")[:, :, HD * HD::HD + 1], 1.0).then_inc(s_state, 1)

            for s in range(NT):
                cur, nxt = s % 2, (s + 1) % 2
                v.wait_ge(s_state, s + 1)
                chain.link(v.tensor_tensor(PR[:, :, :, :], hb(KA[:, s, :]), S[:, cur, :, :, :], ALU.mult))
                chain.link(v.tensor_reduce(W[:, :, :], PR[:, :, :, :], AX.X, ALU.add))
                chain.link(v.tensor_tensor(W[:, :, 0:HD], W[:, :, 0:HD], V0[:, s, :].rearrange("p (h c) -> p h c", h=H0), ALU.add))
                chain.link(v.tensor_tensor(PR[:, :, :, :], hb(KN[:, s, :]),
                                           W[:, :, :].unsqueeze(3).to_broadcast([P, H0, 2 * HD, HD]), ALU.mult))
                v.wait_ge(s_as, s + 1)
                if s >= 1:
                    v.wait_ge(s_qs, s - 0)
                v.tensor_tensor(S[:, nxt, :, :, :], PR[:, :, :, :], AS[:, :, :, :], ALU.add).then_inc(s_state, 1)
                if s >= 1:
                    v.tensor_reduce(O[:, s - 1, :, :], QS[:, (s - 1) % 2, :, :, :], AX.X, ALU.add).then_inc(s_red, 1)
            v.wait_ge(s_qs, NT)
            v.tensor_reduce(O[:, NT - 1, :, :], QS[:, (NT - 1) % 2, :, :, :], AX.X, ALU.add).then_inc(s_red, 1)
            v.wait_ge(s_red, NT)
            v.tensor_copy(SC[:, 0, :, :].rearrange("p c (h i) -> p c h i", h=H0), SF[:, :, 0:HD, :].rearrange("p h c i -> p c h i")).then_inc(s_sfc, 1)
            v.tensor_copy(SC[:, 1, :, :].rearrange("p i (h j) -> p i h j", h=H0), SF[:, :, HD:2 * HD, :].rearrange("p h j i -> p i h j")).then_inc(s_sfc, 1)

        def g_a0(g):
            for s in range(NT):
                cur = s % 2
                g.wait_ge(s_state, s + 1)
                al = SG[:, s, 2 * D + H0:NQ].unsqueeze(2).to_broadcast([P, H0, 2 * HD * HD])
                g.tensor_tensor(AS[:, :, :, :].rearrange("p h c i -> p h (c i)"), al,
                                S[:, cur, :, :, :].rearrange("p h c i -> p h (c i)"), ALU.mult).then_inc(s_as, 1)
                if s >= 1:
                    if s >= 3:
                        g.wait_ge(s_red, s - 2)
                    g.tensor_tensor(QS[:, (s - 1) % 2, :, :, :], hb(QK[:, s - 1, 0:D]), S[:, cur, :, :, :], ALU.mult).then_inc(s_qs, 1)
            g.wait_ge(s_state, NT + 1)
            g.wait_ge(s_red, NT - 2)
            g.tensor_tensor(QS[:, (NT - 1) % 2, :, :, :], hb(QK[:, NT - 1, 0:D]), S[:, NT % 2, :, :, :], ALU.mult).then_inc(s_qs, 1)
            g.wait_ge(s_mtc, 1)
            for k in range(P // 16):
                if k >= 2:
                    g.wait_ge(s_bdu, k - 1)
                g.tensor_tensor(BD[:, k % 2, :, :, :],
                                MT[:, :, 16 * k:16 * k + 16].rearrange("q i p -> q p i").unsqueeze(2).to_broadcast([P, 16, H0, HD]),
                                hmask[:, :].unsqueeze(1).unsqueeze(3).to_broadcast([P, 16, H0, HD]), ALU.mult).then_inc(s_bd, 1)

        SF = S[:, NT % 2, :, :, :]
        SC = QS[:, 0, :, :, :].rearrange("p h c i -> p (h c i)").rearrange("p (b a n) -> p b a n", b=2, a=HD)

        def pe_chain(pe):
            pe.wait_ge(s_sfc, 2)
            for c in range(HD):
                last = pe.transpose(PS[:, c // 4, P * (c % 4):P * (c % 4) + P], SC[:, 0, c, :], ident[:, :])
            last.then_inc(s_nt, 1)
            for i in range(HD):
                last = pe.transpose(PS[:, 2 + i // 4, P * (i % 4):P * (i % 4) + P], SC[:, 1, i, :], ident[:, :])
            last.then_inc(s_mt, 1)
            pe.wait_ge(s_ntc, 1)
            n_flat = NTt[:, :, :].rearrange("q p c -> q (p c)")
            for half in range(2):
                last = pe.matmul(PS[:, 4 + half, :], ident[:, :], n_flat[:, CH * half:CH * half + CH], start=True, stop=False,
                                 skip_group_check=True)
            last.then_inc(s_chain, 1)
            for p in range(1, P - 1):
                if p % 16 == 0 or p == 1:
                    pe.wait_ge(s_bd, p // 16 + 1)
                pe.wait_ge(s_sh, p)
                at = HD * p
                m = pe.matmul(PS[:, 4 + at // CH, at % CH:at % CH + HD],
                              BD[:, p // 16 % 2, p % 16, :, :].rearrange("q h i -> q (h i)"), SH[:, p, :],
                              start=False, stop=True, skip_group_check=True)
                m.then_inc(s_chain, 1)
                if p % 16 == 15:
                    pe.wait_ge(s_chain, p + 1)
                    pe.sem_inc(s_bdu, 1)
            pe.wait_ge(s_sh, P - 1)
            for c in range(HD):
                last = pe.transpose(PS[:, c // 4, P * (c % 4):P * (c % 4) + P], SH[:, 0:P, c], ident[:, :])
            last.then_inc(s_s0, 1)

        def v_chain(v, chain):
            v.wait_ge(s_nt, 1)
            v.tensor_copy(SH[:, 0, :], zero1[:, 0:1].to_broadcast([P, HD]))
            v.tensor_copy(NTt[:, :, :].rearrange("q p c -> q c p"),
                          PS[:, 0:2, :].rearrange("q b n -> q (b n)").rearrange("q (c p) -> q c p", c=HD)).then_inc(s_ntc, 1)
            v.wait_ge(s_mt, 1)
            v.tensor_copy(MT[:, :, :], PS[:, 2:4, :].rearrange("q b n -> q (b n)").rearrange("q (i p) -> q i p", i=HD)).then_inc(s_mtc, 1)
            for p in range(1, P):
                v.wait_ge(s_chain, p)
                at = HD * (p - 1)
                v.tensor_copy(SH[:, p, :], PS[:, 4 + at // CH, at % CH:at % CH + HD]).then_inc(s_sh, 1)
            v.wait_ge(s_s0, 1)
            v.tensor_copy(S0t[:, :, :, :].rearrange("p h c i -> p c h i"),
                          PS[:, 0:2, :].rearrange("p b n -> p (b n)").rearrange("p (c h i) -> p c h i", c=HD, h=H0)).then_inc(s_s0c, 1)

        def half_pr(s):
            return QS[:, s % 2, :, 0:HD, :]

        def g_out(g):
            for s in range(NT):
                if s == 0:
                    g.wait_ge(s_s0c, 1)
                if s == 0:
                    g.wait_ge(s_red, NT)
                if s >= 2:
                    g.wait_ge(s_o2r, s - 1)
                g.tensor_tensor(half_pr(s), O[:, s, :, HD:2 * HD].unsqueeze(2).to_broadcast([P, H0, HD, HD]),
                                S0t[:, :, :, :], ALU.mult).then_inc(s_o2, 1)

        def v_out(v, chain):
            OR = PR[:, :, :, :].rearrange("p h c i -> p (h c i)").rearrange("p (s d) -> p s d", s=NT)
            for s in range(NT):
                v.wait_ge(s_o2, s + 1)
                v.tensor_reduce(OR[:, s, :].rearrange("p (h c) -> p h c", h=H0), half_pr(s), AX.X, ALU.add).then_inc(s_o2r, 1)
            v.wait_ge(s_o2r, NT)
            O4 = OR.rearrange("p s (h c) -> p s h c", h=H0)
            chain.link(v.tensor_tensor(O4, O4, O[:, :, :, 0:HD], ALU.add))
            chain.link(v.tensor_tensor(KN[:, :, :], OR, OR, ALU.mult))
            chain.link(v.tensor_reduce(kn2[:, :], KN[:, :, :].rearrange("p s (h i) -> p (s h) i", i=HD), AX.X, ALU.add))
            v.tensor_scalar(kn2[:, :], kn2[:, :], 1.0 / HD, 1e-6, ALU.mult, ALU.add).then_inc(s_on2, 1)
            v.wait_ge(s_osq, 1)
            chain.link(v.reciprocal(kn2[:, :], kn2[:, :]))
            v.tensor_tensor(Y[:, :, :].rearrange("p s (h c) -> p s h c", h=H0), O4,
                            kn2[:, :].rearrange("p (s h) -> p s h", s=NT).unsqueeze(3).to_broadcast([P, NT, H0, HD]),
                            ALU.mult).then_inc(s_on, 1)
            for c in range(NC):
                v.wait_ge(s_ot, c + 1)
                v.tensor_copy(HT[:, cs(c)], PS[:, c % 2, :]).then_inc(s_otc, 1)
            for c in range(NC):
                v.wait_ge(s_op, c + 1)
                v.tensor_tensor(X[:, ts_(c), :], X[:, ts_(c), :], PS[:, 2 + c % 2, :].rearrange("p (t d) -> p t d", t=TPC),
                                ALU.add).then_inc(s_x1, 1)

        def act_out(a):
            a.wait_ge(s_on2, 1)
            a.activation(kn2[:, :], kn2[:, :], ACT.Sqrt).then_inc(s_osq, 1)

        def pe_out(pe):
            pe.wait_ge(s_on, 1)
            for c in range(NC):
                if c >= 2:
                    pe.wait_ge(s_otc, c - 1)
                for j, t in enumerate(tiles(c)):
                    last = pe.transpose(PS[:, c % 2, P * j:P * j + P], Y[:, t, :], ident[:, :])
                last.then_inc(s_ot, 1)
            for c in range(NC):
                pe.wait_ge(s_otc, c + 1)
                if c >= 2:
                    pe.wait_ge(s_x1, c - 1)
                for j, t in enumerate(tiles(c)):
                    last = pe.matmul(PS[:, 2 + c % 2, P * j:P * j + P], HT[:, P * t:P * t + P], Wo0[:, :], start=True, stop=True)
                last.then_inc(s_op, 1)
        a0.close()

        norms_w = {n: sb("g_" + n, [P, w]) for n, w in (("n1r", D), ("n1c", 1), ("n2r", D))}
        rank8 = sb("rank8", [P, 8])
        below = sb("below", [P, P])
        b0 = ExitStack()
        gw = {n: sb("g_" + n, [P, w], F32, b0) for n, w in
              (("qw", D), ("kw", NKV * HD), ("vw", NKV * HD), ("ow", D), ("vb", NKV * HD), ("ob", D), ("qb", 1), ("kb", 1))}
        gw.update(norms_w)
        QST = sb("QST", [STACK + 3, H0, T], BF16, b0)
        KST = sb("KST", [STACK + 3, NKV, T], BF16, b0)
        VS = sb("VS", [P, NT, NKV, 32], F32, b0)
        tmpb = sb("tmpb", [P, 6 * T], BF16, b0)
        QP = tmpb[:, 0:3 * T].rearrange("p (a n) -> p a n", a=3)
        KP = tmpb[0:NKV * HD, 3 * T:6 * T].rearrange("p (a n) -> p a n", a=3)
        PB = tmpb[:, 0:4 * T].bitcast(F32).rearrange("p (b j n) -> p b j n", b=2, j=REP)
        AO = tmpb[:, 4 * T:6 * T].bitcast(F32).rearrange("p (s d) -> p s d", s=NT)
        PV = sb("PV", [P, CH], F32, b0)
        MX = sb("MX", [P, REP * TPC, NC], F32, b0)
        MM = sb("MM", [P, REP * TPC], F32, b0)
        NM = sb("NM", [REP * TPC, P], F32, b0)
        NMP = sb("NMP", [REP * TPC, 2, 3, P], BF16, b0)
        VG = sb("VG", [P, NT, 32], F32, b0)
        RD = sb("RD", [P, TPC, REP], F32, b0)
        scr_q = nc.dram_tensor("scr_q", (3, P, T), BF16).ap()
        scr_k = nc.dram_tensor("scr_k", (3, NKV * HD, T), BF16).ap()

        s_gw = sem("s_gw")
        s_b0q, s_b0k, s_b0v = sem("s_b0q"), sem("s_b0k"), sem("s_b0v")
        s_q32, s_k32, s_split, s_vs = sem("s_q32"), sem("s_k32"), sem("s_split"), sem("s_vs")
        s_scr, s_stack = sem("s_scr"), sem("s_stack")
        s_mxmm, s_mxred, s_mm = sem("s_mxmm"), sem("s_mxred"), sem("s_mm")
        s_mt0, s_nm, s_nmp = sem("s_mt0"), sem("s_nm"), sem("s_nmp")
        s_row = [sem(f"s_row{k}") for k in range(2)]
        s_qk, s_exp, s_pv = sem("s_qk"), sem("s_exp"), sem("s_pv")
        s_pvc, s_pvt, s_ao = sem("s_pvc"), sem("s_pvt"), sem("s_ao")
        s_at, s_atc, s_ow, s_src = sem("s_at"), sem("s_atc"), sem("s_ow"), sem("s_src")

        s_vg, s_const2, s_nmfree, s_pvfree = sem("s_vg"), sem("s_const2"), sem("s_nmfree"), sem("s_pvfree")
        UI = NT * REP

        def sp_gqa(sp):
            f = "L0_ffn_"
            for n in ("qw", "kw", "vw", "ow"):
                sp.dma_start(gw[n][:, :], A[f + n]).then_inc(s_gw, 16)
            for n, w in (("vb", "vb"), ("ob", "ob"), ("n1r", "norm1_w"), ("n2r", "norm2_w")):
                sp.dma_start(gw[n][:, :], A[f + w].partition_broadcast(P)).then_inc(s_gw, 16)
            sp.dma_start(gw["qb"][:, :], A[f + "qb"].rearrange("(p a) -> p a", a=1)).then_inc(s_gw, 16)
            sp.dma_start(gw["kb"][0:NKV * HD, :], A[f + "kb"].rearrange("(p a) -> p a", a=1)).then_inc(s_gw, 16)
            sp.dma_start(gw["n1c"][:, :], A[f + "norm1_w"].rearrange("(p a) -> p a", a=1)).then_inc(s_gw, 16)

        GW = 11 * 16

        def sp_stacks(sp):
            sp.wait_ge(s_split, 2)
            sp.dma_start(scr_k.rearrange("a r n -> r a n"), KP).then_inc(s_scr, 16)
            sp.dma_start(scr_q.rearrange("a r n -> r a n"), QP).then_inc(s_scr, 16)
            sp.wait_ge(s_const2, 1)
            sp.wait_ge(s_scr, 32)
            for g in range(NKV):
                for a in range(3):
                    for b in range(3):
                        sp.dma_start(KST[(3 * a + b) * HD:(3 * a + b + 1) * HD, g, :], scr_k[b, HD * g:HD * g + HD, :]).then_inc(s_stack, 16)
            for a in range(3):
                for b in range(3):
                    sp.dma_start(QST[(3 * a + b) * HD:(3 * a + b + 1) * HD, :, :],
                                 scr_q[a].rearrange("(h i) n -> i h n", i=HD)).then_inc(s_stack, 16)

        STACKED = (NKV * 9 + 9) * 16

        def g_gqa_pre(g, chain):
            chain.link(g.memset(KST[64:STACK + 3, :, :], 1.0))
            g.memset(VS[:, :, :, :], 0.0).then_inc(s_const2, 1)

        def pe_gqa_pre(pe):
            pe.wait_ge(s_gw, GW)
            for c in range(NC):
                pe.wait_ge(SM["feat"], upto(1, c))
                pe.matmul(PS[:, c, :], gw["qw"][:, :], HT[:, cs(c)], start=True, stop=True).then_inc(s_b0q, 1)
            for c in range(NC):
                if c < 2:
                    pe.matmul(PS[0:NKV * HD, 4 + c, :], gw["kw"][:, :], HT[:, cs(c)], start=True, stop=True).then_inc(s_b0k, 1)
            for c in range(2, NC):
                pe.wait_ge(s_k32, c - 1)
                pe.matmul(PS[0:NKV * HD, 2 + c, :], gw["kw"][:, :], HT[:, cs(c)], start=True, stop=True).then_inc(s_b0k, 1)
            for t in range(NT):
                last = pe.matmul(PS[:, 6, 32 * t:32 * t + 32], HT[:, P * t:P * t + P], gw["vw"][:, :], start=True, stop=True)
            last.then_inc(s_b0v, 1)

        def act_gqa_pre(a):
            a.wait_ge(s_gw, GW)
            for c in range(NC):
                a.wait_ge(s_b0q, c + 1)
                a.activation(Y[:, :, :].rearrange("p s d -> p (s d)")[:, cs(c)], PS[:, c, :], ACT.Identity, bias=gw["qb"][:, 0:1]).then_inc(s_q32, 1)
            a.wait_ge(SM["tok"], NC)
            for c in range(NC):
                a.wait_ge(s_b0k, c + 1)
                a.activation(PVK[:, cs(c)], PS[0:NKV * HD, 4 + c % 2, :], ACT.Identity, bias=gw["kb"][0:NKV * HD, 0:1]).then_inc(s_k32, 1)

        PVK = XN[0:NKV * HD, :, :].rearrange("p s d -> p (s d)")

        def v_gqa_pre(v, chain):
            yq = Y[:, :, :].rearrange("p s d -> p (s d)")
            v.wait_ge(s_k32, NC)
            for x, q in ((PVK, KP), (yq, QP)):
                if x is yq:
                    v.wait_ge(s_q32, NC)
                chain.link(v.tensor_copy(q[:, 0, :], x))
                chain.link(v.tensor_tensor(x, x, q[:, 0, :], ALU.subtract))
                chain.link(v.tensor_copy(q[:, 1, :], x))
                v.tensor_tensor(q[:, 2, :], x, q[:, 1, :], ALU.subtract).then_inc(s_split, 1)
            v.wait_ge(s_b0v, 1)
            v.wait_ge(s_const2, 1)
            v.memset(VS[:, :, :, HD:HD + 1], 1.0)
            v.tensor_tensor(VS[:, :, :, 0:HD], PS[:, 6, :].rearrange("p (t g c) -> p t g c", t=NT, g=NKV),
                            gw["vb"][:, :].rearrange("p (g c) -> p g c", g=NKV).unsqueeze(1).to_broadcast([P, NT, NKV, HD]),
                            ALU.add).then_inc(s_vs, 1)

        def pe_max(pe, g, u, kt):
            g, qc = (g, u) if u < NC else (g + 1, u - NC)
            j, t = kt // TPC, kt % TPC
            for kc in range(NC):
                m = kt * NC + kc
                pe.wait_ge(s_mxred, u * UI + m + 1)
                pe.matmul(PS[:, 5 + m % 2, :], QST[0:STACK, REP * g + j, CH * qc + P * t:CH * qc + P * t + P],
                          KST[0:STACK, g, cs(kc)], start=True, stop=True).then_inc(s_mxmm, 1)

        def v_max(v, chain, u):
            for m in range(UI):
                v.wait_ge(s_mxmm, u * UI + m + 1)
                r = v.tensor_reduce(MX[:, m // NC, m % NC:m % NC + 1], PS[:, 5 + m % 2, :], AX.X, ALU.max)
                if m < UI - 1:
                    r.then_inc(s_mxred, 1)
            chain.link(r)
            v.sem_inc(s_mxred, 1)
            v.tensor_reduce(MM[:, :], MX[:, :, :], AX.X, ALU.max).then_inc(s_mm, 1)

        def pe_rows(pe, u):
            pe.wait_ge(s_mm, u + 1)
            pe.transpose(PS[0:REP * TPC, 7, 0:P], MM[:, :], ident[:, :]).then_inc(s_mt0, 1)

        def v_rows(v, chain, u):
            v.wait_ge(s_mt0, u + 1)
            chain.link(v.tensor_scalar(NM[:, :], PS[0:REP * TPC, 7, 0:P], -1.0, None, ALU.mult))
            v.sem_inc(s_nm, 1)
            v.wait_ge(s_nmfree, u + 1)
            part = NMP[:, u % 2, :, :]
            chain.link(v.tensor_copy(part[:, 0, :], NM[:, :]))
            chain.link(v.tensor_tensor(NM[:, :], NM[:, :], part[:, 0, :], ALU.subtract))
            chain.link(v.tensor_copy(part[:, 1, :], NM[:, :]))
            v.tensor_tensor(part[:, 2, :], NM[:, :], part[:, 1, :], ALU.subtract).then_inc(s_nmp, 1)

        def sp_rows(sp, g, u):
            g, qc = (g, u) if u < NC else (g + 1, u - NC)
            sp.wait_ge(s_nmp, u + 1)
            for a in range(3):
                for j in range(REP):
                    sp.dma_start(QST[STACK + a:STACK + a + 1, REP * g + j, cs(qc)].rearrange("r (t p) -> r t p", p=P),
                                 NMP[TPC * j:TPC * j + TPC, u % 2, a, :]).then_inc(s_row[u % 2], 16)

        ROWS = 3 * REP * 16

        def pe_unit(pe, g, u, ahead):
            def scores(kt):
                for j in range(REP):
                    pe.wait_ge(s_exp, u * UI + kt * REP + j + 1)
                    pe.matmul(PS[:, j, :], KST[0:STACK + 3, g, P * kt:P * kt + P],
                              QST[0:STACK + 3, REP * g + j, cs(u)], start=True, stop=True).then_inc(s_qk, 1)

            def values(kt):
                if kt == 0:
                    pe.wait_ge(s_pvc, u + 1)
                pe.wait_ge(s_exp, u * UI + kt * REP + 2 * REP)
                for j in range(REP):
                    last = pe.matmul(PS[32 * j:32 * j + 32, 4, :], VG[:, kt, :], PB[:, kt % 2, j, :],
                                     start=(kt == 0), stop=(kt == NT - 1), tile_position=(0, 32 * j), skip_group_check=True)
                last.then_inc(s_pv, 1)

            pe.wait_ge(s_row[u % 2], ROWS * (u // 2 + 1))
            pe.sem_inc(s_nmfree, 1)
            if u == 0:
                pe.wait_ge(s_vg, 1)
            for kt in range(NT):
                scores(kt)
                if kt:
                    values(kt - 1)
                if ahead:
                    pe_max(pe, g, u + 2, kt)
            values(NT - 1)
            if ahead:
                pe_rows(pe, u + 2)
            pe.wait_ge(s_nm, u + 3 if ahead else NC)
            pe.wait_ge(s_ao, u + 1)
            pe.wait_ge(s_pvc, u + 2)
            for t in range(TPC):
                m = pe.transpose(PS[:, 7, P * t:P * t + P], PV[:, P * t:P * t + P], ident[:, :])
            m.then_inc(s_pvt, 1)

        def act_unit(a, u):
            for kt in range(NT):
                a.wait_ge(s_pv, u * NT + kt + 1)
                for j in range(REP):
                    a.wait_ge(s_qk, u * UI + kt * REP + j + 1)
                    a.activation(PB[:, kt % 2, j, :], PS[:, j, :], ACT.Exp, scale=HD ** -0.5).then_inc(s_exp, 1)
            a.wait_ge(s_pv, u * NT + NT + 2)
            a.wait_ge(s_pvfree, u + 1)
            a.activation(PV[:, :], PS[:, 4, :], ACT.Copy).then_inc(s_pvc, 1)

        def v_unit(v, chain, g, u, ahead):
            if ahead:
                v_max(v, chain, u + 2)
                v_rows(v, chain, u + 2)
            v.wait_ge(s_pvt, u + 1)
            v.sem_inc(s_pvfree, 1)
            b7 = PS[:, 7, :].rearrange("p (t j c) -> p t j c", t=TPC, j=REP)
            chain.link(v.reciprocal(RD[:, :, :], b7[:, :, :, HD]))
            ao = AO[:, TPC * u:TPC * u + TPC, bass.ds(g * 32, 32)].rearrange("p t (j c) -> p t j c", j=REP)
            v.tensor_tensor(ao, b7[:, :, :, 0:HD], RD[:, :, :].unsqueeze(3).to_broadcast([P, TPC, REP, HD]), ALU.mult).then_inc(s_ao, 1)

        LAST = NKV - 1

        def sp_gqa_rows(sp):
            for u in range(2):
                sp_rows(sp, 0, u)
            with sp.Fori(0, LAST) as g:
                for u in range(NC):
                    sp_rows(sp, g, u + 2)
                sp.sem_inc(s_nmp, -NC)
            for u in range(2):
                sp_rows(sp, LAST, u + 2)

        def pe_gqa(pe):
            pe.sem_inc(s_pv, 2)
            pe.sem_inc(s_nmfree, 2)
            pe.wait_ge(s_stack, STACKED)
            pe.wait_ge(s_vs, 1)
            for u in range(2):
                for kt in range(NT):
                    pe_max(pe, 0, u, kt)
                if u:
                    pe.wait_ge(s_nm, u)
                pe_rows(pe, u)
            with pe.Fori(0, LAST) as g:
                for u in range(NC):
                    pe_unit(pe, g, u, True)
                pe.sem_inc(s_mxred, -NC * UI)
                pe.sem_inc(s_mm, -NC)
                for s in s_row:
                    pe.sem_inc(s, -NC // 2 * ROWS)
                pe.sem_inc(s_exp, -NC * UI)
                pe.sem_inc(s_pvc, -NC)
                pe.sem_inc(s_vg, -1)
                pe.sem_inc(s_nm, -NC)
                pe.sem_inc(s_ao, -NC)
            for u in range(NC):
                pe_unit(pe, LAST, u, u < 2)
            pe.wait_ge(s_ao, NC + 1)
            for c in range(NC):
                if c >= 2:
                    pe.wait_ge(s_atc, c - 1)
                for j, t in enumerate(tiles(c)):
                    last = pe.transpose(PS[:, c % 2, P * j:P * j + P], AO[:, t, :], ident[:, :])
                last.then_inc(s_at, 1)
            for c in range(NC):
                pe.wait_ge(s_atc, c + 1)
                if c >= 2:
                    pe.wait_ge(s_src, c - 1)
                for j, t in enumerate(tiles(c)):
                    last = pe.matmul(PS[:, 2 + c % 2, P * j:P * j + P], AT[:, P * t:P * t + P], gw["ow"][:, :], start=True, stop=True)
                last.then_inc(s_ow, 1)

        AT = XN[:, :, :].rearrange("p s d -> p (s d)")

        def act_gqa(a):
            a.sem_inc(s_exp, REP)
            a.sem_inc(s_pvc, 1)
            with a.Fori(0, LAST):
                for u in range(NC):
                    act_unit(a, u)
                a.sem_inc(s_pv, -NC * NT)
                a.sem_inc(s_qk, -NC * UI)
                a.sem_inc(s_pvfree, -NC)
            for u in range(NC):
                act_unit(a, u)
            for c in range(NC):
                a.wait_ge(s_at, c + 1)
                a.activation(AT[:, cs(c)], PS[:, c % 2, :], ACT.Copy).then_inc(s_atc, 1)

        def v_gqa(v, chain):
            v.sem_inc(s_mxred, 2)
            v.sem_inc(s_ao, 1)
            v.sem_inc(s_pvfree, 1)

            def head(g):
                v.tensor_copy(VG[:, :, :], VS[:, :, bass.ds(g, 1), :].rearrange("p t g c -> p t (g c)")).then_inc(s_vg, 1)

            for u in range(2):
                v_max(v, chain, u)
                v_rows(v, chain, u)
            with v.Fori(0, LAST) as g:
                n = chain.n
                head(g)
                for u in range(NC):
                    v_unit(v, chain, g, u, True)
                chain.take_back(n)
                v.sem_inc(s_mxmm, -NC * UI)
                v.sem_inc(s_mt0, -NC)
                v.sem_inc(s_nmfree, -NC)
                v.sem_inc(s_pvt, -NC)
            head(LAST)
            for u in range(NC):
                v_unit(v, chain, LAST, u, u < 2)
            obr = gw["ob"][:, :].unsqueeze(1).to_broadcast([P, TPC, D])
            v.wait_ge(SM["tok"], NC)
            for c in range(NC):
                v.wait_ge(s_ow, c + 1)
                chain.link(v.tensor_tensor(Y[:, ts_(c), :], PS[:, 2 + c % 2, :].rearrange("p (t d) -> p t d", t=TPC), obr, ALU.add))
                last = v.tensor_tensor(Y[:, ts_(c), :], Y[:, ts_(c), :], H[:, ts_(c), :], ALU.add)
                chain.link(last)
                v.sem_inc(s_src, 1)

        b0.close()

        RS = {"s_" + n: sem(f"s_r{n}") for n in ("in", "mm", "l", "p", "pd", "w", "tr", "trc", "scr", "cnt", "cntd")}

        def router(tag, stack, E, nth):
            r = {n: sb(f"{n}{tag}", [P, NT, E], F32, stack) for n in ("L", "p", "one", "two", "t", "u", "wt")}
            r.update({n: sb(f"{n}{tag}", [P, NT], F32, stack) for n in ("m", "k")})
            r["gate"] = sb(f"gate{tag}", [P, E], F32, stack)
            r["wtT"] = sb(f"wtT{tag}", [P, P], F32, stack)
            r.update(RS, nth=nth)
            r["scr"] = nc.dram_tensor(f"scr_w{tag}", (NT, E, P), F32).ap()
            return r

        def pe_router(pe, r, feat, arrived):
            pe.wait_ge(r["s_in"], arrived)
            pe.wait_ge(SM["feat"], feat)
            for t in range(NT):
                last = pe.matmul(PS[:, 4, 8 * t:8 * t + 8], HT[:, P * t:P * t + P], r["gate"][:, :], start=True, stop=True)
            last.then_inc(r["s_mm"], 1)

        def bc(ap):
            return ap.unsqueeze(2).to_broadcast([P, NT, 8])

        def v_logits(v, chain, r):
            v.wait_ge(r["s_mm"], r["nth"])
            chain.link(v.tensor_copy(r["L"][:, :, :], PS[:, 4, 0:8 * NT].rearrange("p (t e) -> p t e", e=8)))

        def v_top2(v, chain, r):
            L, t, m, k = r["L"], r["t"], r["m"], r["k"]
            for n, one in enumerate(("one", "two")):
                src = L
                if n:
                    chain.link(v.tensor_scalar(r["u"][:, :, :], r["one"][:, :, :], -1e30, None, ALU.mult))
                    chain.link(v.tensor_tensor(r["u"][:, :, :], r["u"][:, :, :], L[:, :, :], ALU.add))
                    src = r["u"]
                chain.link(v.tensor_reduce(m[:, :], src[:, :, :], AX.X, ALU.max))
                chain.link(v.tensor_tensor(t[:, :, :], src[:, :, :], bc(m[:, :]), ALU.is_equal))
                chain.link(v.tensor_tensor(t[:, :, :], t[:, :, :], rank8[:, :].unsqueeze(1).to_broadcast([P, NT, 8]), ALU.mult))
                chain.link(v.tensor_reduce(k[:, :], t[:, :, :], AX.X, ALU.max))
                chain.link(v.tensor_tensor(r[one][:, :, :], t[:, :, :], bc(k[:, :]), ALU.is_equal))

        def pe_weights(pe, r):
            pe.wait_ge(r["s_w"], r["nth"])
            pe.transpose(PS[:, 5, 0:P], r["wt"][:, :, :].rearrange("p s e -> p (s e)"), ident[:, :]).then_inc(r["s_tr"], 1)

        def v_weights(v, chain, r):
            v.wait_ge(r["s_tr"], r["nth"])
            chain.link(v.tensor_copy(r["wtT"][:, :], PS[:, 5, 0:P]))
            v.sem_inc(r["s_trc"], 1)
            v.sem_inc(r["s_pd"], 1)

        def sp_weights(sp, r):
            sp.wait_ge(r["s_trc"], r["nth"])
            sp.dma_start(r["scr"].rearrange("s e p -> (s e) p"), r["wtT"][:, :]).then_inc(r["s_scr"], 16)
            sp.wait_ge(r["s_scr"], 16 * r["nth"])

        def weight_row(r, e):
            return r["scr"].rearrange("s e p -> e s p")[e].partition_broadcast(P)

        c0 = ExitStack()
        R0 = router("0", c0, E0, 1)
        W1 = sb("W1", [P, 2, F0], F32, c0)
        W2 = sb("W2", [P, 2, F0 // P, D], F32, c0)
        SB = sb("SB", [P, 2, NT, P], F32, c0)
        HID = sb("HID", [P, 4, CH], F32, c0)
        OT = sb("OT", [P, T], F32, c0)
        n2g = sb("n2g", [P, D], F32, c0)
        s_rk, s_x2 = sem("s_rk"), sem("s_x2")
        s_ewfree, s_sbfree = sem("s_ewfree"), sem("s_sbfree")
        s_ew = [sem(f"s_ew{k}") for k in range(2)]
        s_sb0 = [sem(f"s_sb{k}") for k in range(2)]
        s_h, s_g, s_hid, s_hfree = sem("s_h"), sem("s_g"), sem("s_hid"), sem("s_hfree")
        s_oc, s_ott, s_y = sem("s_oc"), sem("s_ott"), sem("s_y")
        M0 = F0 // P
        IT = NC * M0

        def g_rank(g, chain):
            for e in range(8):
                chain.link(g.memset(rank8[:, e:e + 1], float(8 - e)))
            chain.link(g.memset(below[:, :], 1.0))
            g.affine_select(out=below[:, :], in_=below[:, :], compare_op=ALU.is_ge, fill=0.0, base=-1,
                            pattern=[[1, P]], channel_multiplier=-1).then_inc(s_rk, 1)

        def act_route0(a, r):
            a.wait_ge(r["s_l"], r["nth"])
            a.activation(r["p"][:, :, :], r["L"][:, :, :], ACT.Sigmoid).then_inc(r["s_p"], 1)

        def v_route0(v, chain, r):
            v_logits(v, chain, r)
            v.sem_inc(r["s_l"], 1)
            v.wait_ge(s_rk, 1)
            v_top2(v, chain, r)
            one, two, t, u, m = r["one"], r["two"], r["t"], r["u"], r["m"]
            chain.link(v.tensor_tensor(one[:, :, :], one[:, :, :], two[:, :, :], ALU.add))
            a, b = one, t
            for sh in (1, 2, 4, 8):
                v.tensor_copy(b[:, 0:sh, :], a[:, 0:sh, :])
                chain.link(v.tensor_tensor(b[:, sh:NT, :], a[:, sh:NT, :], a[:, 0:NT - sh, :], ALU.add))
                a, b = b, (u if b is t else t)
            chain.link(v.tensor_copy(two[:, 0, :], a[:, NT - 1, :]))
            v.sem_inc(r["s_cnt"], 1)
            chain.link(v.tensor_tensor(a[:, :, :], a[:, :, :], one[:, :, :], ALU.subtract))
            v.wait_ge(r["s_cntd"], 1)
            chain.link(v.tensor_tensor(a[:, :, :], a[:, :, :], PS[:, 6, 0:8].unsqueeze(1).to_broadcast([P, NT, 8]), ALU.add))
            chain.link(v.tensor_scalar(a[:, :, :], a[:, :, :], float(CAP), None, ALU.is_lt))
            v.wait_ge(r["s_p"], r["nth"])
            chain.link(v.tensor_tensor(b[:, :, :], one[:, :, :], r["p"][:, :, :], ALU.mult))
            chain.link(v.tensor_reduce(m[:, :], b[:, :, :], AX.X, ALU.add))
            chain.link(v.tensor_scalar(m[:, :], m[:, :], 1e-6, None, ALU.add))
            chain.link(v.reciprocal(m[:, :], m[:, :]))
            chain.link(v.tensor_tensor(b[:, :, :], b[:, :, :], a[:, :, :], ALU.mult))
            v.tensor_tensor(r["wt"][:, :, :], b[:, :, :], bc(m[:, :]), ALU.mult).then_inc(r["s_w"], 1)
            v_weights(v, chain, r)

        def pe_route0(pe, r):
            pe.wait_ge(r["s_cnt"], 1)
            pe.matmul(PS[:, 6, 0:8], below[:, :], r["two"][:, 0, :], start=True, stop=True).then_inc(r["s_cntd"], 1)
            pe_weights(pe, r)

        def sp_expert0(sp, e, k):
            sp.dma_start(W1[:, k, :], A["L0_ffn_w1"].rearrange("e d f -> d e f")[:, e, :] if isinstance(e, int)
                         else A["L0_ffn_w1"].rearrange("e d f -> d e f")[:, bass.ds(e, 1), :].rearrange("d e f -> d (e f)")).then_inc(s_ew[k], 16)
            w2 = A["L0_ffn_w2"].rearrange("e (m f) d -> f e m d", f=P)
            sp.dma_start(W2[:, k, :, :], w2[:, e, :, :] if isinstance(e, int)
                         else w2[:, bass.ds(e, 1), :, :].rearrange("f e m d -> f (e m) d")).then_inc(s_ew[k], 16)

        def sp_row(sp, r, e, k):
            src = r["scr"].rearrange("s e p -> e s p")
            src = src[e] if isinstance(e, int) else src[bass.ds(e, 1), :, :].rearrange("e s p -> (e s) p")
            sp.dma_start(SB[:, k, :, :], src.partition_broadcast(P)).then_inc(s_sb0[k], 16)

        def sp_moe0(sp, r):
            sp.dma_start(r["gate"][:, :], A["L0_ffn_gate_w"]).then_inc(r["s_in"], 16)
            for k in range(2):
                sp_expert0(sp, k, k)
            sp_weights(sp, r)
            for k in range(2):
                sp_row(sp, r, k, k)
            with sp.Fori(0, E0 // 2 - 1) as i:
                for k in range(2):
                    sp.wait_ge(s_ewfree, k + 2)
                    sp_expert0(sp, i * 2 + (k + 2), k)
                    sp.wait_ge(s_sbfree, k + 1)
                    sp_row(sp, r, i * 2 + (k + 2), k)
                sp.sem_inc(s_ewfree, -2)
                sp.sem_inc(s_sbfree, -2)

        def pe_moe0(pe):
            pe.wait_ge(R0["s_pd"], 1)
            for c in range(NC):
                pe.matmul(PS[:, c, :], ident[:, :], HT[:, cs(c)], start=True, stop=False, skip_group_check=True)
            pe.sem_inc(s_hfree, 4)
            with pe.Fori(0, E0 // 2):
                for i in range(2 * IT + 3):
                    if i < 2 * IT:
                        k, c, m = i // IT, i % IT // M0, i % M0
                        if i % IT == 0:
                            pe.wait_ge(s_ew[k], 32)
                        if i >= 4:
                            pe.wait_ge(s_hid, i - 3)
                        pe.matmul(PS[:, 4 + i % 4, :], W1[:, k, P * m:P * m + P], HT[:, cs(c)], start=True, stop=True).then_inc(s_h, 1)
                    if i >= 3:
                        o = i - 3
                        k, c, m = o // IT, o % IT // M0, o % M0
                        pe.wait_ge(s_hid, o + 1)
                        if o % IT == IT - 1:
                            pe.sem_inc(s_sbfree, 1)
                        pe.matmul(PS[:, c, :], W2[:, k, m, :], HID[:, o % 4, :], start=False, stop=False, skip_group_check=True).then_inc(s_hfree, 1)
                for s in s_ew:
                    pe.sem_inc(s, -32)
                pe.sem_inc(s_hid, -2 * IT)

        def act_moe0(a):
            with a.Fori(0, E0 // 2):
                for i in range(2 * IT):
                    a.wait_ge(s_h, i + 1)
                    a.wait_ge(s_hfree, i + 1)
                    if i in (3, IT + 3):
                        a.sem_inc(s_ewfree, 1)
                    a.activation(HID[:, i % 4, :], PS[:, 4 + i % 4, :], ACT.Gelu).then_inc(s_g, 1)
                a.sem_inc(s_h, -2 * IT)
                a.sem_inc(s_hfree, -2 * IT)

        def v_moe0(v):
            with v.Fori(0, E0 // 2):
                for i in range(2 * IT):
                    k, c = i // IT, i % IT // M0
                    if i % IT == 0:
                        v.wait_ge(s_sb0[k], 16)
                    v.wait_ge(s_g, i + 1)
                    v.tensor_tensor(HID[:, i % 4, :], HID[:, i % 4, :], SB[:, k, ts_(c), :].rearrange("p t n -> p (t n)"),
                                    ALU.mult).then_inc(s_hid, 1)
                for s in s_sb0:
                    v.sem_inc(s, -16)
                v.sem_inc(s_g, -2 * IT)

        def pe_back(pe, n, OT):
            for c in range(NC):
                pe.wait_ge(s_oc, NC * n + c + 1)
                if n or c:
                    pe.wait_ge(s_y, NC * n + c)
                for j, t in enumerate(tiles(c)):
                    last = pe.transpose(PS[:, 7, P * j:P * j + P], OT[:, P * t:P * t + P], ident[:, :])
                last.then_inc(s_ott, 1)

        def act_back(a, n, OT, hfree, scale):
            a.wait_ge(hfree, 4)
            for c in range(NC):
                a.activation(OT[:, cs(c)], PS[:, c, :], ACT.Identity, scale=scale).then_inc(s_oc, 1)
        c0.close()

        d0 = ExitStack()
        KF = FB // P
        WA = sb("WA", [P, 2, 4, D], F32, d0)
        WF1 = sb("WF1", [P, 2, FB], F32, d0)
        WF2 = sb("WF2", [P, 2, KF, D], F32, d0)
        RW = sb("RW", [P, 2, 6, D], F32, d0)
        CL = sb("CL", [P, 2, 7 + KF], F32, d0)
        EX = sb("EX", [P, 2, 2, CH], F32, d0)
        TQ = sb("TQ", [P, 2, CH], F32, d0)
        Q1 = sb("Q1", [P, T], F32, d0)
        K1 = sb("K1", [P, CH], F32, d0)
        acc = sb("acc", [P, 2, NC], F32, d0)
        KS = sb("KS", [P, 2], F32, d0)
        Z1 = sb("Z1", [P, 2, 2, TPC, D], F32, d0)
        HF = sb("HF", [P, 2, KF, CH], F32, d0)
        s_lw = [sem(f"s_lw{k}") for k in range(2)]
        s_lwfree, s_lwfree_a = sem("s_lwfree"), sem("s_lwfree_a")
        s_q, s_k, s_v = sem("s_q"), sem("s_k"), sem("s_v")
        s_eq, s_qkvfree = sem("s_eq"), sem("s_qkvfree")
        s_exfree, s_qd, s_ks = sem("s_exfree"), sem("s_qd"), sem("s_ks")
        s_rz, s_vv = sem("s_rz"), sem("s_vv")
        s_wo, s_zfree = sem("s_wo"), sem("s_zfree")
        s_x3 = sem("s_x3")
        s_f1, s_hffree = sem("s_f1"), sem("s_hffree")

        def sp_block(sp, b, k):
            def of(name):
                ap = A["L1_attn_" + name]
                ap = ap[b] if isinstance(b, int) else ap[bass.ds(b, 1)]
                if not isinstance(b, int):
                    ap = ap.rearrange("b i j -> (b i) j") if len(ap.shape) == 3 else ap.rearrange("b i -> (b i)")
                return ap
            for j, w in enumerate(("Wq", "Wk", "Wv", "Wo")):
                sp.dma_start(WA[:, k, j, :], of(w)).then_inc(s_lw[k], 16)
            sp.dma_start(WF1[:, k, :], of("Wf1")).then_inc(s_lw[k], 16)
            sp.dma_start(WF2[:, k, :, :], of("Wf2").rearrange("(m f) d -> f m d", f=P)).then_inc(s_lw[k], 16)
            for j, w in enumerate(("bo", "bf2", "ln1_s", "ln1_b", "ln2_s", "ln2_b")):
                sp.dma_start(RW[:, k, j, :], of(w).partition_broadcast(P)).then_inc(s_lw[k], 16)
            for j, w in enumerate(("bq", "bk", "bv", "ln1_s", "ln1_b", "ln2_s", "ln2_b")):
                sp.dma_start(CL[:, k, j:j + 1], of(w).rearrange("(p a) -> p a", a=1)).then_inc(s_lw[k], 16)
            for m in range(KF):
                sp.dma_start(CL[:, k, 7 + m:8 + m], of("bf1")[P * m:P * m + P].rearrange("(p a) -> p a", a=1)).then_inc(s_lw[k], 16)

        LW = (4 + 2 + 6 + 7 + KF) * 16

        def sp_blocks(sp):
            for k in range(2):
                sp_block(sp, k, k)
            with sp.Fori(0, NB // 2 - 1) as i:
                for k in range(2):
                    sp.wait_ge(s_lwfree, k + 1)
                    sp.wait_ge(s_lwfree_a, k + 1)
                    sp_block(sp, i * 2 + (k + 2), k)
                sp.sem_inc(s_lwfree, -2)
                sp.sem_inc(s_lwfree_a, -2)

        def pe_qkv(pe, k):
            for c in range(NC):
                n = NC * k + c
                pe.wait_ge(S2["feat"], upto(k, c))
                for j, s in enumerate((s_q, s_k, s_v)):
                    if j == 0:
                        pe.wait_ge(s_qkvfree, n + 1)
                    pe.matmul(PS[:, j, :], WA[:, k, j, :], HT[:, cs(c)], start=True, stop=True).then_inc(s, 1)

        def act_qkv(a, k):
            for c in range(NC):
                n = NC * k + c
                a.wait_ge(s_exfree, n + 1)
                for j, s in enumerate((s_q, s_k)):
                    a.wait_ge(s, n + 1)
                    a.activation(EX[:, c % 2, j, :], PS[:, j, :], ACT.Exp, bias=CL[:, k, j:j + 1]).then_inc(s_eq, 1)

        def v_qkv(v, chain, k):
            for c in range(NC):
                n = NC * k + c
                for j in range(2):
                    v.wait_ge(s_eq, 2 * n + j + 1)
                    v.tensor_scalar(EX[:, c % 2, j, :], EX[:, c % 2, j, :], 1.0, -1.0, ALU.min, ALU.add)
                    chain.link(v.tensor_scalar(TQ[:, j, :], PS[:, j, :], CL[:, k, j:j + 1], 0.0, ALU.add, ALU.max))
                    if j == 0:
                        v.scalar_tensor_tensor(out=Q1[:, cs(c)], in0=EX[:, c % 2, 0, :], scalar=1.0, in1=TQ[:, 0, :],
                                               op0=ALU.add, op1=ALU.add)
                    else:
                        chain.link(v.scalar_tensor_tensor(out=K1[:, :], in0=EX[:, c % 2, 1, :], scalar=1.0, in1=TQ[:, 1, :],
                                                          op0=ALU.add, op1=ALU.add, accum_out=acc[:, 1, c:c + 1]))
                v.sem_inc(s_exfree, 1)
                v.wait_ge(s_v, n + 1)
                chain.link(v.scalar_tensor_tensor(out=K1[:, :], in0=PS[:, 2, :], scalar=CL[:, k, 2:3], in1=K1[:, :],
                                                  op0=ALU.add, op1=ALU.mult, accum_out=acc[:, 0, c:c + 1]))
                v.sem_inc(s_qkvfree, 1)
            chain.link(v.tensor_reduce(KS[:, :], acc[:, :, :], AX.X, ALU.add))
            v.sem_inc(s_ks, 1)

        def act_rz(a, chain, k):
            a.wait_ge(s_ks, k + 1)
            for c in range(NC):
                n = NC * k + c
                a.wait_ge(s_qd, n + 1)
                z = ZR[:, c % 2, :]
                chain.link(a.activation(z, Q1[:, cs(c)], ACT.Ln, scale=KS[:, 1:2], bias=eps1[:, 0:1]))
                a.activation(z, z, ACT.Exp, scale=-1.0).then_inc(s_rz, 1)

        ZR = sb("ZR", [P, 2, CH], F32, d0)

        def v_vv(v, chain, k, c):
            n = NC * k + c
            v.wait_ge(s_rz, n + 1)
            chain.link(v.scalar_tensor_tensor(out=Q1[:, cs(c)], in0=Q1[:, cs(c)], scalar=KS[:, 0:1], in1=ZR[:, c % 2, :],
                                              op0=ALU.mult, op1=ALU.mult))
            v.sem_inc(s_qd, 1)
            v.sem_inc(s_vv, 1)

        def pe_wo(pe, k, c):
            n = NC * k + c
            pe.wait_ge(s_vv, n + 1)
            pe.wait_ge(s_zfree, n + 1)
            for j, t in enumerate(tiles(c)):
                last = pe.matmul(PS[:, 3, P * j:P * j + P], Q1[:, P * t:P * t + P], WA[:, k, 3, :], start=True, stop=True)
            last.then_inc(s_wo, 1)

        def v_side(v, chain, k, c, side):
            n = NC * k + c
            bank, done, free = ((3, s_wo, s_zfree), (6, s_f2, s_f2free))[side]
            v.wait_ge(done, n + 1)
            if side:
                v.sem_inc(s_hffree, 1)
            z = Z1[:, side, c % 2, :, :]
            chain.link(v.tensor_tensor(z, PS[:, bank, :].rearrange("p (t d) -> p t d", t=TPC),
                                       RW[:, k, side, :].unsqueeze(1).to_broadcast([P, TPC, D]), ALU.add))
            v.sem_inc(free, 1)
            v.sem_inc(s_z[side], 1)

        def act_side(a, k, c, side):
            n = NC * k + c
            a.wait_ge(s_z[side], n + 1)
            a.activation(Z1[:, side, c % 2, :, :], Z1[:, side, c % 2, :, :], ACT.Gelu_apprx_tanh).then_inc(s_ge[side], 1)

        def v_resid(v, chain, k, c, side):
            n = NC * k + c
            v.wait_ge(s_ge[side], n + 1)
            v.wait_ge((S1 if side else S2)["tok"], upto(k, c))
            chain.link(v.tensor_tensor(Y[:, ts_(c), :], Z1[:, side, c % 2, :, :], H[:, ts_(c), :], ALU.add))
            norm_stats(v, chain, S2 if side else S1, Y, c, 1e-6, False)

        s_z = [sem(f"s_z{i}") for i in range(2)]
        s_ge = [sem(f"s_ge{i}") for i in range(2)]
        s_f2, s_f2free = sem("s_f2"), sem("s_f2free")

        def pe_f1(pe, k, c):
            pe.wait_ge(S1["feat"], upto(k, c))
            for m in range(KF):
                i = KF * (NC * k + c) + m
                pe.wait_ge(s_f1free, i + 1)
                pe.matmul(PS[:, 4 + m % 2, :], WF1[:, k, P * m:P * m + P], HT[:, cs(c)], start=True, stop=True).then_inc(s_f1, 1)

        s_f1free = sem("s_f1free")

        def act_f1(a, k, c):
            n = NC * k + c
            a.wait_ge(s_hffree, n + 1)
            for m in range(KF):
                a.wait_ge(s_f1, KF * n + m + 1)
                a.activation(HF[:, c % 2, m, :], PS[:, 4 + m % 2, :], ACT.Gelu_apprx_tanh,
                             bias=CL[:, k, 7 + m:8 + m]).then_inc(s_f1free, 1)

        def pe_f2(pe, k, c):
            n = NC * k + c
            pe.wait_ge(s_f1free, KF * (n + 1) + 2)
            pe.wait_ge(s_f2free, n + 1)
            for j in range(TPC):
                for m in range(KF):
                    last = pe.matmul(PS[:, 6, P * j:P * j + P], HF[:, c % 2, m, P * j:P * j + P], WF2[:, k, m, :],
                                     start=(m == 0), stop=(m == KF - 1))
            last.then_inc(s_f2, 1)

        SLOTS = NC + 3

        def pe_blocks(pe):
            pe.sem_inc(s_qkvfree, 1)
            pe.sem_inc(s_zfree, 1)
            pe.sem_inc(s_f1free, 2)
            pe.sem_inc(s_f2free, 1)
            with pe.Fori(0, NB // 2):
                for k in range(2):
                    pe.wait_ge(s_lw[k], LW)
                    pe_qkv(pe, k)
                    for t in range(SLOTS):
                        c = t - 3
                        if c >= 0:
                            norm_turn(pe, S2, k, c, (S2["feat"], NC + NC * k + c))
                        c = t - 2
                        if 0 <= c < NC:
                            pe_f2(pe, k, c)
                        c = t - 1
                        if 0 <= c < NC:
                            norm_turn(pe, S1, k, c, (S2["feat"], NC + NC * k + c - 1) if c >= 2 else None)
                            pe_f1(pe, k, c)
                        if t < NC:
                            pe_wo(pe, k, t)
                for s in (S1["normed"], S2["normed"], S1["feat"], S2["feat"], s_qkvfree, s_vv, s_zfree, s_f2free):
                    pe.sem_inc(s, -2 * NC)
                pe.sem_inc(s_f1free, -2 * NC * KF)
                for s in s_lw:
                    pe.sem_inc(s, -LW)

        def act_blocks(a, chain):
            a.sem_inc(s_exfree, 2)
            a.sem_inc(s_qd, 2)
            a.sem_inc(s_hffree, 2)
            with a.Fori(0, NB // 2):
                n = chain.n
                for k in range(2):
                    act_qkv(a, k)
                    act_rz(a, chain, k)
                    for t in range(SLOTS):
                        c = t - 3
                        if c >= 0:
                            norm_apply(a, S2, Y, k, c)
                            norm_feat(a, S2, k, c, CL[:, k, 5:6], CL[:, k, 6:7])
                        c = t - 2
                        if 0 <= c < NC:
                            act_side(a, k, c, 1)
                        c = t - 1
                        if 0 <= c < NC:
                            norm_apply(a, S1, Y, k, c)
                            norm_feat(a, S1, k, c, CL[:, k, 3:4], CL[:, k, 4:5])
                            act_f1(a, k, c)
                        if t < NC:
                            act_side(a, k, t, 0)
                    a.drain()
                    a.sem_inc(s_lwfree_a, 1)
                chain.take_back(n)
                for s in (S1["rstd"], S2["rstd"], S1["turned"], S2["turned"], s_q, s_k, s_exfree, s_qd, s_hffree, *s_z):
                    a.sem_inc(s, -2 * NC)
                a.sem_inc(s_ks, -2)
                a.sem_inc(s_f1, -2 * NC * KF)

        def v_blocks(v, chain):
            with v.Fori(0, NB // 2):
                n = chain.n
                for k in range(2):
                    v_qkv(v, chain, k)
                    for c in range(NC):
                        v_vv(v, chain, k, c)
                    for t in range(SLOTS - 1):
                        if 0 <= t - 2:
                            v_side(v, chain, k, t - 2, 1)
                        if t < NC:
                            v_side(v, chain, k, t, 0)
                            v_resid(v, chain, k, t, 0)
                        if 0 <= t - 2:
                            v_resid(v, chain, k, t - 2, 1)
                chain.take_back(n)
                for s in (S1["tok"], S2["tok"], s_v, s_rz, s_wo, s_f2, *s_ge):
                    v.sem_inc(s, -2 * NC)
                v.sem_inc(s_eq, -4 * NC)

        def g_blocks(g, chain):
            with g.Fori(0, NB // 2):
                n = chain.n
                for k in range(2):
                    for t in range(SLOTS):
                        if t - 3 >= 0:
                            norm_tok(g, chain, S2, k, t - 3, RW[:, k, 4, :], RW[:, k, 5, :])
                        if 0 <= t - 1 < NC:
                            norm_tok(g, chain, S1, k, t - 1, RW[:, k, 2, :], RW[:, k, 3, :])
                        if t < NC:
                            norm_rstd(g, chain, S1, k, t, False)
                        if 0 <= t - 2 < NC:
                            norm_rstd(g, chain, S2, k, t - 2, False)
                    g.drain()
                    g.sem_inc(s_lwfree, 1)
                chain.take_back(n)
                for s in (S1["stat"], S2["stat"], S1["normg"], S2["normg"]):
                    g.sem_inc(s, -2 * NC)
        d0.close()

        e0 = ExitStack()
        R1 = router("1", e0, E1, 2)
        HTILES = [(m, min(P, F1 - m)) for m in range(0, F1, P)]
        M1 = len(HTILES)
        IT1 = NC * M1
        G1 = sb("G1", [P, 2, F1], F32, e0)
        G3 = sb("G3", [P, 2, F1], F32, e0)
        G2 = sb("G2", [P, 2, M1, D], F32, e0)
        SB1 = sb("SB1", [P, 2, NT, P], F32, e0)
        XS = sb("XS", [P, 2, CH], F32, e0)
        HG = sb("HG", [P, 4, CH], F32, e0)
        OT1 = sb("OT1", [P, T], F32, e0)
        zero = sb("zero", [P, CH], F32, e0)
        s_zero = sem("s_zero")
        s_gwfree, s_sb1free = sem("s_gwfree"), sem("s_sb1free")
        s_xs, s_xsfree = sem("s_xs"), sem("s_xsfree")
        s_z3 = sem("s_z3")
        EW1 = 16 * 4

        def v_route1(v, chain, r):
            v_logits(v, chain, r)
            chain.link(v.tensor_reduce(r["m"][:, :], r["L"][:, :, :], AX.X, ALU.max))
            chain.link(v.tensor_tensor(r["wt"][:, :, :], r["L"][:, :, :], bc(r["m"][:, :]), ALU.subtract))
            v.sem_inc(r["s_l"], 1)
            v_top2(v, chain, r)
            chain.link(v.tensor_tensor(r["one"][:, :, :], r["one"][:, :, :], r["two"][:, :, :], ALU.add))
            v.wait_ge(r["s_p"], r["nth"])
            chain.link(v.tensor_reduce(r["m"][:, :], r["p"][:, :, :], AX.X, ALU.add))
            chain.link(v.reciprocal(r["m"][:, :], r["m"][:, :]))
            chain.link(v.tensor_tensor(r["one"][:, :, :], r["one"][:, :, :], r["p"][:, :, :], ALU.mult))
            v.tensor_tensor(r["wt"][:, :, :], r["one"][:, :, :], bc(r["m"][:, :]), ALU.mult).then_inc(r["s_w"], 1)
            v_weights(v, chain, r)

        def act_route1(a, r):
            a.wait_ge(r["s_l"], r["nth"])
            a.activation(r["p"][:, :, :], r["wt"][:, :, :], ACT.Exp).then_inc(r["s_p"], 1)

        def sp_expert1(sp, e, k):
            def of(name):
                return A["L1_ffn_" + name][bass.ds(e, 1)].rearrange("e i j -> (e i) j")
            w2 = of("w2")
            full = F1 // P * P
            sp.dma_start(G1[:, k, :], of("w1")).then_inc(s_ew[k], 16)
            sp.dma_start(G3[:, k, :], of("w3")).then_inc(s_ew[k], 16)
            sp.dma_start(G2[:, k, 0:full // P, :], w2[0:full].rearrange("(m f) d -> f m d", f=P)).then_inc(s_ew[k], 16)
            sp.dma_start(G2[0:F1 - full, k, M1 - 1, :], w2[full:F1]).then_inc(s_ew[k], 16)

        def sp_row1(sp, e, k):
            src = R1["scr"].rearrange("s e p -> e s p")[bass.ds(e, 1), :, :].rearrange("e s p -> (e s) p")
            sp.dma_start(SB1[:, k, :, :], src.partition_broadcast(P)).then_inc(s_sb0[k], 16)

        def sp_moe1(sp):
            for e in range(E1):
                sp.dma_start(R1["gate"][:, e:e + 1], A["L1_ffn_gate_w"][e].rearrange("(p a) -> p a", a=1)).then_inc(R1["s_in"], 16)
            for k in range(2):
                sp_expert1(sp, k, k)
            sp_weights(sp, R1)
            for k in range(2):
                sp_row1(sp, k, k)
            with sp.Fori(0, E1 // 2 - 1) as i:
                for k in range(2):
                    sp.wait_ge(s_gwfree, k + 2)
                    sp_expert1(sp, i * 2 + (k + 2), k)
                    sp.wait_ge(s_sb1free, k + 1)
                    sp_row1(sp, i * 2 + (k + 2), k)
                sp.sem_inc(s_gwfree, -2)
                sp.sem_inc(s_sb1free, -2)

        def g_moe1(g, chain):
            with g.Fori(0, E1 // 2):
                n = chain.n
                for k in range(2):
                    g.wait_ge(s_sb0[k], 16)
                    for c in range(NC):
                        i = NC * k + c
                        g.wait_ge(s_xsfree, i + 1)
                        chain.link(g.tensor_tensor(XS[:, c % 2, :], HT[:, cs(c)],
                                                   SB1[:, k, ts_(c), :].rearrange("p t n -> p (t n)"), ALU.mult))
                        g.sem_inc(s_xs, 1)
                    g.sem_inc(s_sb1free, 1)
                chain.take_back(n)
                for s in s_sb0:
                    g.sem_inc(s, -16)
                g.sem_inc(s_xsfree, -2 * NC)

        def pe_moe1(pe):
            pe.wait_ge(R1["s_pd"], 2)
            pe.wait_ge(s_zero, 1)
            for c in range(NC):
                pe.matmul(PS[:, c, :], ident[:, :], zero[:, :], start=True, stop=False, skip_group_check=True)
            pe.sem_inc(s_xsfree, 2)
            with pe.Fori(0, E1 // 2):
                for i in range(2 * IT1 + 2):
                    if i < 2 * IT1:
                        k, c, (f, w) = i // IT1, i % IT1 // M1, HTILES[i % M1]
                        if i % IT1 == 0:
                            pe.wait_ge(s_ew[k], EW1)
                        if i % M1 == 0:
                            pe.wait_ge(s_xs, i // M1 + 1)
                        if i >= 2:
                            pe.wait_ge(s_hid, i - 1)
                        b = 4 + 2 * (i % 2)
                        pe.matmul(PS[0:w, b, :], G1[:, k, f:f + w], XS[:, c % 2, :], start=True, stop=True).then_inc(s_h, 1)
                        last = pe.matmul(PS[0:w, b + 1, :], G3[:, k, f:f + w], XS[:, c % 2, :], start=True, stop=True)
                        last.then_inc(s_z3, 1)
                    if i >= 2:
                        o = i - 2
                        k, c, m = o // IT1, o % IT1 // M1, o % M1
                        w = HTILES[m][1]
                        pe.wait_ge(s_hid, o + 1)
                        if m == M1 - 1:
                            pe.sem_inc(s_xsfree, 1)
                        pe.matmul(PS[:, c, :], G2[0:w, k, m, :], HG[0:w, o % 4, :], start=False, stop=False,
                                  skip_group_check=True).then_inc(s_hfree, 1)
                for s in s_ew:
                    pe.sem_inc(s, -EW1)
                pe.sem_inc(s_xs, -2 * NC)
                pe.sem_inc(s_hid, -2 * IT1)

        def act_moe1(a):
            with a.Fori(0, E1 // 2):
                for i in range(2 * IT1):
                    w = HTILES[i % M1][1]
                    a.wait_ge(s_h, i + 1)
                    a.wait_ge(s_hfree, i + 1)
                    if i in (3, IT1 + 3):
                        a.sem_inc(s_gwfree, 1)
                    a.activation(HG[0:w, i % 4, :], PS[0:w, 4 + 2 * (i % 2), :], ACT.Silu).then_inc(s_g, 1)
                a.sem_inc(s_h, -2 * IT1)
                a.sem_inc(s_hfree, -2 * IT1)

        def v_moe1(v):
            with v.Fori(0, E1 // 2):
                for i in range(2 * IT1):
                    w = HTILES[i % M1][1]
                    v.wait_ge(s_g, i + 1)
                    v.wait_ge(s_z3, i + 1)
                    v.tensor_tensor(HG[0:w, i % 4, :], HG[0:w, i % 4, :], PS[0:w, 5 + 2 * (i % 2), :], ALU.mult).then_inc(s_hid, 1)
                v.sem_inc(s_g, -2 * IT1)
                v.sem_inc(s_z3, -2 * IT1)

        def v_last(v):
            for c in range(NC):
                v.wait_ge(s_ott, NC + c + 1)
                v.tensor_tensor(X[:, ts_(c), :], X[:, ts_(c), :], PS[:, 7, :].rearrange("p (t d) -> p t d", t=TPC),
                                ALU.add).then_inc(s_y, 1)
        e0.close()

        block = ctx.enter_context(nc.Block())

        @block.sync
        def _(sp):
            sp_pre(sp)
            sp.wait_ge(s_x1, NC)
            sp_gqa(sp)
            sp_stacks(sp)
            sp_gqa_rows(sp)
            sp.wait_ge(s_src, NC)
            sp_moe0(sp, R0)
            sp.wait_ge(s_x2, NC)
            sp_blocks(sp)
            sp.wait_ge(s_x3, NC)
            sp_moe1(sp)
            for c in range(NC):
                sp.wait_ge(s_y, NC + c + 1)
                sp.dma_start(out[0].rearrange("(p s) d -> p s d", p=P)[:, ts_(c), :], X[:, ts_(c), :]).then_inc(s_done, 16)
            sp.wait_ge(s_done, 16 * NC)

        @block.gpsimd
        def _(g):
            chain = Chain(g, ch_g)
            g_pre(g, chain)
            for c in range(NC):
                norm_rstd(g, chain, SM, 0, c, False)
            g_a0(g)
            g_out(g)
            g.wait_ge(s_x1, NC)
            g_gqa_pre(g, chain)
            for c in range(NC):
                norm_rstd(g, chain, SM, 1, c, False)
                norm_tok(g, chain, SM, 1, c, modr[:, 0, 4, :], modr[:, 0, 3, :])
            g_rank(g, chain)
            for c in range(NC):
                norm_rstd(g, chain, SM, 2, c, True)
            for c in range(NC):
                norm_rstd(g, chain, SM, 3, c, True)
            for c in range(NC):
                norm_rstd(g, chain, S4, 4, c, False)
                norm_tok(g, chain, S4, 4, c, modr[:, 1, 1, :], modr[:, 1, 0, :])
            g_blocks(g, chain)
            g.wait_ge(s_x3, NC)
            g.memset(zero[:, :], 0.0).then_inc(s_zero, 1)
            for c in range(NC):
                norm_rstd(g, chain, SM, 5, c, False)
            g.wait_ge(SM["feat"], 6 * NC)
            g_moe1(g, chain)

        @block.scalar
        def _(a):
            act_pre(a)
            a.wait_ge(s_mod, 1)
            for c in range(NC):
                norm_apply(a, SM, X, 0, c)
                norm_feat(a, SM, 0, c, modc[:, 0, 1:2], modc[:, 0, 0:1])
            act_a0(a)
            act_out(a)
            for c in range(NC):
                norm_apply(a, SM, X, 1, c)
                norm_feat(a, SM, 1, c, modc[:, 0, 4:5], modc[:, 0, 3:4])
            act_gqa_pre(a)
            act_gqa(a)
            for c in range(NC):
                norm_apply(a, SM, Y, 2, c)
                norm_feat(a, SM, 2, c, gw["n1c"][:, 0:1], zero1[:, 0:1])
            act_route0(a, R0)
            act_moe0(a)
            act_back(a, 0, OT, s_hfree, 1.0)
            for c in range(NC):
                norm_apply(a, SM, Y, 3, c)
            for c in range(NC):
                norm_apply(a, S4, X, 4, c)
                norm_feat(a, S4, 4, c, modc[:, 1, 1:2], modc[:, 1, 0:1])
            act_blocks(a, Chain(a, ch_a))
            for c in range(NC):
                norm_apply(a, SM, X, 5, c)
                norm_feat(a, SM, 5, c, modc[:, 1, 4:5], modc[:, 1, 3:4])
            act_route1(a, R1)
            act_moe1(a)
            act_back(a, 1, OT1, s_hfree, modc[:, 1, 5:6])

        @block.tensor
        def _(pe):
            pe_pre(pe)
            pe.wait_ge(s_const, 1)
            for c in range(NC):
                norm_turn(pe, SM, 0, c, (SM["feat"], NC * 0 + c) if c else None)
            pe_a0(pe)
            pe_chain(pe)
            pe_out(pe)
            for c in range(NC):
                norm_turn(pe, SM, 1, c, (SM["feat"], NC * 1 + c))
            pe_gqa_pre(pe)
            pe_gqa(pe)
            for c in range(NC):
                norm_turn(pe, SM, 2, c, (SM["feat"], NC * 2 + c))
            pe_router(pe, R0, 3 * NC, 16)
            pe_route0(pe, R0)
            pe_moe0(pe)
            pe_back(pe, 0, OT)
            pe.wait_ge(SM["normed"], 4 * NC)
            pe.sem_inc(SM["normg"], NC)
            pe.sem_inc(SM["turned"], NC)
            for c in range(NC):
                norm_turn(pe, S4, 4, c, (S2["feat"], c) if c else (s_y, NC))
            pe_blocks(pe)
            pe.sem_inc(SM["feat"], 2 * NC)
            for c in range(NC):
                norm_turn(pe, SM, 5, c, (SM["feat"], 5 * NC + c) if c else (S2["feat"], NC))
            pe_router(pe, R1, 6 * NC, 16 + 16 * E1)
            pe_weights(pe, R1)
            pe_moe1(pe)
            pe_back(pe, 1, OT1)

        @block.vector
        def _(v):
            chain = Chain(v, ch_v)
            v.wait_ge(s_x, 16)
            for c in range(NC):
                norm_stats(v, chain, SM, X, c, 1e-5, False)
            v_pre(v, chain)
            v_a0(v, chain)
            v_chain(v, chain)
            v_out(v, chain)
            v.wait_ge(s_x1, NC)
            for c in range(NC):
                norm_stats(v, chain, SM, X, c, 1e-5, False)
            v_gqa_pre(v, chain)
            v_gqa(v, chain)
            for c in range(NC):
                norm_stats(v, chain, SM, Y, c, 1e-6, True)
            v_route0(v, chain, R0)
            v_moe0(v)
            v.tensor_tensor(n2g[:, :], modr[:, 0, 5, :], gw["n2r"][:, :], ALU.mult)
            for c in range(NC):
                v.wait_ge(s_ott, c + 1)
                chain.link(v.tensor_copy(Y[:, ts_(c), :], PS[:, 7, :].rearrange("p (t d) -> p t d", t=TPC)))
                v.sem_inc(s_y, 1)
            for c in range(NC):
                norm_stats(v, chain, SM, Y, c, 1e-6, True)
            for c in range(NC):
                v.wait_ge(SM["normed"], 3 * NC + c + 1)
                chain.link(v.tensor_tensor(XN[:, ts_(c), :], XN[:, ts_(c), :], n2g[:, :].unsqueeze(1).to_broadcast([P, TPC, D]), ALU.mult))
                v.tensor_tensor(X[:, ts_(c), :], X[:, ts_(c), :], XN[:, ts_(c), :], ALU.add).then_inc(s_x2, 1)
            v.wait_ge(s_x2, NC)
            for c in range(NC):
                norm_stats(v, chain, S4, X, c, 1e-5, False)
            v_blocks(v, chain)
            for c in range(NC):
                v.wait_ge(S2["tok"], upto(0, c))
                chain.link(v.tensor_tensor(H[:, ts_(c), :], H[:, ts_(c), :], modr[:, 1, 2, :].unsqueeze(1).to_broadcast([P, TPC, D]), ALU.mult))
                v.tensor_tensor(X[:, ts_(c), :], X[:, ts_(c), :], H[:, ts_(c), :], ALU.add).then_inc(s_x3, 1)
            v.wait_ge(s_x3, NC)
            for c in range(NC):
                norm_stats(v, chain, SM, X, c, 1e-5, False)
            v_route1(v, chain, R1)
            v_moe1(v)
            v_last(v)



NAMES = [
    "L0_attn_x", "L0_attn_Wq", "L0_attn_Wk", "L0_attn_Wv", "L0_attn_Wo", "L0_attn_Wbet", "L0_attn_Wf", "L0_attn_norm_w",
    "L0_ffn_qw", "L0_ffn_qb", "L0_ffn_kw", "L0_ffn_kb", "L0_ffn_vw", "L0_ffn_vb", "L0_ffn_ow", "L0_ffn_ob",
    "L0_ffn_gate_w", "L0_ffn_w1", "L0_ffn_w2", "L0_ffn_norm1_w", "L0_ffn_norm2_w", "L0_c", "L0_wmod",
    "L1_attn_Wq", "L1_attn_bq", "L1_attn_Wk", "L1_attn_bk", "L1_attn_Wv", "L1_attn_bv", "L1_attn_Wo", "L1_attn_bo",
    "L1_attn_ln1_s", "L1_attn_ln1_b", "L1_attn_Wf1", "L1_attn_bf1", "L1_attn_Wf2", "L1_attn_bf2",
    "L1_attn_ln2_s", "L1_attn_ln2_b", "L1_ffn_gate_w", "L1_ffn_w1", "L1_ffn_w2", "L1_ffn_w3", "L1_c", "L1_wmod",
]


def kernel(**inputs):
    import numpy as np
    import concourse.bacc as bacc
    from concourse.bass_utils import run_bass_kernel_spmd

    nc = bacc.Bacc("TRN2", target_bir_lowering=False, num_devices=1)
    arrays, A = {}, {}
    for name in NAMES:
        a = np.ascontiguousarray(inputs[name])
        arrays[f"in_{name}"] = a
        A[name] = nc.dram_tensor(f"in_{name}", a.shape, mybir.dt.from_np(a.dtype), kind="ExternalInput").ap()
    out = nc.dram_tensor("out_x", (1, T, D), F32, kind="ExternalOutput").ap()
    build(nc, A, out)
    r = run_bass_kernel_spmd(nc, [arrays], core_ids=[0])
    return r.results[0]["out_x"]
```

```python
from contextlib import ExitStack

import concourse.bass as bass
from concourse import mybir

F32 = mybir.dt.float32
BF16 = mybir.dt.bfloat16
I32 = mybir.dt.int32
ALU = mybir.AluOpType
ACT = mybir.ActivationFunctionType
AX = mybir.AxisListType

P = 128
T = 2048
D = 128
NT = T // P
CH = 512
NC = T // CH
TPC = CH // P
RSQRT_SEED = float(0x5F3759DF - 0x400000)

H0, HD = 16, 8
NKV, REP = 4, 4
E0, F0 = 8, 256
CAP = int(1.25 * T * 2 / E0)
NB, FB = 8, 512
E1, F1 = 8, 352
STACK = 9 * HD


class Chain:

    def __init__(self, eng, sem):
        self.eng, self.sem, self.n = eng, sem, 0

    def link(self, ins):
        self.n += 1
        ins.then_inc(self.sem, 1)
        self.eng.wait_ge(self.sem, self.n)

    def take_back(self, n):
        self.eng.sem_inc(self.sem, n - self.n)
        self.n = n



def build(nc, A, out):
    ctx = ExitStack()
    with ctx:
        def sb(name, shape, dt=F32, stack=ctx):
            return stack.enter_context(nc.sbuf_tensor(name, shape, dt))

        def sem(name):
            return ctx.enter_context(nc.semaphore(name))

        PS = ctx.enter_context(nc.psum_tensor("PS", [P, 8, CH], F32))

        X = sb("X", [P, NT, D])
        Y = sb("Y", [P, NT, D])
        XN = sb("XN", [P, NT, D])
        H = sb("H", [P, NT, D])
        HT = sb("HT", [P, T])
        ident = sb("ident", [P, P])
        st = sb("st", [P, NT, 6])
        ag = sb("ag", [P, NT, 2])
        vh = sb("vh", [P, NT])
        rs = sb("rs", [P, NT])
        nt = sb("nt", [P, NT])
        ny = sb("ny", [P, NT])
        nm1 = sb("nm1", [P, NT])
        nb = sb("nb", [P, NT])
        modr = sb("modr", [P, 2, 6, D])
        modc = sb("modc", [P, 2, 6])
        zero1 = sb("zero1", [P, 1])
        eps1 = sb("eps1", [P, 1])

        ch_v, ch_g, ch_a = sem("ch_v"), sem("ch_g"), sem("ch_a")
        s_const = sem("s_const")
        s_done = sem("s_done")
        s_x = sem("s_x")
        s_mod_in = sem("s_mod_in")
        s_sc, s_scb = sem("s_sc"), sem("s_scb")
        s_modps, s_mod = sem("s_modps"), sem("s_mod")
        s_w0 = sem("s_w0")

        def norm_set(tag, **kw):
            s = {n: sem(f"s_{n}{tag}") for n in ("stat", "rstd", "normed", "normg", "turned", "feat", "tok") if n not in kw}
            s.update(kw)
            return s

        SM = norm_set("M")
        S1, S2 = norm_set("A"), norm_set("B")
        S4 = dict(SM, feat=S2["feat"], tok=S2["tok"])

        def upto(k, c):
            return NC * k + c + 1

        def tiles(c):
            return range(TPC * c, TPC * c + TPC)

        def ts_(c):
            return slice(TPC * c, TPC * c + TPC)

        def cs(c):
            return slice(CH * c, CH * c + CH)

        def norm_stats(v, chain, S_, src, c, eps, rms):
            for t in tiles(c):
                last = v.bn_stats(st[:, t, :], src[:, t, :])
            chain.link(last)
            for t in tiles(c):
                last = v.bn_aggr(ag[:, t, :], st[:, t, :])
            chain.link(last)
            if rms:
                chain.link(v.tensor_tensor(vh[:, ts_(c)], ag[:, ts_(c), 0], ag[:, ts_(c), 0], ALU.mult))
                chain.link(v.tensor_tensor(vh[:, ts_(c)], vh[:, ts_(c)], ag[:, ts_(c), 1], ALU.add))
                chain.link(v.tensor_scalar(vh[:, ts_(c)], vh[:, ts_(c)], eps, 0.5, ALU.add, ALU.mult))
            else:
                chain.link(v.tensor_scalar(vh[:, ts_(c)], ag[:, ts_(c), 1], eps, 0.5, ALU.add, ALU.mult))
            v.tensor_scalar(rs[:, ts_(c)].bitcast(I32), vh[:, ts_(c)].bitcast(I32), -0.5, RSQRT_SEED,
                            ALU.mult, ALU.add).then_inc(S_["stat"], 1)

        def norm_rstd(g, chain, S_, k, c, rms):
            g.wait_ge(S_["stat"], upto(k, c))
            a = ts_(c)
            g.tensor_scalar(nm1[:, a], ag[:, a, 0], 0.0 if rms else -1.0, None, ALU.mult)
            for last in (False, True):
                chain.link(g.tensor_tensor(nt[:, a], rs[:, a], rs[:, a], ALU.mult))
                chain.link(g.tensor_tensor(nt[:, a], nt[:, a], vh[:, a], ALU.mult))
                if last:
                    chain.link(g.tensor_scalar(ny[:, a], nt[:, a], 1.5, -2.5, ALU.mult, ALU.add))
                    chain.link(g.tensor_tensor(nt[:, a], ny[:, a], nt[:, a], ALU.mult))
                    chain.link(g.tensor_scalar(nt[:, a], nt[:, a], 1.875, None, ALU.add))
                else:
                    chain.link(g.tensor_scalar(nt[:, a], nt[:, a], -1.0, 1.5, ALU.mult, ALU.add))
                chain.link(g.tensor_tensor(rs[:, a], rs[:, a], nt[:, a], ALU.mult))
            g.tensor_tensor(nb[:, a], nm1[:, a], rs[:, a], ALU.mult).then_inc(S_["rstd"], 1)

        def norm_apply(a, S_, src, k, c):
            a.wait_ge(S_["rstd"], upto(k, c))
            for t in tiles(c):
                last = a.activation(XN[:, t, :], src[:, t, :], ACT.Identity, scale=rs[:, t:t + 1],
                                    bias=nb[:, t:t + 1])
            last.then_inc(S_["normed"], 1)

        def norm_turn(pe, S_, k, c, free=None):
            pe.wait_ge(S_["normed"], upto(k, c))
            pe.sem_inc(S_["normg"], 1)
            if free:
                pe.wait_ge(*free)
            for j, t in enumerate(tiles(c)):
                last = pe.transpose(PS[:, 7, P * j:P * j + P], XN[:, t, :], ident[:, :])
            last.then_inc(S_["turned"], 1)

        def norm_feat(a, S_, k, c, scale, bias):
            a.wait_ge(S_["turned"], upto(k, c))
            return a.activation(HT[:, cs(c)], PS[:, 7, :], ACT.Identity, scale=scale, bias=bias).then_inc(S_["feat"], 1)

        def norm_tok(v, chain, S_, k, c, scale, bias):
            v.wait_ge(S_["normg"], upto(k, c))
            a = ts_(c)
            m = v.tensor_tensor(H[:, a, :], XN[:, a, :], scale.unsqueeze(1).to_broadcast([P, TPC, D]), ALU.mult)
            if bias is not None:
                chain.link(m)
                m = v.tensor_tensor(H[:, a, :], H[:, a, :], bias.unsqueeze(1).to_broadcast([P, TPC, D]), ALU.add)
            m.then_inc(S_["tok"], 1)

        a0 = ExitStack()
        NQ = 2 * D + 2 * H0
        WC = sb("WC", [P, NQ + D], F32, a0)
        Wo0 = sb("Wo0", [P, D], F32, a0)
        nw0 = sb("nw0", [P, 1], F32, a0)
        scol = sb("scol", [P, 2], F32, a0)
        ccol = sb("ccol", [P, 2], F32, a0)
        scb = sb("scb", [P, 2, P], F32, a0)
        gt = sb("gt", [P, 2, 2, D + 1], F32, a0)
        SG = sb("SG", [P, NT, NQ], F32, a0)
        QK = sb("QK", [P, NT, 2 * D], F32, a0)
        V0 = sb("V0", [P, NT, D], F32, a0)
        KA = sb("KA", [P, NT, D], F32, a0)
        KN = sb("KN", [P, NT, D], F32, a0)
        kn2 = sb("kn2", [P, NT * H0], F32, a0)
        ba = sb("ba", [P, NT, H0], F32, a0)
        S = sb("S", [P, 2, H0, 2 * HD, HD], F32, a0)
        ASPR = sb("ASPR", [P, 2, H0, 2 * HD, HD], F32, a0)
        AS, PR = ASPR[:, 0, :, :, :], ASPR[:, 1, :, :, :]
        QS = sb("QS", [P, 2, H0, 2 * HD, HD], F32, a0)
        wm = QS[:, :, :, :, :].rearrange("p b h c i -> p (b h c i)")[:, 0:2 * 6 * D].rearrange("p (l n) -> p l n", l=2)
        W = sb("W", [P, H0, 2 * HD], F32, a0)
        O = sb("O", [P, NT, H0, 2 * HD], F32, a0)
        hmask = sb("hmask", [P, H0], F32, a0)
        MT = sb("MT", [P, HD, P], F32, a0)
        BD = ASPR[:, :, :, :, :].rearrange("q b h c i -> q (b h c i)").rearrange("q (b s h i) -> q b s h i", b=2, s=16, h=H0)
        NTt = sb("NTt", [P, P, HD], F32, a0)
        SH = sb("SH", [P, P + 1, HD], F32, a0)
        S0t = sb("S0t", [P, H0, HD, HD], F32, a0)

        s_amm, s_asig, s_av, s_aev = sem("s_amm"), sem("s_asig"), sem("s_av"), sem("s_aev")
        s_kn2, s_ksq = sem("s_kn2"), sem("s_ksq")
        s_state, s_as, s_qs, s_red = sem("s_state"), sem("s_as"), sem("s_qs"), sem("s_red")
        s_mt, s_mtc, s_bd, s_bdu = sem("s_mt"), sem("s_mtc"), sem("s_bd"), sem("s_bdu")
        s_nt, s_ntc, s_chain, s_sh = sem("s_nt"), sem("s_ntc"), sem("s_chain"), sem("s_sh")
        s_s0, s_s0c, s_o2, s_o2r = sem("s_s0"), sem("s_s0c"), sem("s_o2"), sem("s_o2r")
        s_on2, s_osq, s_on = sem("s_on2"), sem("s_osq"), sem("s_on")
        s_ot, s_otc, s_op, s_x1 = sem("s_ot"), sem("s_otc"), sem("s_op"), sem("s_x1")
        s_sfc = sem("s_sfc")

        HH = H0 // 2
        s_kw = sem("s_kw")

        def heads(x):
            return slice(HH * x, HH * x + HH)

        def hb(ap, x):
            return ap[:, HH * HD * x:HH * HD * (x + 1)].rearrange("p (h i) -> p h i", h=HH).unsqueeze(2).to_broadcast([P, HH, 2 * HD, HD])

        def sp_pre(sp):
            sp.dma_start(X[:, :, :], A["L0_attn_x"][0].rearrange("(p s) d -> p s d", p=P)).then_inc(s_x, 16)
            at = 0
            for n, w in (("Wq", D), ("Wk", D), ("Wbet", H0), ("Wf", H0), ("Wv", D)):
                sp.dma_start(WC[:, at:at + w], A["L0_attn_" + n]).then_inc(s_w0, 16)
                at += w
            sp.dma_start(Wo0[:, :], A["L0_attn_Wo"]).then_inc(s_w0, 16)
            sp.dma_start(nw0[:, :], A["L0_attn_norm_w"].rearrange("(p a) -> p a", a=1)).then_inc(s_w0, 16)

        def act_pre(a):
            for l in range(2):
                a.dma_start(ccol[:, l:l + 1], A[f"L{l}_c"].rearrange("a d -> d a")).then_inc(s_mod_in, 16)
                a.dma_start(wm[:, l, :], A[f"L{l}_wmod"]).then_inc(s_mod_in, 16)
            a.wait_ge(s_mod_in, 64)
            a.activation(scol[:, :], ccol[:, :], ACT.Silu).then_inc(s_sc, 1)

        def g_pre(g, chain):
            chain.link(g.memset(ident[:, :], 0.0))
            chain.link(g.memset(hmask[:, :], 1.0))
            g.memset(zero1[:, :], 0.0)
            chain.link(g.memset(eps1[:, :], 1e-6))
            chain.link(g.affine_select(out=ident[:, :], in_=ident[:, :], compare_op=ALU.not_equal, fill=1.0,
                                       base=0, pattern=[[-1, P]], channel_multiplier=1))
            chain.link(g.affine_select(out=hmask[:, :], in_=hmask[:, :], compare_op=ALU.is_ge, fill=0.0,
                                       base=0, pattern=[[-HD, H0]], channel_multiplier=1))
            g.affine_select(out=hmask[:, :], in_=hmask[:, :], compare_op=ALU.is_ge, fill=0.0,
                            base=HD - 1, pattern=[[HD, H0]], channel_multiplier=-1).then_inc(s_const, 1)

        def pe_pre(pe):
            pe.wait_ge(s_scb, 1)
            for l in range(2):
                for half in range(2):
                    pe.matmul(PS[:, 2 * l + half, 0:3 * D], scb[:, l, :], wm[:, l, half * 3 * D:(half + 1) * 3 * D],
                              start=True, stop=True)
                for j in range(6):
                    last = pe.matmul(PS[:, 4 + l, j:j + 1], wm[:, l, j * D:(j + 1) * D], scol[:, l:l + 1],
                                     start=True, stop=True)
            last.then_inc(s_modps, 1)

        def v_pre(v, chain):
            v.wait_ge(s_sc, 1)
            v.tensor_copy(scb[:, :, :], scol[:, :].unsqueeze(2).to_broadcast([P, 2, P])).then_inc(s_scb, 1)
            v.wait_ge(s_modps, 1)
            for l in range(2):
                v.tensor_copy(modr[:, l, 0:3, :], PS[:, 2 * l, 0:3 * D].rearrange("p (a d) -> p a d", a=3))
                v.tensor_copy(modr[:, l, 3:6, :], PS[:, 2 * l + 1, 0:3 * D].rearrange("p (a d) -> p a d", a=3))
                last = v.tensor_copy(modc[:, l, :], PS[:, 4 + l, 0:6])
            chain.link(last)
            for l in range(2):
                for j in (1, 4):
                    for m in (modr[:, l, j, :], modc[:, l, j:j + 1]):
                        last = v.tensor_scalar(m, m, 1.0, None, ALU.add)
            chain.link(last)
            for l in range(2):
                for n, j in enumerate((2, 5)):
                    for m, w in ((modr[:, l, j, :], slice(0, D)), (modc[:, l, j:j + 1], slice(D, D + 1))):
                        s, t = gt[:, 0, n, w], gt[:, 1, n, w]
                        v.tensor_scalar(s, m, 0.0, 2.0, ALU.is_ge, ALU.mult)
                        chain.link(v.tensor_scalar(t, m, -1.0, None, ALU.mult))
                        chain.link(v.tensor_tensor(t, t, m, ALU.max))
                        v.tensor_scalar(t, t, 0.25, None, ALU.max)
                        chain.link(v.tensor_scalar(s, s, -1.0, None, ALU.add))
                        chain.link(v.tensor_tensor(m, s, t, ALU.mult))
            v.wait_ge(s_w0, 7 * 16)
            chain.link(v.tensor_scalar(Wo0[:, :], Wo0[:, :], nw0[:, 0:1], None, ALU.mult))
            chain.link(v.tensor_tensor(Wo0[:, :], Wo0[:, :], modr[:, 0, 2, :], ALU.mult))
            v.sem_inc(s_mod, 1)

        def pe_a0(pe):
            pe.wait_ge(s_w0, 7 * 16)
            for s in range(NT):
                pe.wait_ge(SM["feat"], s // TPC + 1)
                if s >= 4:
                    pe.wait_ge(s_aev, s - 3)
                    pe.wait_ge(s_av, s - 3)
                pe.matmul(PS[:, s % 4, 0:NQ + D], HT[:, P * s:P * s + P], WC[:, :], start=True, stop=True).then_inc(s_amm, 1)

        def act_a0(a):
            for s in range(NT):
                a.wait_ge(s_amm, s + 1)
                a.activation(SG[:, s, :], PS[:, s % 4, 0:NQ], ACT.Sigmoid).then_inc(s_asig, 1)
                a.activation(V0[:, s, :], PS[:, s % 4, NQ:NQ + D], ACT.Copy).then_inc(s_av, 1)
            a.wait_ge(s_kn2, 1)
            a.activation(kn2[:, :], kn2[:, :], ACT.Sqrt).then_inc(s_ksq, 1)
            act_state(a)

        def v_a0(v, chain):
            for s in range(NT):
                v.wait_ge(s_av, s + 1)
                v.tensor_tensor(QK[:, s, :], PS[:, s % 4, 0:2 * D], SG[:, s, 0:2 * D], ALU.mult).then_inc(s_aev, 1)
            v.wait_ge(s_aev, NT)
            v.wait_ge(s_av, NT)
            kv = QK[:, :, D:2 * D]
            chain.link(v.tensor_tensor(KN[:, :, :], kv, kv, ALU.mult))
            chain.link(v.tensor_reduce(kn2[:, :], KN[:, :, :].rearrange("p s (h i) -> p (s h) i", i=HD), AX.X, ALU.add))
            v.tensor_scalar(kn2[:, :], kn2[:, :], 1e-12, None, ALU.add).then_inc(s_kn2, 1)
            beta = SG[:, :, 2 * D:2 * D + H0]
            alpha = SG[:, :, 2 * D + H0:NQ]
            chain.link(v.tensor_scalar(beta, beta, 2.0, None, ALU.mult))
            chain.link(v.tensor_scalar(ba[:, :, :], alpha, -1.0, None, ALU.mult))
            chain.link(v.tensor_tensor(ba[:, :, :], ba[:, :, :], beta, ALU.mult))
            v4 = V0[:, :, :].rearrange("p s (h c) -> p s h c", h=H0)
            chain.link(v.tensor_tensor(v4, v4, beta.unsqueeze(3).to_broadcast([P, NT, H0, HD]), ALU.mult))
            v.wait_ge(s_ksq, 1)
            chain.link(v.reciprocal(kn2[:, :], kn2[:, :]))
            chain.link(v.tensor_tensor(KN[:, :, :].rearrange("p s (h i) -> p s h i", h=H0),
                                       kv.rearrange("p s (h i) -> p s h i", h=H0),
                                       kn2[:, :].rearrange("p (s h) -> p s h", s=NT).unsqueeze(3).to_broadcast([P, NT, H0, HD]),
                                       ALU.mult))
            chain.link(v.tensor_tensor(KA[:, :, :].rearrange("p s (h i) -> p s h i", h=H0),
                                       KN[:, :, :].rearrange("p s (h i) -> p s h i", h=H0),
                                       ba[:, :, :].unsqueeze(3).to_broadcast([P, NT, H0, HD]), ALU.mult))
            chain.link(v.memset(S[:, 0, :, :, :], 0.0))
            chain.link(v.memset(S[:, 0, :, :, :].rearrange("p h c i -> p h (c i)")[:, :, HD * HD::HD + 1], 1.0))
            v.sem_inc(s_state, 2)

            for s in range(NT):
                for x in range(2):
                    h = heads(x)
                    v.wait_ge(s_state, 2 * s + x + 1)
                    chain.link(v.tensor_tensor(PR[:, h, :, :], hb(KA[:, s, :], x), S[:, s % 2, h, :, :], ALU.mult))
                    chain.link(v.tensor_reduce(W[:, h, :], PR[:, h, :, :], AX.X, ALU.add))
                    chain.link(v.tensor_tensor(W[:, h, 0:HD], W[:, h, 0:HD],
                                               V0[:, s, :].rearrange("p (h c) -> p h c", h=H0)[:, h, :], ALU.add))
                    v.tensor_tensor(PR[:, h, :, :], hb(KN[:, s, :], x),
                                    W[:, h, :].unsqueeze(3).to_broadcast([P, HH, 2 * HD, HD]), ALU.mult).then_inc(s_kw, 1)
                if s >= 2:
                    v_o(v, s - 2)
            v_o(v, NT - 2)
            v_o(v, NT - 1)
            v.wait_ge(s_red, NT)
            v.tensor_copy(SC[:, 0, :, :].rearrange("p c (h i) -> p c h i", h=H0), SF[:, :, 0:HD, :].rearrange("p h c i -> p c h i")).then_inc(s_sfc, 1)
            v.tensor_copy(SC[:, 1, :, :].rearrange("p i (h j) -> p i h j", h=H0), SF[:, :, HD:2 * HD, :].rearrange("p h j i -> p i h j")).then_inc(s_sfc, 1)

        def act_state(a):
            for s in range(NT):
                for x in range(2):
                    a.wait_ge(s_state, 2 * s + x + 1)
                    for h in range(HH * x, HH * x + HH):
                        at = 2 * D + H0 + h
                        last = a.activation(AS[:, h, :, :], S[:, s % 2, h, :, :], ACT.Copy, scale=SG[:, s, at:at + 1])
                    last.then_inc(s_as, 1)

        def v_o(v, s):
            v.wait_ge(s_qs, 2 * (s + 1))
            v.tensor_reduce(O[:, s, :, :], QS[:, s % 2, :, :, :], AX.X, ALU.add).then_inc(s_red, 1)

        def g_qs(g, s, x):
            g.wait_ge(s_state, 2 * (s + 1) + x + 1)
            if s >= 2:
                g.wait_ge(s_red, s - 1)
            g.tensor_tensor(QS[:, s % 2, heads(x), :, :], hb(QK[:, s, 0:D], x), S[:, (s + 1) % 2, heads(x), :, :],
                            ALU.mult).then_inc(s_qs, 1)

        def g_a0(g):
            for s in range(NT):
                for x in range(2):
                    h = heads(x)
                    g.wait_ge(s_as, 2 * s + x + 1)
                    g.wait_ge(s_kw, 2 * s + x + 1)
                    if s >= 2:
                        g.wait_ge(s_qs, 2 * (s - 2) + x + 1)
                    g.tensor_tensor(S[:, (s + 1) % 2, h, :, :], PR[:, h, :, :], AS[:, h, :, :], ALU.add).then_inc(s_state, 1)
                    if s >= 1:
                        g_qs(g, s - 1, x)
            for x in range(2):
                g_qs(g, NT - 1, x)
            g.wait_ge(s_mtc, 1)
            for k in range(P // 16):
                if k >= 2:
                    g.wait_ge(s_bdu, k - 1)
                g.tensor_tensor(BD[:, k % 2, :, :, :],
                                MT[:, :, 16 * k:16 * k + 16].rearrange("q i p -> q p i").unsqueeze(2).to_broadcast([P, 16, H0, HD]),
                                hmask[:, :].unsqueeze(1).unsqueeze(3).to_broadcast([P, 16, H0, HD]), ALU.mult).then_inc(s_bd, 1)

        SF = S[:, NT % 2, :, :, :]
        SC = QS[:, 0, :, :, :].rearrange("p h c i -> p (h c i)").rearrange("p (b a n) -> p b a n", b=2, a=HD)

        def pe_chain(pe):
            pe.wait_ge(s_sfc, 2)
            for c in range(HD):
                last = pe.transpose(PS[:, c // 4, P * (c % 4):P * (c % 4) + P], SC[:, 0, c, :], ident[:, :])
            last.then_inc(s_nt, 1)
            for i in range(HD):
                last = pe.transpose(PS[:, 2 + i // 4, P * (i % 4):P * (i % 4) + P], SC[:, 1, i, :], ident[:, :])
            last.then_inc(s_mt, 1)
            pe.wait_ge(s_ntc, 1)
            n_flat = NTt[:, :, :].rearrange("q p c -> q (p c)")
            for half in range(2):
                last = pe.matmul(PS[:, 4 + half, :], ident[:, :], n_flat[:, CH * half:CH * half + CH], start=True, stop=False,
                                 skip_group_check=True)
            last.then_inc(s_chain, 1)
            for p in range(1, P - 1):
                if p % 16 == 0 or p == 1:
                    pe.wait_ge(s_bd, p // 16 + 1)
                pe.wait_ge(s_sh, p)
                at = HD * p
                m = pe.matmul(PS[:, 4 + at // CH, at % CH:at % CH + HD],
                              BD[:, p // 16 % 2, p % 16, :, :].rearrange("q h i -> q (h i)"), SH[:, p, :],
                              start=False, stop=True, skip_group_check=True)
                m.then_inc(s_chain, 1)
                if p % 16 == 15:
                    pe.wait_ge(s_chain, p + 1)
                    pe.sem_inc(s_bdu, 1)
            pe.wait_ge(s_sh, P - 1)
            for c in range(HD):
                last = pe.transpose(PS[:, c // 4, P * (c % 4):P * (c % 4) + P], SH[:, 0:P, c], ident[:, :])
            last.then_inc(s_s0, 1)

        def v_chain(v, chain):
            v.wait_ge(s_nt, 1)
            v.tensor_copy(SH[:, 0, :], zero1[:, 0:1].to_broadcast([P, HD]))
            v.tensor_copy(NTt[:, :, :].rearrange("q p c -> q c p"),
                          PS[:, 0:2, :].rearrange("q b n -> q (b n)").rearrange("q (c p) -> q c p", c=HD)).then_inc(s_ntc, 1)
            v.wait_ge(s_mt, 1)
            v.tensor_copy(MT[:, :, :], PS[:, 2:4, :].rearrange("q b n -> q (b n)").rearrange("q (i p) -> q i p", i=HD)).then_inc(s_mtc, 1)
            for p in range(1, P):
                v.wait_ge(s_chain, p)
                at = HD * (p - 1)
                v.tensor_copy(SH[:, p, :], PS[:, 4 + at // CH, at % CH:at % CH + HD]).then_inc(s_sh, 1)
            v.wait_ge(s_s0, 1)
            v.tensor_copy(S0t[:, :, :, :].rearrange("p h c i -> p c h i"),
                          PS[:, 0:2, :].rearrange("p b n -> p (b n)").rearrange("p (c h i) -> p c h i", c=HD, h=H0)).then_inc(s_s0c, 1)

        def half_pr(s):
            b, c = ((0, 0), (1, 0), (0, HD))[s % 3]
            return QS[:, b, :, c:c + HD, :]

        def g_out(g):
            for s in range(NT):
                if s == 0:
                    g.wait_ge(s_s0c, 1)
                    g.wait_ge(s_red, NT)
                if s % 3 == 2:
                    continue
                if s >= 3:
                    g.wait_ge(s_o2r, s - 2)
                g.tensor_tensor(half_pr(s), O[:, s, :, HD:2 * HD].unsqueeze(2).to_broadcast([P, H0, HD, HD]),
                                S0t[:, :, :, :], ALU.mult).then_inc(s_o2, 1)

        def v_out(v, chain):
            OR = PR[:, :, :, :].rearrange("p h c i -> p (h c i)").rearrange("p (s d) -> p s d", s=NT)
            for s in range(NT):
                if s % 3 == 2:
                    v.wait_ge(s_o2r, s)
                    chain.link(v.tensor_tensor(half_pr(s), O[:, s, :, HD:2 * HD].unsqueeze(2).to_broadcast([P, H0, HD, HD]),
                                               S0t[:, :, :, :], ALU.mult))
                else:
                    v.wait_ge(s_o2, s + 1 - (s + 1) // 3)
                v.tensor_reduce(OR[:, s, :].rearrange("p (h c) -> p h c", h=H0), half_pr(s), AX.X, ALU.add).then_inc(s_o2r, 1)
            v.wait_ge(s_o2r, NT)
            O4 = OR.rearrange("p s (h c) -> p s h c", h=H0)
            chain.link(v.tensor_tensor(O4, O4, O[:, :, :, 0:HD], ALU.add))
            chain.link(v.tensor_tensor(KN[:, :, :], OR, OR, ALU.mult))
            chain.link(v.tensor_reduce(kn2[:, :], KN[:, :, :].rearrange("p s (h i) -> p (s h) i", i=HD), AX.X, ALU.add))
            v.tensor_scalar(kn2[:, :], kn2[:, :], 1.0 / HD, 1e-6, ALU.mult, ALU.add).then_inc(s_on2, 1)
            v.wait_ge(s_osq, 1)
            chain.link(v.reciprocal(kn2[:, :], kn2[:, :]))
            v.tensor_tensor(Y[:, :, :].rearrange("p s (h c) -> p s h c", h=H0), O4,
                            kn2[:, :].rearrange("p (s h) -> p s h", s=NT).unsqueeze(3).to_broadcast([P, NT, H0, HD]),
                            ALU.mult).then_inc(s_on, 1)
            for c in range(NC):
                v.wait_ge(s_ot, c + 1)
                v.tensor_copy(HT[:, cs(c)], PS[:, c % 2, :]).then_inc(s_otc, 1)
            for c in range(NC):
                v.wait_ge(s_op, c + 1)
                v.tensor_tensor(X[:, ts_(c), :], X[:, ts_(c), :], PS[:, 2 + c % 2, :].rearrange("p (t d) -> p t d", t=TPC),
                                ALU.add).then_inc(s_x1, 1)

        def act_out(a):
            a.wait_ge(s_on2, 1)
            a.activation(kn2[:, :], kn2[:, :], ACT.Sqrt).then_inc(s_osq, 1)

        def pe_out(pe):
            pe.wait_ge(s_on, 1)
            for c in range(NC):
                if c >= 2:
                    pe.wait_ge(s_otc, c - 1)
                for j, t in enumerate(tiles(c)):
                    last = pe.transpose(PS[:, c % 2, P * j:P * j + P], Y[:, t, :], ident[:, :])
                last.then_inc(s_ot, 1)
            for c in range(NC):
                pe.wait_ge(s_otc, c + 1)
                if c >= 2:
                    pe.wait_ge(s_x1, c - 1)
                for j, t in enumerate(tiles(c)):
                    last = pe.matmul(PS[:, 2 + c % 2, P * j:P * j + P], HT[:, P * t:P * t + P], Wo0[:, :], start=True, stop=True)
                last.then_inc(s_op, 1)
        a0.close()

        norms_w = {n: sb("g_" + n, [P, w]) for n, w in (("n1r", D), ("n1c", 1), ("n2r", D))}
        rank8 = sb("rank8", [P, 8])
        below = sb("below", [P, P])
        b0 = ExitStack()
        gw = {n: sb("g_" + n, [P, w], F32, b0) for n, w in
              (("qw", D), ("kw", NKV * HD), ("vw", NKV * HD), ("ow", D), ("vb", NKV * HD), ("ob", D), ("qb", 1), ("kb", 1))}
        gw.update(norms_w)
        QST = sb("QST", [STACK + 3, H0, T], BF16, b0)
        KST = sb("KST", [STACK + 3, NKV, T], BF16, b0)
        VS = sb("VS", [P, NT, NKV, 32], F32, b0)
        tmpb = sb("tmpb", [P, 6 * T], BF16, b0)
        QP = tmpb[:, 0:3 * T].rearrange("p (a n) -> p a n", a=3)
        KP = tmpb[0:NKV * HD, 3 * T:6 * T].rearrange("p (a n) -> p a n", a=3)
        PB = tmpb[:, 0:4 * T].bitcast(F32).rearrange("p (b j n) -> p b j n", b=2, j=REP)
        AO = tmpb[:, 4 * T:6 * T].bitcast(F32).rearrange("p (s d) -> p s d", s=NT)
        PV = sb("PV", [P, CH], F32, b0)
        MX = sb("MX", [P, REP * TPC, NC], F32, b0)
        MM = sb("MM", [P, REP * TPC], F32, b0)
        NM = sb("NM", [REP * TPC, P], F32, b0)
        NMP = sb("NMP", [REP * TPC, 2, 3, P], BF16, b0)
        VG = sb("VG", [P, NT, 32], F32, b0)
        RD = sb("RD", [P, TPC, REP], F32, b0)
        scr_q = nc.dram_tensor("scr_q", (3, P, T), BF16).ap()
        scr_k = nc.dram_tensor("scr_k", (3, NKV * HD, T), BF16).ap()

        s_gw = sem("s_gw")
        s_b0q, s_b0k, s_b0v = sem("s_b0q"), sem("s_b0k"), sem("s_b0v")
        s_q32, s_k32, s_split, s_vs = sem("s_q32"), sem("s_k32"), sem("s_split"), sem("s_vs")
        s_scr, s_stack, s_stack_rest = sem("s_scr"), sem("s_stack"), sem("s_stack_rest")
        s_mxmm, s_mxred, s_mm = sem("s_mxmm"), sem("s_mxred"), sem("s_mm")
        s_mt0, s_nm, s_nmp = sem("s_mt0"), sem("s_nm"), sem("s_nmp")
        s_row = [sem(f"s_row{k}") for k in range(2)]
        s_qk, s_exp, s_pv = sem("s_qk"), sem("s_exp"), sem("s_pv")
        s_pvc, s_pvt, s_ao = sem("s_pvc"), sem("s_pvt"), sem("s_ao")
        s_at, s_atc, s_ow, s_src = sem("s_at"), sem("s_atc"), sem("s_ow"), sem("s_src")

        s_vg, s_const2, s_nmfree, s_pvfree = sem("s_vg"), sem("s_const2"), sem("s_nmfree"), sem("s_pvfree")
        UI = NT * REP

        def sp_gqa(sp):
            f = "L0_ffn_"
            for n in ("qw", "kw", "vw", "ow"):
                sp.dma_start(gw[n][:, :], A[f + n]).then_inc(s_gw, 16)
            for n, w in (("vb", "vb"), ("ob", "ob"), ("n1r", "norm1_w"), ("n2r", "norm2_w")):
                sp.dma_start(gw[n][:, :], A[f + w].partition_broadcast(P)).then_inc(s_gw, 16)
            sp.dma_start(gw["qb"][:, :], A[f + "qb"].rearrange("(p a) -> p a", a=1)).then_inc(s_gw, 16)
            sp.dma_start(gw["kb"][0:NKV * HD, :], A[f + "kb"].rearrange("(p a) -> p a", a=1)).then_inc(s_gw, 16)
            sp.dma_start(gw["n1c"][:, :], A[f + "norm1_w"].rearrange("(p a) -> p a", a=1)).then_inc(s_gw, 16)

        GW = 11 * 16

        def sp_stacks(sp):
            sp.wait_ge(s_split, 1)
            sp.dma_start(scr_k.rearrange("a r n -> r a n"), KP).then_inc(s_scr, 16)
            sp.wait_ge(s_const2, 1)
            sp.wait_ge(s_scr, 16)
            for a in range(3):
                for b in range(3):
                    sp.dma_start(KST[(3 * a + b) * HD:(3 * a + b + 1) * HD, :, :],
                                 scr_k[b].rearrange("(g i) n -> i g n", i=HD)).then_inc(s_stack, 16)
            sp.wait_ge(s_split, 2)
            sp.dma_start(scr_q.rearrange("a r n -> r a n"), QP).then_inc(s_scr, 16)
            sp.wait_ge(s_scr, 32)
            for heads, arrived in ((slice(0, REP), s_stack), (slice(REP, H0), s_stack_rest)):
                for a in range(3):
                    for b in range(3):
                        sp.dma_start(QST[(3 * a + b) * HD:(3 * a + b + 1) * HD, heads, :],
                                     scr_q[a].rearrange("(h i) n -> i h n", i=HD)[:, heads, :]).then_inc(arrived, 16)

        STACKED = 2 * 9 * 16

        def g_gqa_pre(g, chain):
            chain.link(g.memset(KST[64:STACK + 3, :, :], 1.0))
            g.memset(VS[:, :, :, :], 0.0).then_inc(s_const2, 1)

        def pe_gqa_pre(pe):
            pe.wait_ge(s_gw, GW)
            for c in range(NC):
                pe.wait_ge(SM["feat"], upto(1, c))
                pe.matmul(PS[:, c, :], gw["qw"][:, :], HT[:, cs(c)], start=True, stop=True).then_inc(s_b0q, 1)
            for c in range(NC):
                if c < 2:
                    pe.matmul(PS[0:NKV * HD, 4 + c, :], gw["kw"][:, :], HT[:, cs(c)], start=True, stop=True).then_inc(s_b0k, 1)
            for c in range(2, NC):
                pe.wait_ge(s_k32, c - 1)
                pe.matmul(PS[0:NKV * HD, 2 + c, :], gw["kw"][:, :], HT[:, cs(c)], start=True, stop=True).then_inc(s_b0k, 1)
            for t in range(NT):
                last = pe.matmul(PS[:, 6, 32 * t:32 * t + 32], HT[:, P * t:P * t + P], gw["vw"][:, :], start=True, stop=True)
            last.then_inc(s_b0v, 1)

        def act_gqa_pre(a):
            a.wait_ge(s_gw, GW)
            for c in range(NC):
                a.wait_ge(s_b0q, c + 1)
                a.activation(Y[:, :, :].rearrange("p s d -> p (s d)")[:, cs(c)], PS[:, c, :], ACT.Identity, bias=gw["qb"][:, 0:1]).then_inc(s_q32, 1)
            a.wait_ge(SM["tok"], NC)
            for c in range(NC):
                a.wait_ge(s_b0k, c + 1)
                a.activation(PVK[:, cs(c)], PS[0:NKV * HD, 4 + c % 2, :], ACT.Identity, bias=gw["kb"][0:NKV * HD, 0:1]).then_inc(s_k32, 1)

        PVK = XN[0:NKV * HD, :, :].rearrange("p s d -> p (s d)")

        def v_gqa_pre(v, chain):
            yq = Y[:, :, :].rearrange("p s d -> p (s d)")
            v.wait_ge(s_k32, NC)
            for x, q in ((PVK, KP), (yq, QP)):
                if x is yq:
                    v.wait_ge(s_q32, NC)
                chain.link(v.tensor_copy(q[:, 0, :], x))
                chain.link(v.tensor_tensor(x, x, q[:, 0, :], ALU.subtract))
                chain.link(v.tensor_copy(q[:, 1, :], x))
                v.tensor_tensor(q[:, 2, :], x, q[:, 1, :], ALU.subtract).then_inc(s_split, 1)
            v.wait_ge(s_b0v, 1)
            v.wait_ge(s_const2, 1)
            v.memset(VS[:, :, :, HD:HD + 1], 1.0)
            v.tensor_tensor(VS[:, :, :, 0:HD], PS[:, 6, :].rearrange("p (t g c) -> p t g c", t=NT, g=NKV),
                            gw["vb"][:, :].rearrange("p (g c) -> p g c", g=NKV).unsqueeze(1).to_broadcast([P, NT, NKV, HD]),
                            ALU.add).then_inc(s_vs, 1)

        def pe_max(pe, g, u, m):
            g, qc = (g, u) if u < NC else (g + 1, u - NC)
            j, t, kc = m // (TPC * NC), m // NC % TPC, m % NC
            pe.wait_ge(s_mxred, u * UI + m + 1)
            pe.matmul(PS[:, 5 + m % 2, :], QST[0:STACK, REP * g + j, CH * qc + P * t:CH * qc + P * t + P],
                      KST[0:STACK, g, cs(kc)], start=True, stop=True).then_inc(s_mxmm, 1)

        def v_max(v, chain, u):
            for m in range(UI):
                v.wait_ge(s_mxmm, u * UI + m + 1)
                r = v.tensor_reduce(MX[:, m // NC, m % NC:m % NC + 1], PS[:, 5 + m % 2, :], AX.X, ALU.max)
                if m < UI - 1:
                    r.then_inc(s_mxred, 1)
            chain.link(r)
            v.sem_inc(s_mxred, 1)
            v.tensor_reduce(MM[:, :], MX[:, :, :], AX.X, ALU.max).then_inc(s_mm, 1)

        def pe_rows(pe, u):
            pe.wait_ge(s_mm, u + 1)
            pe.transpose(PS[0:REP * TPC, 7, 0:P], MM[:, :], ident[:, :]).then_inc(s_mt0, 1)

        def v_rows(v, chain, u):
            v.wait_ge(s_mt0, u + 1)
            chain.link(v.tensor_scalar(NM[:, :], PS[0:REP * TPC, 7, 0:P], -1.0, None, ALU.mult))
            v.sem_inc(s_nm, 1)
            v.wait_ge(s_nmfree, u + 1)
            part = NMP[:, u % 2, :, :]
            chain.link(v.tensor_copy(part[:, 0, :], NM[:, :]))
            chain.link(v.tensor_tensor(NM[:, :], NM[:, :], part[:, 0, :], ALU.subtract))
            chain.link(v.tensor_copy(part[:, 1, :], NM[:, :]))
            v.tensor_tensor(part[:, 2, :], NM[:, :], part[:, 1, :], ALU.subtract).then_inc(s_nmp, 1)

        def sp_rows(sp, g, u):
            g, qc = (g, u) if u < NC else (g + 1, u - NC)
            sp.wait_ge(s_nmp, u + 1)
            for a in range(3):
                for j in range(REP):
                    sp.dma_start(QST[STACK + a:STACK + a + 1, REP * g + j, cs(qc)].rearrange("r (t p) -> r t p", p=P),
                                 NMP[TPC * j:TPC * j + TPC, u % 2, a, :]).then_inc(s_row[u % 2], 16)

        ROWS = 3 * REP * 16

        def pe_unit(pe, g, u, ahead):
            def scores(kt, j):
                pe.wait_ge(s_exp, u * UI + kt * REP + j + 1)
                pe.matmul(PS[:, j, :], KST[0:STACK + 3, g, P * kt:P * kt + P],
                          QST[0:STACK + 3, REP * g + j, cs(u)], start=True, stop=True).then_inc(s_qk, 1)

            def values(kt):
                if kt == 0:
                    pe.wait_ge(s_pvc, u + 1)
                pe.wait_ge(s_exp, u * UI + kt * REP + 2 * REP)
                for j in range(REP):
                    last = pe.matmul(PS[32 * j:32 * j + 32, 4, :], VG[:, kt, :], PB[:, kt % 2, j, :],
                                     start=(kt == 0), stop=(kt == NT - 1), tile_position=(0, 32 * j), skip_group_check=True)
                last.then_inc(s_pv, 1)

            pe.wait_ge(s_row[u % 2], ROWS * (u // 2 + 1))
            pe.sem_inc(s_nmfree, 1)
            if u == 0:
                pe.wait_ge(s_vg, 1)
            for kt in range(NT):
                for j in range(REP):
                    scores(kt, j)
                    if ahead:
                        pe_max(pe, g, u + 2, REP * kt + j)
                if kt:
                    values(kt - 1)
            values(NT - 1)
            if ahead:
                pe_rows(pe, u + 2)
            pe.wait_ge(s_nm, u + 3 if ahead else NC)
            pe.wait_ge(s_ao, u + 1)
            pe.wait_ge(s_pvc, u + 2)
            for t in range(TPC):
                m = pe.transpose(PS[:, 7, P * t:P * t + P], PV[:, P * t:P * t + P], ident[:, :])
            m.then_inc(s_pvt, 1)

        def act_unit(a, u):
            for kt in range(NT):
                a.wait_ge(s_pv, u * NT + kt + 1)
                for j in range(REP):
                    a.wait_ge(s_qk, u * UI + kt * REP + j + 1)
                    a.activation(PB[:, kt % 2, j, :], PS[:, j, :], ACT.Exp, scale=HD ** -0.5).then_inc(s_exp, 1)
            a.wait_ge(s_pv, u * NT + NT + 2)
            a.wait_ge(s_pvfree, u + 1)
            a.activation(PV[:, :], PS[:, 4, :], ACT.Copy).then_inc(s_pvc, 1)

        def v_unit(v, chain, g, u, ahead):
            if ahead:
                v_max(v, chain, u + 2)
                v_rows(v, chain, u + 2)
            v.wait_ge(s_pvt, u + 1)
            v.sem_inc(s_pvfree, 1)
            b7 = PS[:, 7, :].rearrange("p (t j c) -> p t j c", t=TPC, j=REP)
            chain.link(v.reciprocal(RD[:, :, :], b7[:, :, :, HD]))
            ao = AO[:, TPC * u:TPC * u + TPC, bass.ds(g * 32, 32)].rearrange("p t (j c) -> p t j c", j=REP)
            v.tensor_tensor(ao, b7[:, :, :, 0:HD], RD[:, :, :].unsqueeze(3).to_broadcast([P, TPC, REP, HD]), ALU.mult).then_inc(s_ao, 1)

        LAST = NKV - 1

        def sp_gqa_rows(sp):
            for u in range(2):
                sp_rows(sp, 0, u)
            with sp.Fori(0, LAST) as g:
                for u in range(NC):
                    sp_rows(sp, g, u + 2)
                sp.sem_inc(s_nmp, -NC)
            for u in range(2):
                sp_rows(sp, LAST, u + 2)

        def pe_gqa(pe):
            pe.sem_inc(s_pv, 2)
            pe.sem_inc(s_nmfree, 2)
            pe.wait_ge(s_stack, STACKED)
            pe.wait_ge(s_vs, 1)
            for u in range(2):
                for m in range(UI):
                    pe_max(pe, 0, u, m)
                if u:
                    pe.wait_ge(s_nm, u)
                pe_rows(pe, u)
            pe.wait_ge(s_stack_rest, 9 * 16)
            with pe.Fori(0, LAST) as g:
                for u in range(NC):
                    pe_unit(pe, g, u, True)
                pe.sem_inc(s_mxred, -NC * UI)
                pe.sem_inc(s_mm, -NC)
                for s in s_row:
                    pe.sem_inc(s, -NC // 2 * ROWS)
                pe.sem_inc(s_exp, -NC * UI)
                pe.sem_inc(s_pvc, -NC)
                pe.sem_inc(s_vg, -1)
                pe.sem_inc(s_nm, -NC)
                pe.sem_inc(s_ao, -NC)
            for u in range(NC):
                pe_unit(pe, LAST, u, u < 2)
            pe.wait_ge(s_ao, NC + 1)
            for c in range(NC):
                if c >= 2:
                    pe.wait_ge(s_atc, c - 1)
                for j, t in enumerate(tiles(c)):
                    last = pe.transpose(PS[:, c % 2, P * j:P * j + P], AO[:, t, :], ident[:, :])
                last.then_inc(s_at, 1)
            for c in range(NC):
                pe.wait_ge(s_atc, c + 1)
                if c >= 2:
                    pe.wait_ge(s_src, c - 1)
                for j, t in enumerate(tiles(c)):
                    last = pe.matmul(PS[:, 2 + c % 2, P * j:P * j + P], AT[:, P * t:P * t + P], gw["ow"][:, :], start=True, stop=True)
                last.then_inc(s_ow, 1)

        AT = XN[:, :, :].rearrange("p s d -> p (s d)")

        def act_gqa(a):
            a.sem_inc(s_exp, REP)
            a.sem_inc(s_pvc, 1)
            with a.Fori(0, LAST):
                for u in range(NC):
                    act_unit(a, u)
                a.sem_inc(s_pv, -NC * NT)
                a.sem_inc(s_qk, -NC * UI)
                a.sem_inc(s_pvfree, -NC)
            for u in range(NC):
                act_unit(a, u)
            for c in range(NC):
                a.wait_ge(s_at, c + 1)
                a.activation(AT[:, cs(c)], PS[:, c % 2, :], ACT.Copy).then_inc(s_atc, 1)

        def v_gqa(v, chain):
            v.sem_inc(s_mxred, 2)
            v.sem_inc(s_ao, 1)
            v.sem_inc(s_pvfree, 1)

            def head(g):
                v.tensor_copy(VG[:, :, :], VS[:, :, bass.ds(g, 1), :].rearrange("p t g c -> p t (g c)")).then_inc(s_vg, 1)

            for u in range(2):
                v_max(v, chain, u)
                v_rows(v, chain, u)
            with v.Fori(0, LAST) as g:
                n = chain.n
                head(g)
                for u in range(NC):
                    v_unit(v, chain, g, u, True)
                chain.take_back(n)
                v.sem_inc(s_mxmm, -NC * UI)
                v.sem_inc(s_mt0, -NC)
                v.sem_inc(s_nmfree, -NC)
                v.sem_inc(s_pvt, -NC)
            head(LAST)
            for u in range(NC):
                v_unit(v, chain, LAST, u, u < 2)
            obr = gw["ob"][:, :].unsqueeze(1).to_broadcast([P, TPC, D])
            v.wait_ge(SM["tok"], NC)
            for c in range(NC):
                v.wait_ge(s_ow, c + 1)
                chain.link(v.tensor_tensor(Y[:, ts_(c), :], PS[:, 2 + c % 2, :].rearrange("p (t d) -> p t d", t=TPC), obr, ALU.add))
                last = v.tensor_tensor(Y[:, ts_(c), :], Y[:, ts_(c), :], H[:, ts_(c), :], ALU.add)
                chain.link(last)
                v.sem_inc(s_src, 1)

        b0.close()

        RS = {"s_" + n: sem(f"s_r{n}") for n in ("in", "mm", "l", "p", "pd", "w", "tr", "trc", "scr", "cnt", "cntd")}

        def router(tag, stack, E, nth):
            r = {n: sb(f"{n}{tag}", [P, NT, E], F32, stack) for n in ("L", "p", "one", "two", "t", "u", "wt")}
            r.update({n: sb(f"{n}{tag}", [P, NT], F32, stack) for n in ("m", "k")})
            r["gate"] = sb(f"gate{tag}", [P, E], F32, stack)
            r["wtT"] = sb(f"wtT{tag}", [P, P], F32, stack)
            r.update(RS, nth=nth)
            r["scr"] = nc.dram_tensor(f"scr_w{tag}", (NT, E, P), F32).ap()
            return r

        def pe_router(pe, r, feat, arrived):
            pe.wait_ge(r["s_in"], arrived)
            pe.wait_ge(SM["feat"], feat)
            for t in range(NT):
                last = pe.matmul(PS[:, 4, 8 * t:8 * t + 8], HT[:, P * t:P * t + P], r["gate"][:, :], start=True, stop=True)
            last.then_inc(r["s_mm"], 1)

        def bc(ap):
            return ap.unsqueeze(2).to_broadcast([P, NT, 8])

        def v_logits(v, chain, r):
            v.wait_ge(r["s_mm"], r["nth"])
            chain.link(v.tensor_copy(r["L"][:, :, :], PS[:, 4, 0:8 * NT].rearrange("p (t e) -> p t e", e=8)))

        def v_top2(v, chain, r):
            L, t, m, k = r["L"], r["t"], r["m"], r["k"]
            for n, one in enumerate(("one", "two")):
                src = L
                if n:
                    chain.link(v.tensor_scalar(r["u"][:, :, :], r["one"][:, :, :], -1e30, None, ALU.mult))
                    chain.link(v.tensor_tensor(r["u"][:, :, :], r["u"][:, :, :], L[:, :, :], ALU.add))
                    src = r["u"]
                chain.link(v.tensor_reduce(m[:, :], src[:, :, :], AX.X, ALU.max))
                chain.link(v.tensor_tensor(t[:, :, :], src[:, :, :], bc(m[:, :]), ALU.is_equal))
                chain.link(v.tensor_tensor(t[:, :, :], t[:, :, :], rank8[:, :].unsqueeze(1).to_broadcast([P, NT, 8]), ALU.mult))
                chain.link(v.tensor_reduce(k[:, :], t[:, :, :], AX.X, ALU.max))
                chain.link(v.tensor_tensor(r[one][:, :, :], t[:, :, :], bc(k[:, :]), ALU.is_equal))

        def pe_weights(pe, r):
            pe.wait_ge(r["s_w"], r["nth"])
            pe.transpose(PS[:, 5, 0:P], r["wt"][:, :, :].rearrange("p s e -> p (s e)"), ident[:, :]).then_inc(r["s_tr"], 1)

        def v_weights(v, chain, r):
            v.wait_ge(r["s_tr"], r["nth"])
            chain.link(v.tensor_copy(r["wtT"][:, :], PS[:, 5, 0:P]))
            v.sem_inc(r["s_trc"], 1)
            v.sem_inc(r["s_pd"], 1)

        def sp_weights(sp, r):
            sp.wait_ge(r["s_trc"], r["nth"])
            sp.dma_start(r["scr"].rearrange("s e p -> (s e) p"), r["wtT"][:, :]).then_inc(r["s_scr"], 16)
            sp.wait_ge(r["s_scr"], 16 * r["nth"])

        def weight_row(r, e):
            return r["scr"].rearrange("s e p -> e s p")[e].partition_broadcast(P)

        c0 = ExitStack()
        R0 = router("0", c0, E0, 1)
        W1 = sb("W1", [P, 2, F0], F32, c0)
        W2 = sb("W2", [P, 2, F0 // P, D], F32, c0)
        SB = sb("SB", [P, 2, NT, P], F32, c0)
        HID = sb("HID", [P, 4, CH], F32, c0)
        OT = sb("OT", [P, T], F32, c0)
        n2g = sb("n2g", [P, D], F32, c0)
        s_rk, s_x2 = sem("s_rk"), sem("s_x2")
        s_ewfree, s_sbfree = sem("s_ewfree"), sem("s_sbfree")
        s_ew = [sem(f"s_ew{k}") for k in range(2)]
        s_sb0 = [sem(f"s_sb{k}") for k in range(2)]
        s_h, s_g, s_hid, s_hfree = sem("s_h"), sem("s_g"), sem("s_hid"), sem("s_hfree")
        s_oc, s_ott, s_y = sem("s_oc"), sem("s_ott"), sem("s_y")
        M0 = F0 // P
        IT = NC * M0

        def g_rank(g, chain):
            for e in range(8):
                chain.link(g.memset(rank8[:, e:e + 1], float(8 - e)))
            chain.link(g.memset(below[:, :], 1.0))
            g.affine_select(out=below[:, :], in_=below[:, :], compare_op=ALU.is_ge, fill=0.0, base=-1,
                            pattern=[[1, P]], channel_multiplier=-1).then_inc(s_rk, 1)

        def act_route0(a, r):
            a.wait_ge(r["s_l"], r["nth"])
            a.activation(r["p"][:, :, :], r["L"][:, :, :], ACT.Sigmoid).then_inc(r["s_p"], 1)

        def v_route0(v, chain, r):
            v_logits(v, chain, r)
            v.sem_inc(r["s_l"], 1)
            v.wait_ge(s_rk, 1)
            v_top2(v, chain, r)
            one, two, t, u, m = r["one"], r["two"], r["t"], r["u"], r["m"]
            chain.link(v.tensor_tensor(one[:, :, :], one[:, :, :], two[:, :, :], ALU.add))
            a, b = one, t
            for sh in (1, 2, 4, 8):
                v.tensor_copy(b[:, 0:sh, :], a[:, 0:sh, :])
                chain.link(v.tensor_tensor(b[:, sh:NT, :], a[:, sh:NT, :], a[:, 0:NT - sh, :], ALU.add))
                a, b = b, (u if b is t else t)
            chain.link(v.tensor_copy(two[:, 0, :], a[:, NT - 1, :]))
            v.sem_inc(r["s_cnt"], 1)
            chain.link(v.tensor_tensor(a[:, :, :], a[:, :, :], one[:, :, :], ALU.subtract))
            v.wait_ge(r["s_cntd"], 1)
            chain.link(v.tensor_tensor(a[:, :, :], a[:, :, :], PS[:, 6, 0:8].unsqueeze(1).to_broadcast([P, NT, 8]), ALU.add))
            chain.link(v.tensor_scalar(a[:, :, :], a[:, :, :], float(CAP), None, ALU.is_lt))
            v.wait_ge(r["s_p"], r["nth"])
            chain.link(v.tensor_tensor(b[:, :, :], one[:, :, :], r["p"][:, :, :], ALU.mult))
            chain.link(v.tensor_reduce(m[:, :], b[:, :, :], AX.X, ALU.add))
            chain.link(v.tensor_scalar(m[:, :], m[:, :], 1e-6, None, ALU.add))
            chain.link(v.reciprocal(m[:, :], m[:, :]))
            chain.link(v.tensor_tensor(b[:, :, :], b[:, :, :], a[:, :, :], ALU.mult))
            v.tensor_tensor(r["wt"][:, :, :], b[:, :, :], bc(m[:, :]), ALU.mult).then_inc(r["s_w"], 1)
            v_weights(v, chain, r)

        def pe_route0(pe, r):
            pe.wait_ge(r["s_cnt"], 1)
            pe.matmul(PS[:, 6, 0:8], below[:, :], r["two"][:, 0, :], start=True, stop=True).then_inc(r["s_cntd"], 1)
            pe_weights(pe, r)

        def sp_expert0(sp, e, k):
            sp.dma_start(W1[:, k, :], A["L0_ffn_w1"].rearrange("e d f -> d e f")[:, e, :] if isinstance(e, int)
                         else A["L0_ffn_w1"].rearrange("e d f -> d e f")[:, bass.ds(e, 1), :].rearrange("d e f -> d (e f)")).then_inc(s_ew[k], 16)
            w2 = A["L0_ffn_w2"].rearrange("e (m f) d -> f e m d", f=P)
            sp.dma_start(W2[:, k, :, :], w2[:, e, :, :] if isinstance(e, int)
                         else w2[:, bass.ds(e, 1), :, :].rearrange("f e m d -> f (e m) d")).then_inc(s_ew[k], 16)

        def sp_row(sp, r, e, k):
            src = r["scr"].rearrange("s e p -> e s p")
            src = src[e] if isinstance(e, int) else src[bass.ds(e, 1), :, :].rearrange("e s p -> (e s) p")
            sp.dma_start(SB[:, k, :, :], src.partition_broadcast(P)).then_inc(s_sb0[k], 16)

        def sp_moe0(sp, r):
            sp.dma_start(r["gate"][:, :], A["L0_ffn_gate_w"]).then_inc(r["s_in"], 16)
            for k in range(2):
                sp_expert0(sp, k, k)
            sp_weights(sp, r)
            for k in range(2):
                sp_row(sp, r, k, k)
            with sp.Fori(0, E0 // 2 - 1) as i:
                for k in range(2):
                    sp.wait_ge(s_ewfree, k + 2)
                    sp_expert0(sp, i * 2 + (k + 2), k)
                    sp.wait_ge(s_sbfree, k + 1)
                    sp_row(sp, r, i * 2 + (k + 2), k)
                sp.sem_inc(s_ewfree, -2)
                sp.sem_inc(s_sbfree, -2)

        def pe_moe0(pe):
            pe.wait_ge(R0["s_pd"], 1)
            for c in range(NC):
                pe.matmul(PS[:, c, :], ident[:, :], HT[:, cs(c)], start=True, stop=False, skip_group_check=True)
            pe.sem_inc(s_hfree, 4)
            with pe.Fori(0, E0 // 2):
                for i in range(2 * IT + 3):
                    if i < 2 * IT:
                        k, c, m = i // IT, i % IT // M0, i % M0
                        if i % IT == 0:
                            pe.wait_ge(s_ew[k], 32)
                        if i >= 4:
                            pe.wait_ge(s_hid, i - 3)
                        pe.matmul(PS[:, 4 + i % 4, :], W1[:, k, P * m:P * m + P], HT[:, cs(c)], start=True, stop=True).then_inc(s_h, 1)
                    if i >= 3:
                        o = i - 3
                        k, c, m = o // IT, o % IT // M0, o % M0
                        pe.wait_ge(s_hid, o + 1)
                        if o % IT == IT - 1:
                            pe.sem_inc(s_sbfree, 1)
                        pe.matmul(PS[:, c, :], W2[:, k, m, :], HID[:, o % 4, :], start=False, stop=False, skip_group_check=True).then_inc(s_hfree, 1)
                for s in s_ew:
                    pe.sem_inc(s, -32)
                pe.sem_inc(s_hid, -2 * IT)

        def act_moe0(a):
            with a.Fori(0, E0 // 2):
                for i in range(2 * IT):
                    a.wait_ge(s_h, i + 1)
                    a.wait_ge(s_hfree, i + 1)
                    if i in (3, IT + 3):
                        a.sem_inc(s_ewfree, 1)
                    a.activation(HID[:, i % 4, :], PS[:, 4 + i % 4, :], ACT.Gelu).then_inc(s_g, 1)
                a.sem_inc(s_h, -2 * IT)
                a.sem_inc(s_hfree, -2 * IT)

        def v_moe0(v):
            with v.Fori(0, E0 // 2):
                for i in range(2 * IT):
                    k, c = i // IT, i % IT // M0
                    if i % IT == 0:
                        v.wait_ge(s_sb0[k], 16)
                    v.wait_ge(s_g, i + 1)
                    v.tensor_tensor(HID[:, i % 4, :], HID[:, i % 4, :], SB[:, k, ts_(c), :].rearrange("p t n -> p (t n)"),
                                    ALU.mult).then_inc(s_hid, 1)
                for s in s_sb0:
                    v.sem_inc(s, -16)
                v.sem_inc(s_g, -2 * IT)

        def pe_back(pe, n, OT):
            for c in range(NC):
                pe.wait_ge(s_oc, NC * n + c + 1)
                if n or c:
                    pe.wait_ge(s_y, NC * n + c)
                for j, t in enumerate(tiles(c)):
                    last = pe.transpose(PS[:, 7, P * j:P * j + P], OT[:, P * t:P * t + P], ident[:, :])
                last.then_inc(s_ott, 1)

        def act_back(a, n, OT, hfree, scale):
            a.wait_ge(hfree, 4)
            for c in range(NC):
                a.activation(OT[:, cs(c)], PS[:, c, :], ACT.Identity, scale=scale).then_inc(s_oc, 1)
        c0.close()

        d0 = ExitStack()
        KF = FB // P
        WA = sb("WA", [P, 2, 4, D], F32, d0)
        WF1 = sb("WF1", [P, 2, FB], F32, d0)
        WF2 = sb("WF2", [P, 2, KF, D], F32, d0)
        RW = sb("RW", [P, 2, 4, D], F32, d0)
        CL = sb("CL", [P, 2, 9 + KF], F32, d0)
        EX = sb("EX", [P, 2, 2, CH], F32, d0)
        TQ = sb("TQ", [P, 2, 2, CH], F32, d0)
        Q1 = sb("Q1", [P, T], F32, d0)
        K1 = sb("K1", [P, CH], F32, d0)
        acc = sb("acc", [P, 2, NC], F32, d0)
        KS = sb("KS", [P, 2], F32, d0)
        Z1 = sb("Z1", [P, 2, 2, CH], F32, d0)
        HF = sb("HF", [P, 2, KF, CH], F32, d0)
        s_lw = [sem(f"s_lw{k}") for k in range(2)]
        s_lwfree, s_lwfree_a = sem("s_lwfree"), sem("s_lwfree_a")
        s_q, s_k, s_v = sem("s_q"), sem("s_k"), sem("s_v")
        s_eq, s_qkvfree = sem("s_eq"), sem("s_qkvfree")
        s_exfree, s_qd, s_ks = sem("s_exfree"), sem("s_qd"), sem("s_ks")
        s_rz, s_vv = sem("s_rz"), sem("s_vv")
        s_wo, s_zfree = sem("s_wo"), sem("s_zfree")
        s_x3 = sem("s_x3")
        s_f1 = sem("s_f1")

        def sp_block(sp, b, k):
            def of(name):
                ap = A["L1_attn_" + name]
                ap = ap[b] if isinstance(b, int) else ap[bass.ds(b, 1)]
                if not isinstance(b, int):
                    ap = ap.rearrange("b i j -> (b i) j") if len(ap.shape) == 3 else ap.rearrange("b i -> (b i)")
                return ap
            for j, w in enumerate(("Wq", "Wk", "Wv", "Wo")):
                sp.dma_start(WA[:, k, j, :], of(w)).then_inc(s_lw[k], 16)
            sp.dma_start(WF1[:, k, :], of("Wf1")).then_inc(s_lw[k], 16)
            sp.dma_start(WF2[:, k, :, :], of("Wf2").rearrange("(m f) d -> f m d", f=P)).then_inc(s_lw[k], 16)
            for j, w in enumerate(("ln1_s", "ln1_b", "ln2_s", "ln2_b")):
                sp.dma_start(RW[:, k, j, :], of(w).partition_broadcast(P)).then_inc(s_lw[k], 16)
            for j, w in enumerate(("bq", "bk", "bv", "ln1_s", "ln1_b", "ln2_s", "ln2_b", "bo", "bf2")):
                sp.dma_start(CL[:, k, j:j + 1], of(w).rearrange("(p a) -> p a", a=1)).then_inc(s_lw[k], 16)
            for m in range(KF):
                sp.dma_start(CL[:, k, 9 + m:10 + m], of("bf1")[P * m:P * m + P].rearrange("(p a) -> p a", a=1)).then_inc(s_lw[k], 16)

        LW = (4 + 2 + 4 + 9 + KF) * 16

        def sp_blocks(sp):
            for k in range(2):
                sp_block(sp, k, k)
            with sp.Fori(0, NB // 2 - 1) as i:
                for k in range(2):
                    sp.wait_ge(s_lwfree, k + 1)
                    sp.wait_ge(s_lwfree_a, k + 1)
                    sp_block(sp, i * 2 + (k + 2), k)
                sp.sem_inc(s_lwfree, -2)
                sp.sem_inc(s_lwfree_a, -2)

        def pe_qkv(pe, k):
            for c in range(NC):
                n = NC * k + c
                pe.wait_ge(S2["feat"], upto(k, c))
                for j, s in enumerate((s_q, s_k, s_v)):
                    if j == 0:
                        pe.wait_ge(s_qkvfree, n + 1)
                    pe.matmul(PS[:, 3 * (c % 2) + j, :], WA[:, k, j, :], HT[:, cs(c)], start=True, stop=True).then_inc(s, 1)

        def act_qkv(a, k):
            for c in range(NC):
                n = NC * k + c
                a.wait_ge(s_exfree, n + 1)
                for j, s in enumerate((s_q, s_k)):
                    a.wait_ge(s, n + 1)
                    a.activation(TQ[:, c % 2, j, :], PS[:, 3 * (c % 2) + j, :], ACT.Relu, bias=CL[:, k, j:j + 1])
                    a.activation(EX[:, c % 2, j, :], PS[:, 3 * (c % 2) + j, :], ACT.Exp, bias=CL[:, k, j:j + 1]).then_inc(s_eq, 1)

        def v_qkv(v, chain, k):
            for c in range(NC):
                n, b = NC * k + c, 3 * (c % 2)
                v.wait_ge(s_eq, 2 * n + 2)
                chain.link(v.tensor_scalar(EX[:, c % 2, :, :], EX[:, c % 2, :, :], 1.0, -1.0, ALU.min, ALU.add))
                for j in range(2):
                    if j == 0:
                        v.scalar_tensor_tensor(out=Q1[:, cs(c)], in0=EX[:, c % 2, 0, :], scalar=1.0, in1=TQ[:, c % 2, 0, :],
                                               op0=ALU.add, op1=ALU.add)
                    else:
                        chain.link(v.scalar_tensor_tensor(out=K1[:, :], in0=EX[:, c % 2, 1, :], scalar=1.0, in1=TQ[:, c % 2, 1, :],
                                                          op0=ALU.add, op1=ALU.add, accum_out=acc[:, 1, c:c + 1]))
                v.sem_inc(s_exfree, 1)
                v.wait_ge(s_v, n + 1)
                chain.link(v.scalar_tensor_tensor(out=K1[:, :], in0=PS[:, b + 2, :], scalar=CL[:, k, 2:3], in1=K1[:, :],
                                                  op0=ALU.add, op1=ALU.mult, accum_out=acc[:, 0, c:c + 1]))
                v.sem_inc(s_qkvfree, 1)
            chain.link(v.tensor_reduce(KS[:, :], acc[:, :, :], AX.X, ALU.add))
            v.sem_inc(s_ks, 1)

        def act_rz(a, chain, k):
            a.wait_ge(s_ks, k + 1)
            for c in range(NC):
                n = NC * k + c
                a.wait_ge(s_qd, n + 1)
                last = a.activation(ZR[:, c, :], Q1[:, cs(c)], ACT.Ln, scale=KS[:, 1:2], bias=eps1[:, 0:1])
            chain.link(last)
            for c in range(NC):
                a.activation(ZR[:, c, :], ZR[:, c, :], ACT.Exp, scale=-1.0).then_inc(s_rz, 1)

        ZR = sb("ZR", [P, NC, CH], F32, d0)

        def v_vv(v, chain, k, c):
            n = NC * k + c
            v.wait_ge(s_rz, n + 1)
            chain.link(v.scalar_tensor_tensor(out=Q1[:, cs(c)], in0=Q1[:, cs(c)], scalar=KS[:, 0:1], in1=ZR[:, c, :],
                                              op0=ALU.mult, op1=ALU.mult))
            v.sem_inc(s_qd, 1)
            v.sem_inc(s_vv, 1)

        def pe_wo(pe, k, c):
            n = NC * k + c
            pe.wait_ge(s_vv, n + 1)
            pe.wait_ge(s_zfree, n + 1)
            pe.matmul(PS[:, 3, :], WA[:, k, 3, :], Q1[:, cs(c)], start=True, stop=True).then_inc(s_wo, 1)

        def act_side(a, k, c, side):
            bank, done = ((3, s_wo), (6, s_f2))[side]
            a.wait_ge(done, NC * k + c + 1)
            a.activation(Z1[:, side, c % 2, :], PS[:, bank, :], ACT.Gelu_apprx_tanh,
                         bias=CL[:, k, 7 + side:8 + side]).then_inc(s_ge[side], 1)

        def pe_side(pe, k, c, side):
            pe.wait_ge(s_ge[side], NC * k + c + 1)
            for j in range(TPC):
                last = pe.transpose(PS[:, 3 + 3 * side, P * j:P * j + P], Z1[:, side, c % 2, P * j:P * j + P], ident[:, :])
            last.then_inc(s_z[side], 1)

        def v_resid(v, chain, k, c, side):
            v.wait_ge(s_z[side], NC * k + c + 1)
            v.wait_ge((S1 if side else S2)["tok"], upto(k, c))
            chain.link(v.tensor_tensor(Y[:, ts_(c), :], PS[:, 3 + 3 * side, :].rearrange("p (t d) -> p t d", t=TPC),
                                       H[:, ts_(c), :], ALU.add))
            v.sem_inc((s_zfree, s_f2free)[side], 1)
            norm_stats(v, chain, S2 if side else S1, Y, c, 1e-6, False)

        s_z = [sem(f"s_z{i}") for i in range(2)]
        s_ge = [sem(f"s_ge{i}") for i in range(2)]
        s_f2, s_f2free = sem("s_f2"), sem("s_f2free")

        def pe_f1(pe, k, c):
            pe.wait_ge(S1["feat"], upto(k, c))
            for m in range(KF):
                i = KF * (NC * k + c) + m
                pe.wait_ge(s_f1free, i + 1)
                pe.matmul(PS[:, 4 + m % 2, :], WF1[:, k, P * m:P * m + P], HT[:, cs(c)], start=True, stop=True).then_inc(s_f1, 1)

        s_f1free = sem("s_f1free")

        def act_f1(a, k, c):
            n = NC * k + c
            for m in range(KF):
                a.wait_ge(s_f1, KF * n + m + 1)
                a.activation(HF[:, c % 2, m, :], PS[:, 4 + m % 2, :], ACT.Gelu_apprx_tanh,
                             bias=CL[:, k, 9 + m:10 + m]).then_inc(s_f1free, 1)

        def pe_f2(pe, k, c):
            n = NC * k + c
            pe.wait_ge(s_f1free, KF * (n + 1) + 2)
            pe.wait_ge(s_f2free, n + 1)
            for m in range(KF):
                last = pe.matmul(PS[:, 6, :], WF2[:, k, m, :], HF[:, c % 2, m, :], start=(m == 0), stop=(m == KF - 1))
            last.then_inc(s_f2, 1)

        SLOTS = NC + 2

        def pe_blocks(pe):
            pe.sem_inc(s_qkvfree, 2)
            pe.sem_inc(s_zfree, 1)
            pe.sem_inc(s_f1free, 2)
            pe.sem_inc(s_f2free, 1)
            with pe.Fori(0, NB // 2):
                for k in range(2):
                    pe.wait_ge(s_lw[k], LW)
                    pe_qkv(pe, k)
                    for t in range(SLOTS):
                        first, middle, last = t < NC, 0 <= t - 1 < NC, t - 2 >= 0
                        if first:
                            pe_wo(pe, k, t)
                        if middle:
                            norm_turn(pe, S1, k, t - 1, (S2["feat"], NC + NC * k + t - 2) if t >= 3 else None)
                        if last:
                            pe_side(pe, k, t - 2, 1)
                        if first:
                            pe_side(pe, k, t, 0)
                        if middle:
                            pe_f1(pe, k, t - 1)
                            pe_f2(pe, k, t - 1)
                        if last:
                            norm_turn(pe, S2, k, t - 2, (S2["feat"], NC + NC * k + t - 2))
                for s in (S1["normed"], S2["normed"], S1["feat"], S2["feat"], s_qkvfree, s_vv, s_zfree, s_f2free, *s_ge):
                    pe.sem_inc(s, -2 * NC)
                pe.sem_inc(s_f1free, -2 * NC * KF)
                for s in s_lw:
                    pe.sem_inc(s, -LW)

        def act_blocks(a, chain):
            a.sem_inc(s_exfree, 2)
            a.sem_inc(s_qd, NC)
            with a.Fori(0, NB // 2):
                n = chain.n
                for k in range(2):
                    act_qkv(a, k)
                    act_rz(a, chain, k)
                    for t in range(SLOTS):
                        first, middle, last = t < NC, 0 <= t - 1 < NC, t - 2 >= 0
                        if last:
                            act_side(a, k, t - 2, 1)
                        if first:
                            act_side(a, k, t, 0)
                        if middle:
                            norm_feat(a, S1, k, t - 1, CL[:, k, 3:4], CL[:, k, 4:5])
                            act_f1(a, k, t - 1)
                        if last:
                            norm_apply(a, S2, Y, k, t - 2)
                        if first:
                            norm_apply(a, S1, Y, k, t)
                        if last:
                            norm_feat(a, S2, k, t - 2, CL[:, k, 5:6], CL[:, k, 6:7])
                    a.drain()
                    a.sem_inc(s_lwfree_a, 1)
                chain.take_back(n)
                for s in (S1["rstd"], S2["rstd"], S1["turned"], S2["turned"], s_q, s_k, s_exfree, s_qd, s_wo, s_f2):
                    a.sem_inc(s, -2 * NC)
                a.sem_inc(s_ks, -2)
                a.sem_inc(s_f1, -2 * NC * KF)

        def v_blocks(v, chain):
            with v.Fori(0, NB // 2):
                n = chain.n
                for k in range(2):
                    v_qkv(v, chain, k)
                    for c in range(NC):
                        v_vv(v, chain, k, c)
                    for t in range(SLOTS):
                        if t - 2 >= 0:
                            v_resid(v, chain, k, t - 2, 1)
                        if t < NC:
                            v_resid(v, chain, k, t, 0)
                        if 0 <= t - 1 < NC:
                            norm_tok(v, chain, S1, k, t - 1, RW[:, k, 0, :], RW[:, k, 1, :])
                        if t - 2 >= 0:
                            norm_tok(v, chain, S2, k, t - 2, RW[:, k, 2, :], RW[:, k, 3, :])
                    v.drain()
                    v.sem_inc(s_lwfree, 1)
                chain.take_back(n)
                for s in (S1["tok"], S2["tok"], S1["normg"], S2["normg"], s_v, s_rz, *s_z):
                    v.sem_inc(s, -2 * NC)
                v.sem_inc(s_eq, -4 * NC)

        def g_blocks(g, chain):
            with g.Fori(0, NB // 2):
                n = chain.n
                for k in range(2):
                    for t in range(SLOTS):
                        if t - 2 >= 0:
                            norm_rstd(g, chain, S2, k, t - 2, False)
                        if t < NC:
                            norm_rstd(g, chain, S1, k, t, False)
                chain.take_back(n)
                for s in (S1["stat"], S2["stat"]):
                    g.sem_inc(s, -2 * NC)
        d0.close()

        e0 = ExitStack()
        R1 = router("1", e0, E1, 2)
        HTILES = [(m, min(P, F1 - m)) for m in range(0, F1, P)]
        M1 = len(HTILES)
        IT1 = NC * M1
        G1 = sb("G1", [P, 2, F1], F32, e0)
        G3 = sb("G3", [P, 2, F1], F32, e0)
        G2 = sb("G2", [P, 2, M1, D], F32, e0)
        SB1 = sb("SB1", [P, 2, NT, P], F32, e0)
        XS = sb("XS", [P, 2, CH], F32, e0)
        HG = sb("HG", [P, 4, CH], F32, e0)
        OT1 = sb("OT1", [P, T], F32, e0)
        zero = sb("zero", [P, CH], F32, e0)
        s_zero = sem("s_zero")
        s_gwfree, s_sb1free = sem("s_gwfree"), sem("s_sb1free")
        s_xs, s_xsfree = sem("s_xs"), sem("s_xsfree")
        s_z3 = sem("s_z3")
        EW1 = 16 * 4

        def v_route1(v, chain, r):
            v_logits(v, chain, r)
            chain.link(v.tensor_reduce(r["m"][:, :], r["L"][:, :, :], AX.X, ALU.max))
            chain.link(v.tensor_tensor(r["wt"][:, :, :], r["L"][:, :, :], bc(r["m"][:, :]), ALU.subtract))
            v.sem_inc(r["s_l"], 1)
            v_top2(v, chain, r)
            chain.link(v.tensor_tensor(r["one"][:, :, :], r["one"][:, :, :], r["two"][:, :, :], ALU.add))
            v.wait_ge(r["s_p"], r["nth"])
            chain.link(v.tensor_reduce(r["m"][:, :], r["p"][:, :, :], AX.X, ALU.add))
            chain.link(v.reciprocal(r["m"][:, :], r["m"][:, :]))
            chain.link(v.tensor_tensor(r["one"][:, :, :], r["one"][:, :, :], r["p"][:, :, :], ALU.mult))
            v.tensor_tensor(r["wt"][:, :, :], r["one"][:, :, :], bc(r["m"][:, :]), ALU.mult).then_inc(r["s_w"], 1)
            v_weights(v, chain, r)

        def act_route1(a, r):
            a.wait_ge(r["s_l"], r["nth"])
            a.activation(r["p"][:, :, :], r["wt"][:, :, :], ACT.Exp).then_inc(r["s_p"], 1)

        def sp_expert1(sp, e, k):
            def of(name):
                return A["L1_ffn_" + name][bass.ds(e, 1)].rearrange("e i j -> (e i) j")
            w2 = of("w2")
            full = F1 // P * P
            sp.dma_start(G1[:, k, :], of("w1")).then_inc(s_ew[k], 16)
            sp.dma_start(G3[:, k, :], of("w3")).then_inc(s_ew[k], 16)
            sp.dma_start(G2[:, k, 0:full // P, :], w2[0:full].rearrange("(m f) d -> f m d", f=P)).then_inc(s_ew[k], 16)
            sp.dma_start(G2[0:F1 - full, k, M1 - 1, :], w2[full:F1]).then_inc(s_ew[k], 16)

        def sp_row1(sp, e, k):
            src = R1["scr"].rearrange("s e p -> e s p")[bass.ds(e, 1), :, :].rearrange("e s p -> (e s) p")
            sp.dma_start(SB1[:, k, :, :], src.partition_broadcast(P)).then_inc(s_sb0[k], 16)

        def sp_moe1(sp):
            for e in range(E1):
                sp.dma_start(R1["gate"][:, e:e + 1], A["L1_ffn_gate_w"][e].rearrange("(p a) -> p a", a=1)).then_inc(R1["s_in"], 16)
            for k in range(2):
                sp_expert1(sp, k, k)
            sp_weights(sp, R1)
            for k in range(2):
                sp_row1(sp, k, k)
            with sp.Fori(0, E1 // 2 - 1) as i:
                for k in range(2):
                    sp.wait_ge(s_gwfree, k + 2)
                    sp_expert1(sp, i * 2 + (k + 2), k)
                    sp.wait_ge(s_sb1free, k + 1)
                    sp_row1(sp, i * 2 + (k + 2), k)
                sp.sem_inc(s_gwfree, -2)
                sp.sem_inc(s_sb1free, -2)

        def g_moe1(g, chain):
            with g.Fori(0, E1 // 2):
                n = chain.n
                for k in range(2):
                    g.wait_ge(s_sb0[k], 16)
                    for c in range(NC):
                        i = NC * k + c
                        g.wait_ge(s_xsfree, i + 1)
                        chain.link(g.tensor_tensor(XS[:, c % 2, :], HT[:, cs(c)],
                                                   SB1[:, k, ts_(c), :].rearrange("p t n -> p (t n)"), ALU.mult))
                        g.sem_inc(s_xs, 1)
                    g.sem_inc(s_sb1free, 1)
                chain.take_back(n)
                for s in s_sb0:
                    g.sem_inc(s, -16)
                g.sem_inc(s_xsfree, -2 * NC)

        def pe_moe1(pe):
            pe.wait_ge(R1["s_pd"], 2)
            pe.wait_ge(s_zero, 1)
            for c in range(NC):
                pe.matmul(PS[:, c, :], ident[:, :], zero[:, :], start=True, stop=False, skip_group_check=True)
            pe.sem_inc(s_xsfree, 2)
            with pe.Fori(0, E1 // 2):
                for i in range(2 * IT1 + 2):
                    if i < 2 * IT1:
                        k, c, (f, w) = i // IT1, i % IT1 // M1, HTILES[i % M1]
                        if i % IT1 == 0:
                            pe.wait_ge(s_ew[k], EW1)
                        if i % M1 == 0:
                            pe.wait_ge(s_xs, i // M1 + 1)
                        if i >= 2:
                            pe.wait_ge(s_hid, i - 1)
                        b = 4 + 2 * (i % 2)
                        pe.matmul(PS[0:w, b, :], G1[:, k, f:f + w], XS[:, c % 2, :], start=True, stop=True).then_inc(s_h, 1)
                        last = pe.matmul(PS[0:w, b + 1, :], G3[:, k, f:f + w], XS[:, c % 2, :], start=True, stop=True)
                        last.then_inc(s_z3, 1)
                    if i >= 2:
                        o = i - 2
                        k, c, m = o // IT1, o % IT1 // M1, o % M1
                        w = HTILES[m][1]
                        pe.wait_ge(s_hid, o + 1)
                        if m == M1 - 1:
                            pe.sem_inc(s_xsfree, 1)
                        pe.matmul(PS[:, c, :], G2[0:w, k, m, :], HG[0:w, o % 4, :], start=False, stop=False,
                                  skip_group_check=True).then_inc(s_hfree, 1)
                for s in s_ew:
                    pe.sem_inc(s, -EW1)
                pe.sem_inc(s_xs, -2 * NC)
                pe.sem_inc(s_hid, -2 * IT1)

        def act_moe1(a):
            with a.Fori(0, E1 // 2):
                for i in range(2 * IT1):
                    w = HTILES[i % M1][1]
                    a.wait_ge(s_h, i + 1)
                    a.wait_ge(s_hfree, i + 1)
                    if i in (3, IT1 + 3):
                        a.sem_inc(s_gwfree, 1)
                    a.activation(HG[0:w, i % 4, :], PS[0:w, 4 + 2 * (i % 2), :], ACT.Silu).then_inc(s_g, 1)
                a.sem_inc(s_h, -2 * IT1)
                a.sem_inc(s_hfree, -2 * IT1)

        def v_moe1(v):
            with v.Fori(0, E1 // 2):
                for i in range(2 * IT1):
                    w = HTILES[i % M1][1]
                    v.wait_ge(s_g, i + 1)
                    v.wait_ge(s_z3, i + 1)
                    v.tensor_tensor(HG[0:w, i % 4, :], HG[0:w, i % 4, :], PS[0:w, 5 + 2 * (i % 2), :], ALU.mult).then_inc(s_hid, 1)
                v.sem_inc(s_g, -2 * IT1)
                v.sem_inc(s_z3, -2 * IT1)

        def v_last(v):
            for c in range(NC):
                v.wait_ge(s_ott, NC + c + 1)
                v.tensor_tensor(X[:, ts_(c), :], X[:, ts_(c), :], PS[:, 7, :].rearrange("p (t d) -> p t d", t=TPC),
                                ALU.add).then_inc(s_y, 1)
        e0.close()

        block = ctx.enter_context(nc.Block())

        @block.sync
        def _(sp):
            sp_pre(sp)
            sp.wait_ge(s_x1, NC)
            sp_gqa(sp)
            sp_stacks(sp)
            sp_gqa_rows(sp)
            sp.wait_ge(s_src, NC)
            sp_moe0(sp, R0)
            sp.wait_ge(s_x2, NC)
            sp_blocks(sp)
            sp.wait_ge(s_x3, NC)
            sp_moe1(sp)
            for c in range(NC):
                sp.wait_ge(s_y, NC + c + 1)
                sp.dma_start(out[0].rearrange("(p s) d -> p s d", p=P)[:, ts_(c), :], X[:, ts_(c), :]).then_inc(s_done, 16)
            sp.wait_ge(s_done, 16 * NC)

        @block.gpsimd
        def _(g):
            chain = Chain(g, ch_g)
            g_pre(g, chain)
            for c in range(NC):
                norm_rstd(g, chain, SM, 0, c, False)
            g_a0(g)
            g_out(g)
            g.wait_ge(s_x1, NC)
            for c in range(NC):
                norm_rstd(g, chain, SM, 1, c, False)
            g.wait_ge(SM["rstd"], 2 * NC)
            g_gqa_pre(g, chain)
            g.wait_ge(s_const2, 1)
            g_rank(g, chain)
            for c in range(NC):
                norm_rstd(g, chain, SM, 2, c, True)
            for c in range(NC):
                norm_rstd(g, chain, SM, 3, c, True)
            for c in range(NC):
                norm_rstd(g, chain, S4, 4, c, False)
            g_blocks(g, chain)
            g.wait_ge(s_x3, NC)
            g.memset(zero[:, :], 0.0).then_inc(s_zero, 1)
            for c in range(NC):
                norm_rstd(g, chain, SM, 5, c, False)
            g.wait_ge(SM["feat"], 6 * NC)
            g_moe1(g, chain)

        @block.scalar
        def _(a):
            act_pre(a)
            a.wait_ge(s_mod, 1)
            for c in range(NC):
                norm_apply(a, SM, X, 0, c)
                norm_feat(a, SM, 0, c, modc[:, 0, 1:2], modc[:, 0, 0:1])
            act_a0(a)
            act_out(a)
            for c in range(NC):
                norm_apply(a, SM, X, 1, c)
                norm_feat(a, SM, 1, c, modc[:, 0, 4:5], modc[:, 0, 3:4])
            act_gqa_pre(a)
            act_gqa(a)
            for c in range(NC):
                norm_apply(a, SM, Y, 2, c)
                norm_feat(a, SM, 2, c, gw["n1c"][:, 0:1], zero1[:, 0:1])
            act_route0(a, R0)
            act_moe0(a)
            act_back(a, 0, OT, s_hfree, 1.0)
            for c in range(NC):
                norm_apply(a, SM, Y, 3, c)
            for c in range(NC):
                norm_apply(a, S4, X, 4, c)
                norm_feat(a, S4, 4, c, modc[:, 1, 1:2], modc[:, 1, 0:1])
            act_blocks(a, Chain(a, ch_a))
            for c in range(NC):
                norm_apply(a, SM, X, 5, c)
                norm_feat(a, SM, 5, c, modc[:, 1, 4:5], modc[:, 1, 3:4])
            act_route1(a, R1)
            act_moe1(a)
            act_back(a, 1, OT1, s_hfree, modc[:, 1, 5:6])

        @block.tensor
        def _(pe):
            pe_pre(pe)
            pe.wait_ge(s_const, 1)
            for c in range(NC):
                norm_turn(pe, SM, 0, c, (SM["feat"], NC * 0 + c) if c else None)
            pe_a0(pe)
            pe_chain(pe)
            pe_out(pe)
            for c in range(NC):
                norm_turn(pe, SM, 1, c, (SM["feat"], NC * 1 + c))
            pe_gqa_pre(pe)
            pe_gqa(pe)
            for c in range(NC):
                norm_turn(pe, SM, 2, c, (SM["feat"], NC * 2 + c))
            pe_router(pe, R0, 3 * NC, 16)
            pe_route0(pe, R0)
            pe_moe0(pe)
            pe_back(pe, 0, OT)
            pe.wait_ge(SM["normed"], 4 * NC)
            pe.sem_inc(SM["normg"], NC)
            pe.sem_inc(SM["turned"], NC)
            for c in range(NC):
                norm_turn(pe, S4, 4, c, (S2["feat"], c) if c else (s_y, NC))
            pe_blocks(pe)
            pe.sem_inc(SM["feat"], 2 * NC)
            for c in range(NC):
                norm_turn(pe, SM, 5, c, (SM["feat"], 5 * NC + c) if c else (S2["feat"], NC))
            pe_router(pe, R1, 6 * NC, 16 + 16 * E1)
            pe_weights(pe, R1)
            pe_moe1(pe)
            pe_back(pe, 1, OT1)

        @block.vector
        def _(v):
            chain = Chain(v, ch_v)
            v.wait_ge(s_x, 16)
            for c in range(NC):
                norm_stats(v, chain, SM, X, c, 1e-5, False)
            v_pre(v, chain)
            v_a0(v, chain)
            v_chain(v, chain)
            v_out(v, chain)
            v.wait_ge(s_x1, NC)
            for c in range(NC):
                norm_stats(v, chain, SM, X, c, 1e-5, False)
            for c in range(NC):
                norm_tok(v, chain, SM, 1, c, modr[:, 0, 4, :], modr[:, 0, 3, :])
            v_gqa_pre(v, chain)
            v_gqa(v, chain)
            for c in range(NC):
                norm_stats(v, chain, SM, Y, c, 1e-6, True)
            v_route0(v, chain, R0)
            v_moe0(v)
            v.tensor_tensor(n2g[:, :], modr[:, 0, 5, :], gw["n2r"][:, :], ALU.mult)
            for c in range(NC):
                v.wait_ge(s_ott, c + 1)
                chain.link(v.tensor_copy(Y[:, ts_(c), :], PS[:, 7, :].rearrange("p (t d) -> p t d", t=TPC)))
                v.sem_inc(s_y, 1)
            for c in range(NC):
                norm_stats(v, chain, SM, Y, c, 1e-6, True)
            for c in range(NC):
                v.wait_ge(SM["normed"], 3 * NC + c + 1)
                chain.link(v.tensor_tensor(XN[:, ts_(c), :], XN[:, ts_(c), :], n2g[:, :].unsqueeze(1).to_broadcast([P, TPC, D]), ALU.mult))
                v.tensor_tensor(X[:, ts_(c), :], X[:, ts_(c), :], XN[:, ts_(c), :], ALU.add).then_inc(s_x2, 1)
            v.wait_ge(s_x2, NC)
            for c in range(NC):
                norm_stats(v, chain, S4, X, c, 1e-5, False)
            for c in range(NC):
                norm_tok(v, chain, S4, 4, c, modr[:, 1, 1, :], modr[:, 1, 0, :])
            v_blocks(v, chain)
            for c in range(NC):
                v.wait_ge(S2["tok"], upto(0, c))
                chain.link(v.tensor_tensor(H[:, ts_(c), :], H[:, ts_(c), :], modr[:, 1, 2, :].unsqueeze(1).to_broadcast([P, TPC, D]), ALU.mult))
                v.tensor_tensor(X[:, ts_(c), :], X[:, ts_(c), :], H[:, ts_(c), :], ALU.add).then_inc(s_x3, 1)
            v.wait_ge(s_x3, NC)
            for c in range(NC):
                norm_stats(v, chain, SM, X, c, 1e-5, False)
            v_route1(v, chain, R1)
            v_moe1(v)
            v_last(v)



NAMES = [
    "L0_attn_x", "L0_attn_Wq", "L0_attn_Wk", "L0_attn_Wv", "L0_attn_Wo", "L0_attn_Wbet", "L0_attn_Wf", "L0_attn_norm_w",
    "L0_ffn_qw", "L0_ffn_qb", "L0_ffn_kw", "L0_ffn_kb", "L0_ffn_vw", "L0_ffn_vb", "L0_ffn_ow", "L0_ffn_ob",
    "L0_ffn_gate_w", "L0_ffn_w1", "L0_ffn_w2", "L0_ffn_norm1_w", "L0_ffn_norm2_w", "L0_c", "L0_wmod",
    "L1_attn_Wq", "L1_attn_bq", "L1_attn_Wk", "L1_attn_bk", "L1_attn_Wv", "L1_attn_bv", "L1_attn_Wo", "L1_attn_bo",
    "L1_attn_ln1_s", "L1_attn_ln1_b", "L1_attn_Wf1", "L1_attn_bf1", "L1_attn_Wf2", "L1_attn_bf2",
    "L1_attn_ln2_s", "L1_attn_ln2_b", "L1_ffn_gate_w", "L1_ffn_w1", "L1_ffn_w2", "L1_ffn_w3", "L1_c", "L1_wmod",
]


def kernel(**inputs):
    import numpy as np
    import concourse.bacc as bacc
    from concourse.bass_utils import run_bass_kernel_spmd

    nc = bacc.Bacc("TRN2", target_bir_lowering=False, num_devices=1)
    arrays, A = {}, {}
    for name in NAMES:
        a = np.ascontiguousarray(inputs[name])
        arrays[f"in_{name}"] = a
        A[name] = nc.dram_tensor(f"in_{name}", a.shape, mybir.dt.from_np(a.dtype), kind="ExternalInput").ap()
    out = nc.dram_tensor("out_x", (1, T, D), F32, kind="ExternalOutput").ap()
    build(nc, A, out)
    r = run_bass_kernel_spmd(nc, [arrays], core_ids=[0])
    return r.results[0]["out_x"]
```
